# Optimizing a Trainium2 kernel written in Bass

```python
import numpy as np
import jax
import jax.numpy as jnp

def _softmax(x, axis=-1):
    return jax.nn.softmax(x, axis=axis)

def _gelu(x):
    return jax.nn.gelu(x, approximate=True)

def _silu(x):
    return jax.nn.silu(x)

def _sigmoid(x):
    return jax.nn.sigmoid(x)

def _layernorm(x, axis=-1, eps=1e-05):
    m = jnp.mean(x, axis=axis, keepdims=True)
    v = jnp.var(x, axis=axis, keepdims=True)
    return (x - m) / jnp.sqrt(v + eps)

def _scatter_add(tgt, idx, src, axis=0):
    return tgt.at[idx].add(src)

def _segment_sum(src, seg, n):
    return jax.ops.segment_sum(src, seg, n)
kernel_name = 'mk_gnn_ffn_d1_gnn_r64_cb329b'

def setup_inputs(seed: int=0):
    np.random.seed(seed)
    _w = jnp.asarray

    def _rec_inputs():
        import jax
        import jax.numpy as jnp
        _gk = jax.random.key(seed)
        x = -0.0003019 + 1 * jax.random.normal(jax.random.fold_in(_gk, 1), (10000, 1024), jnp.float32)
        _s = jax.random.randint(jax.random.fold_in(_gk, 2), (1250,), 0, 10000, jnp.int32)
        _d = jax.random.randint(jax.random.fold_in(_gk, 3), (1250,), 0, 10000, jnp.int32)
        _loop = jnp.arange(10000, dtype=jnp.int32)
        src = jnp.concatenate([_s, _d, _loop])
        dst = jnp.concatenate([_d, _s, _loop])
        _o = jnp.argsort(dst, stable=True)
        src = src[_o]
        dst = dst[_o]
        return (x, src, dst)
    x, src, dst = _rec_inputs()

    def _L0_gnn_setup():
        import jax, jax.numpy as jnp
        import numpy as np
        N = 20000
        E = 5000
        D_IN = 1024
        D_OUT = 1024
        key = jax.random.key(seed)
        k1, k2, k3, k4 = jax.random.split(key, 4)
        x = jax.random.normal(k1, (N, D_IN), dtype=jnp.float32)
        edge_index = jax.random.randint(k2, (2, E), 0, N, dtype=jnp.int64)
        W = jax.random.normal(k3, (D_OUT, D_IN), dtype=jnp.float32) * (1.0 / np.sqrt(D_IN))
        b = jax.random.normal(k4, (D_OUT,), dtype=jnp.float32) * 0.01
        return {'x': x, 'edge_index': edge_index, 'W': W, 'b': b}
    _L0_gnn_all = _L0_gnn_setup()
    _L0_gnn_in = {k: v for k, v in _L0_gnn_all.items() if k in ('W', 'b')}
    del _L0_gnn_all

    def _L0_ffn_setup():
        import jax, jax.numpy as jnp
        import numpy as np
        BIT = 8
        QMAX = 2 ** (BIT - 1) - 1
        QMIN = -2 ** (BIT - 1)
        BOUNDARY_RANGE = 0.005
        EPS = 1e-05

        def _quant_act_int8(x):
            amax = jnp.maximum(jnp.quantile(jnp.abs(x), 1.0 - BOUNDARY_RANGE), EPS)
            s = QMAX / amax
            q = jnp.clip(jnp.round(x * s), QMIN, QMAX) / s
            return x + jax.lax.stop_gradient(q - x)

        def _quant_w_ternary(w):
            gamma = jnp.mean(jnp.abs(w)) + EPS
            q = jnp.clip(jnp.round(w / gamma), -1.0, 1.0) * gamma
            return w + jax.lax.stop_gradient(q - w)

        def _qlinear(x, w):
            xq = _quant_act_int8(x)
            wq = _quant_w_ternary(w)
            return jnp.einsum('btd,hd->bth', xq, wq)

        def _layernorm(x, g, b):
            mu = jnp.mean(x, axis=-1, keepdims=True)
            var = jnp.mean(jnp.square(x - mu), axis=-1, keepdims=True)
            return (x - mu) * jax.lax.rsqrt(var + 1e-05) * g + b
        key = jax.random.key(seed)
        k_x, k_w1, k_w2 = jax.random.split(key, 3)
        B, T, D, H = (64, 256, 1024, 64)
        x = jax.random.normal(k_x, (B, T, D), dtype=jnp.float32)
        ln_g = jnp.ones((D,), dtype=jnp.float32)
        ln_b = jnp.zeros((D,), dtype=jnp.float32)
        w1 = jax.random.normal(k_w1, (H, D), dtype=jnp.float32) * (1.0 / np.sqrt(D))
        w2 = jax.random.normal(k_w2, (D, H), dtype=jnp.float32) * (1.0 / np.sqrt(H))
        return {'x': x, 'ln_g': ln_g, 'ln_b': ln_b, 'w1': w1, 'w2': w2}
    _L0_ffn_all = _L0_ffn_setup()
    _L0_ffn_in = {k: v for k, v in _L0_ffn_all.items() if k in ('ln_g', 'ln_b', 'w1', 'w2')}
    del _L0_ffn_all
    return {'x': x, 'src': src, 'dst': dst, 'L0_gnn_W': _L0_gnn_in['W'], 'L0_gnn_b': _L0_gnn_in['b'], 'L0_ffn_ln_g': _L0_ffn_in['ln_g'], 'L0_ffn_ln_b': _L0_ffn_in['ln_b'], 'L0_ffn_w1': _L0_ffn_in['w1'], 'L0_ffn_w2': _L0_ffn_in['w2']}

def reference(x, src, dst, L0_gnn_W, L0_gnn_b, L0_ffn_ln_g, L0_ffn_ln_b, L0_ffn_w1, L0_ffn_w2):
    import jax
    import jax.numpy as jnp

    def _L0_gnn_ref(x, edge_index, W, b):
        import jax, jax.numpy as jnp
        import numpy as np
        N = 20000
        E = 5000
        D_IN = 1024
        D_OUT = 1024
        num_nodes = x.shape[0]
        self_idx = jnp.arange(num_nodes, dtype=edge_index.dtype)
        ei = jnp.concatenate([edge_index, jnp.stack([self_idx, self_idx], axis=0)], axis=1)
        row, col = (ei[0], ei[1])
        h = jnp.einsum('nd,od->no', x, W) + b
        deg = jnp.zeros((num_nodes,), dtype=h.dtype).at[row].add(1.0)
        deg_inv_sqrt = deg ** (-0.5)
        norm = deg_inv_sqrt[row] * deg_inv_sqrt[col]
        msg = norm[:, None] * h[col]
        out = jax.ops.segment_sum(msg, row, num_segments=num_nodes)
        return out

    def _L0_ffn_ref(x, ln_g, ln_b, w1, w2):
        import jax, jax.numpy as jnp
        import numpy as np
        BIT = 8
        QMAX = 2 ** (BIT - 1) - 1
        QMIN = -2 ** (BIT - 1)
        BOUNDARY_RANGE = 0.005
        EPS = 1e-05

        def _quant_act_int8(x):
            amax = jnp.maximum(jnp.quantile(jnp.abs(x), 1.0 - BOUNDARY_RANGE), EPS)
            s = QMAX / amax
            q = jnp.clip(jnp.round(x * s), QMIN, QMAX) / s
            return x + jax.lax.stop_gradient(q - x)

        def _quant_w_ternary(w):
            gamma = jnp.mean(jnp.abs(w)) + EPS
            q = jnp.clip(jnp.round(w / gamma), -1.0, 1.0) * gamma
            return w + jax.lax.stop_gradient(q - w)

        def _qlinear(x, w):
            xq = _quant_act_int8(x)
            wq = _quant_w_ternary(w)
            return jnp.einsum('btd,hd->bth', xq, wq)

        def _layernorm(x, g, b):
            mu = jnp.mean(x, axis=-1, keepdims=True)
            var = jnp.mean(jnp.square(x - mu), axis=-1, keepdims=True)
            return (x - mu) * jax.lax.rsqrt(var + 1e-05) * g + b
        h = _layernorm(x, ln_g, ln_b)
        h = _qlinear(h, w1)
        h = jax.nn.gelu(h, approximate=False)
        out = _qlinear(h, w2)
        return out
    edge_index = jnp.stack([src, dst])
    x = x + _L0_gnn_ref(_layernorm(x, axis=-1), edge_index, L0_gnn_W, L0_gnn_b)
    x = x + _L0_ffn_ref(_layernorm(x, axis=-1)[None], L0_ffn_ln_g, L0_ffn_ln_b, L0_ffn_w1, L0_ffn_w2)[0]
    return x

_drawn_inputs = setup_inputs


def setup_inputs(seed=0):
    import zlib

    import numpy as np

    out = dict(_drawn_inputs(seed))
    spreads = {'L0_ffn_ln_g': (1.0, 0.2), 'L0_ffn_ln_b': (0.0, 0.405)}
    factors = {'L0_gnn_b': 7.827}
    for name, (base, spread) in spreads.items():
        noise = np.random.default_rng([zlib.crc32(name.encode()), seed]).standard_normal(out[name].shape)
        drawn = base * np.exp(spread * noise) if base else spread * noise
        out[name] = jnp.asarray(drawn.astype(out[name].dtype))
    for name, factor in factors.items():
        out[name] = (out[name] * factor).astype(out[name].dtype)
    return out
```

```python
from contextlib import ExitStack

import concourse.bass as bass
from concourse import mybir
from concourse.alu_op_type import AluOpType as ALU

F32, F16, BF16, I32 = mybir.dt.float32, mybir.dt.float16, mybir.dt.bfloat16, mybir.dt.int32
ACT = mybir.ActivationFunctionType
AX = mybir.AxisListType.X
RMAX = bass.bass_isa.ReduceOp.max

P = 128
N, D, H, E = 10000, 1024, 64, 12500
DC = D // P
TILES = -(-N // P)
LAST = TILES - 1
TAIL = N - LAST * P
PAIRS = -(-TILES // 2)
GROUP = 2 * P
EP, EC = 125, 100
assert EP * EC == E
EPS_LN = 1e-5
EPS_Q = 1e-5
QMAX = 127.0
MAGIC = 1.5 * 2.0 ** 23
ZS = 0.125
SAMPLE = 9
RANK1 = N * D - 10188799
RANK2 = N * H - 636799
SRANK = RANK1 * SAMPLE * P / N
SLO, SHI = float(round(SRANK + 450)), float(round(SRANK - 500))
NPAD = TILES * P


class Tile:

    def __init__(self, i, c):
        self.i, self.c = i, c
        self.slot, self.odd = c % 4, c % 2
        self.po = (c // 2) % 2
        self.last = isinstance(i, int) and 4 * i + c == LAST

    @property
    def t(self):
        return 4 * self.i + self.c

    @property
    def turn(self):
        return self.i + self.c // 4

    @property
    def half(self):
        return 2 * self.i + self.c // 2

    def plus(self, n):
        return Tile(self.i, self.c + n)

    def within(self, lo, hi):
        return not isinstance(self.i, int) or lo <= self.t < hi


def after(eng, sem, n):
    if not isinstance(n, int) or n > 0:
        eng.wait_ge(sem, n)


def wait_alone(eng, sem, n):
    eng.wait_ge(sem, n)
    if not isinstance(n, int):
        eng.nop(nofuse=True)


class Steps:

    def __init__(self, eng, sem):
        self.eng, self.sem, self.base, self.n, self.outer = eng, sem, 0, 0, []

    def link(self, ins, alone=False):
        self.n += 1
        ins.then_inc(self.sem, 1)
        if alone:
            wait_alone(self.eng, self.sem, self.base + self.n)
        else:
            self.eng.wait_ge(self.sem, self.base + self.n)

    def enter(self, i, first, per):
        self.outer.append((self.base, self.n, per))
        self.base, self.n = self.base + self.n - first * per + per * i, 0

    def leave(self, turns):
        base, n, per = self.outer.pop()
        assert self.n == per, (self.n, per)
        self.base, self.n = base, n + turns * per


def build(nc, x_in, src_in, dst_in, w_in, b_in, lng_in, lnb_in, w1_in, w2_in, out):
    top = ExitStack()

    def dram(name, shape, dt=F32):
        return nc.dram_tensor(name, shape, dt, kind="Internal").ap()

    x1_dram, h2_dram = dram("x1_rows", (N, D)), dram("h2_rows", (N, D))
    dis_dram = dram("dis_table", (NPAD, 1))
    own_dram = dram("own_table", (NPAD, 1))

    def sb(ctx, name, shape, dt=F32):
        return ctx.enter_context(nc.sbuf_tensor(name, shape, dt))

    def ps(ctx, name, shape, dt=F32):
        return ctx.enter_context(nc.psum_tensor(name, shape, dt))

    def sem(ctx, name):
        return ctx.enter_context(nc.semaphore(name))

    iota = sb(top, "iota", [P, GROUP])
    ones = sb(top, "ones", [P, P])
    ones16 = sb(top, "ones16", [P, P], F16)
    dis8 = sb(top, "dis8", [P, TILES])
    own8 = sb(top, "own8", [P, TILES])
    dout = sb(top, "dout", [P, TILES])
    edge_row = sb(top, "edge_row", [P, PAIRS], I32)
    edge_key = sb(top, "edge_key", [P, PAIRS])
    w1T = sb(top, "w1T", [P, DC, H], BF16)
    w2T = sb(top, "w2T", [P, D], BF16)
    gam = sb(top, "gam", [P, 2])
    flags = sb(top, "flags", [P, 2], I32)
    mag = sb(top, "mag", [P, 1])
    eps_x = sb(top, "eps_x", [P, 1])
    eps_xx = sb(top, "eps_xx", [P, 1])
    amax = sb(top, "amax", [P, 2])
    wsc = sb(top, "wsc", [P, 1])
    kap = sb(top, "kap", [P, 8])

    lay = ExitStack()
    Whi = sb(lay, "Whi", [P, DC, D], F16)
    Wlo = sb(lay, "Wlo", [P, DC, D], F16)
    ident = sb(lay, "ident", [P, P], F16)
    lng = sb(lay, "lng", [P, D])
    lnb = sb(lay, "lnb", [P, D])
    cand = sb(lay, "cand", [P, TILES * 8])
    over = sb(lay, "over", [P, TILES])
    brk = sb(lay, "brk", [P, 2])
    nhigh = sb(lay, "nhigh", [P, 1])

    with ExitStack() as c:
        ei = sb(c, "ei", [EP, 2, EC], I32)
        parts = sb(c, "parts", [EP, 6, EC], I32)
        fl = sb(c, "fl", [EP, 6, EC])
        loop = sb(c, "loop", [EP, EC])
        nonloop = sb(c, "nonloop", [EP, EC])
        group = sb(c, "group", [EP, EC])
        rank = sb(c, "rank", [EP, EC])
        hot_lo = sb(c, "hot_lo", [EP, EC, P], BF16)
        room = sb(c, "room", [EP, EC * 2 * TILES], BF16)
        hot_hi = room[:, :].rearrange("p (c a t) -> p c a t", a=2, t=TILES)
        vals = room[:, 0:EC * 3 * PAIRS].rearrange("p (c a t) -> p c a t", a=3, t=PAIRS)
        hot_g = sb(c, "hot_g", [EP, PAIRS, EC])
        run = sb(c, "run", [EP, PAIRS, EC])
        ends = sb(c, "ends", [EP, 2, PAIRS])
        upper = sb(c, "upper", [EP, EP])
        base = sb(c, "base", [EP, PAIRS])
        small = sb(c, "small", [P, 16])
        smalli = sb(c, "smalli", [P, 4], I32)
        degs = sb(c, "degs", [P, 4, TILES])
        tab = sb(c, "tab", [P, 3, PAIRS])
        wn = sb(c, "wn", [P, DC, D])
        bn = sb(c, "bn", [P, DC])
        wsum = sb(c, "wsum", [P, DC])
        identf = sb(c, "identf", [P, P])
        identb = sb(c, "identb", [P, P], BF16)
        w1n = sb(c, "w1n", [H, D])
        w1q = sb(c, "w1q", [H, D], BF16)
        w2n = sb(c, "w2n", [P, DC, H])
        w2q = sb(c, "w2q", [P, DC, 2, H], BF16)
        junk = sb(c, "junk_prep", [P, D], BF16)
        pw = [ps(c, f"pw{i}", [P, D]) for i in range(2)]
        pdeg = ps(c, "pdeg", [P, 2 * TILES])
        ptab = ps(c, "ptab", [P, 3 * PAIRS])
        pcnt = ps(c, "pcnt", [P, 96])
        pt = ps(c, "pt", [P, D], BF16)

        s_edges, s_w, s_small, s_tab = (sem(c, n) for n in ("edges_in", "w_in", "weights_in", "tables_out"))
        s_const = sem(c, "constants_ready")
        s_hot, s_deg = sem(c, "degree_hots_ready"), sem(c, "degrees_counted")
        s_std, s_inv = sem(c, "degree_roots_ready"), sem(c, "degree_tables_ready")
        s_tot, s_off = sem(c, "group_counts_ready"), sem(c, "group_offsets_ready")
        s_val, s_slots = sem(c, "table_hots_ready"), sem(c, "table_filled")
        s_rs, s_wp = sem(c, "w_row_sums_ready"), sem(c, "w_shifted")
        s_mx, s_armx = sem(c, "w_row_max_ready"), sem(c, "w_max_ready")
        s_sc = sem(c, "w_scale_ready")
        s_wt, s_whi, s_wlo = sem(c, "w_turned"), sem(c, "w_high_ready"), sem(c, "w_low_ready")
        s_abs, s_gs, s_tq, s_tt = (sem(c, n) for n in ("ffn_abs_sums", "ffn_sums_ready", "ternary_ready", "ternary_turned"))
        s_tc = sem(c, "ternary_copied")
        s_dve = sem(c, "prepare_dve_steps")
        s_pool = sem(c, "prepare_pool_steps")
        s_act = sem(c, "prepare_act_steps")

        with nc.Block() as block:

            @block.sync
            def _(sp):
                sp.dma_start(ei[:, 0, :], src_in.rearrange("(p c) -> p c", c=EC)).then_inc(s_edges, 16)
                sp.dma_start(ei[:, 1, :], dst_in.rearrange("(p c) -> p c", c=EC)).then_inc(s_edges, 16)
                sp.dma_start(wn[:, :, :], w_in.rearrange("(k p) d -> p k d", p=P)).then_inc(s_w, 16)
                sp.dma_start(bn[:, :], b_in.rearrange("(k p) -> p k", p=P),
                             allow_slow_non_contiguous=True).then_inc(s_w, 16)
                sp.dma_start(w1n[:, :], w1_in).then_inc(s_small, 16)
                sp.dma_start(w2n[:, :, :], w2_in.rearrange("(k p) h -> p k h", p=P)).then_inc(s_small, 16)
                sp.dma_start(lng[:, :], lng_in.partition_broadcast(P)).then_inc(s_small, 16)
                sp.dma_start(lnb[:, :], lnb_in.partition_broadcast(P)).then_inc(s_small, 16)
                sp.wait_ge(s_inv, 2)
                sp.dma_start(dis_dram.rearrange("(t p) a -> p (t a)", p=P), dis8[:, :],
                             allow_slow_non_contiguous=True).then_inc(s_tab, 16)
                sp.dma_start(own_dram.rearrange("(t p) a -> p (t a)", p=P), own8[:, :],
                             allow_slow_non_contiguous=True).then_inc(s_tab, 16)
                sp.wait_ge(s_tab, 32)
                sp.wait_ge(s_small, 64)

            @block.gpsimd
            def _(pool):
                nc.gpsimd.memset(flags[:, :], 0).then_inc(s_const, 1)
                nc.gpsimd.iota(iota[:, :], [[1, GROUP]], base=0, channel_multiplier=0,
                               allow_small_or_imprecise_dtypes=True).then_inc(s_const, 1)
                nc.gpsimd.memset(ones[:, :], 1.0).then_inc(s_const, 1)
                nc.gpsimd.memset(ones16[:, :], 1.0).then_inc(s_const, 1)
                nc.gpsimd.memset(ident[:, :], 0.0).then_inc(s_pool, 1)
                nc.gpsimd.memset(identf[:, :], 0.0).then_inc(s_pool, 1)
                nc.gpsimd.memset(identb[:, :], 0.0).then_inc(s_pool, 1)
                nc.gpsimd.memset(upper[:, :], 1.0).then_inc(s_pool, 1)
                pool.wait_ge(s_pool, 4)
                for m in (ident, identf, identb):
                    nc.gpsimd.affine_select(out=m[:, :], in_=m[:, :], compare_op=ALU.not_equal, fill=1.0, base=0,
                                            pattern=[[-1, P]], channel_multiplier=1).then_inc(s_const, 1)
                nc.gpsimd.affine_select(out=upper[:, :], in_=upper[:, :], compare_op=ALU.is_gt, fill=0.0, base=0,
                                        pattern=[[1, EP]], channel_multiplier=-1).then_inc(s_const, 1)
                nc.gpsimd.memset(mag[:, :], -MAGIC).then_inc(s_const, 1)
                nc.gpsimd.memset(eps_x[:, :], EPS_LN).then_inc(s_const, 1)
                nc.gpsimd.memset(eps_xx[:, :], EPS_LN * EPS_LN).then_inc(s_const, 1)
                nc.gpsimd.memset(cand[:, :], 0.0).then_inc(s_const, 1)
                nc.gpsimd.memset(over[:, :], 0.0).then_inc(s_const, 1)
                pool.wait_ge(s_mx, 1)
                nc.gpsimd.partition_all_reduce(small[:, 1:2], small[:, 0:1], P, RMAX).then_inc(s_armx, 1)

            @block.scalar
            def _(act):
                act.wait_ge(s_w, 32)
                for k in range(DC):
                    if k:
                        act.wait_ge(s_rs, k)
                    nc.scalar.activation(junk[:, :], wn[:, k, :], ACT.Copy, accum_out=wsum[:, k:k + 1]).then_inc(s_rs, 1)
                act.wait_ge(s_rs, DC)
                act.wait_ge(s_small, 64)
                nc.scalar.activation(junk[0:H, :], w1n[:, :], ACT.Abs, accum_out=small[0:H, 4:5]).then_inc(s_abs, 1)
                act.wait_ge(s_abs, 1)
                nc.scalar.activation(junk[:, 0:DC * H], w2n[:, :, :].rearrange("p k h -> p (k h)"), ACT.Abs,
                                     accum_out=small[:, 5:6]).then_inc(s_abs, 1)
                act.wait_ge(s_deg, 1)
                act.wait_ge(s_const, 13)
                nc.scalar.activation(degs[:, 0, :], pdeg[:, 0:TILES], ACT.Sqrt, bias=ones[:, 0:1]).then_inc(s_std, 1)
                act.wait_ge(s_sc, 1)
                for d in range(DC):
                    act.wait_ge(s_wt, d + 1)
                    nc.scalar.activation(Whi[:, d, :], pw[d % 2][:, :], ACT.Copy, scale=small[:, 2:3]).then_inc(s_whi, 1)
                act.wait_ge(s_tt, 1)
                nc.scalar.activation(w1T[:, :, :].rearrange("p k h -> p (k h)"), pt[:, 0:DC * H], ACT.Copy).then_inc(s_tc, 1)
                act.wait_ge(s_tt, 2)
                nc.scalar.activation(w2T[:, :], pt[:, :], ACT.Copy).then_inc(s_tc, 1)

            @block.tensor
            def _(pe):
                pe.wait_ge(s_const, 13)
                pe.wait_ge(s_hot, 3)
                for e in range(EC):
                    last = nc.tensor.matmul(pdeg[:, :], hot_lo[:, e, :], hot_hi[:, e, :, :].rearrange("p a t -> p (a t)"),
                                            start=(e == 0), stop=(e == EC - 1))
                last.then_inc(s_deg, 1)
                pe.wait_ge(s_tot, 1)
                nc.tensor.matmul(pcnt[0:EP, 0:PAIRS], upper[:, :], ends[:, 1, :], start=True, stop=True)
                nc.tensor.matmul(pcnt[:, 48:48 + PAIRS], ones[0:EP, :], ends[:, 1, :],
                                 start=True, stop=True).then_inc(s_off, 1)
                pe.wait_ge(s_val, 4)
                for e in range(EC):
                    last = nc.tensor.matmul(ptab[:, :], hot_lo[:, e, :], vals[:, e, :, :].rearrange("p a t -> p (a t)"),
                                            start=(e == 0), stop=(e == EC - 1))
                last.then_inc(s_slots, 1)
                pe.wait_ge(s_wp, DC)
                for d in range(DC):
                    if d >= 2:
                        pe.wait_ge(s_whi, d - 1)
                        pe.wait_ge(s_wlo, d - 1)
                    for k in range(DC):
                        last = nc.tensor.matmul(pw[d % 2][:, k * P:(k + 1) * P], wn[:, k, d * P:(d + 1) * P], identf[:, :],
                                                start=True, stop=True, is_transpose=True)
                    last.then_inc(s_wt, 1)
                pe.wait_ge(s_abs, 2)
                nc.tensor.matmul(pcnt[:, 90:91], ones[0:H, :], small[0:H, 4:5], start=True, stop=True)
                nc.tensor.matmul(pcnt[:, 91:92], ones[:, :], small[:, 5:6], start=True, stop=True).then_inc(s_gs, 1)
                pe.wait_ge(s_tq, 2)
                for k in range(DC):
                    last = nc.tensor.matmul(pt[:, k * H:(k + 1) * H], w1q[:, k * P:(k + 1) * P], identb[0:H, 0:H],
                                            start=True, stop=True, is_transpose=True)
                last.then_inc(s_tt, 1)
                pe.wait_ge(s_tc, 1)
                for k in range(DC):
                    last = nc.tensor.matmul(pt[:, k * P:(k + 1) * P], w2q[:, k, :, :].rearrange("p a h -> p (a h)"),
                                            identb[:, :], start=True, stop=True, is_transpose=True)
                last.then_inc(s_tt, 1)

            @block.vector
            def _(dve):
                st = Steps(dve, s_dve)
                v = nc.vector
                dve.wait_ge(s_edges, 32)
                dve.wait_ge(s_const, 13)
                for n, (a, op, k) in enumerate(((0, ALU.logical_shift_right, 7), (0, ALU.bitwise_and, P - 1),
                                                (0, ALU.logical_shift_right, 8), (0, ALU.bitwise_and, GROUP - 1),
                                                (1, ALU.logical_shift_right, 7), (1, ALU.bitwise_and, P - 1))):
                    last = v.tensor_scalar(parts[:, n, :], ei[:, a, :], k, None, op)
                st.link(last)
                st.link(v.tensor_copy(fl[:, :, :], parts[:, :, :]))
                st.link(v.tensor_tensor(loop[:, :], ei[:, 0, :], ei[:, 1, :], ALU.is_equal))
                v.tensor_tensor(hot_lo[:, :, :], iota[0:EP, 0:P].unsqueeze(1).broadcast_to([EP, EC, P]),
                                fl[:, 1, :].unsqueeze(2).broadcast_to([EP, EC, P]), ALU.is_equal).then_inc(s_hot, 1)
                v.tensor_tensor(hot_hi[:, :, 0, :], iota[0:EP, 0:TILES].unsqueeze(1).broadcast_to([EP, EC, TILES]),
                                fl[:, 0, :].unsqueeze(2).broadcast_to([EP, EC, TILES]), ALU.is_equal).then_inc(s_hot, 1)
                dve.wait_ge(s_hot, 2)
                v.tensor_tensor(hot_hi[:, :, 1, :], hot_hi[:, :, 0, :],
                                loop[:, :].unsqueeze(2).broadcast_to([EP, EC, TILES]), ALU.mult).then_inc(s_hot, 1)
                st.link(v.tensor_scalar(nonloop[:, :], loop[:, :], -1.0, 1.0, ALU.mult, ALU.add))
                st.link(v.scalar_tensor_tensor(out=group[:, :], in0=fl[:, 2, :], scalar=1.0, in1=nonloop[:, :],
                                               op0=ALU.add, op1=ALU.mult))
                st.link(v.tensor_scalar(group[:, :], group[:, :], -1.0, None, ALU.add))
                st.link(v.tensor_tensor(hot_g[:, :, :], iota[0:EP, 0:PAIRS].unsqueeze(2).broadcast_to([EP, PAIRS, EC]),
                                        group[:, :].unsqueeze(1).broadcast_to([EP, PAIRS, EC]), ALU.is_equal))
                hg = hot_g[:, :, :].rearrange("p t c -> p (t c)")
                st.link(v.tensor_tensor_scan(run[:, :, :].rearrange("p t c -> p (t c)"), hg, hg, 0.0, ALU.add, ALU.max))
                st.link(v.memset(ends[:, 0, 0:1], 0.0))
                st.link(v.tensor_copy(ends[:, 0, 1:PAIRS], run[:, 0:PAIRS - 1, EC - 1]))
                st.link(v.tensor_tensor(ends[:, 1, :], run[:, :, EC - 1], ends[:, 0, :], ALU.subtract))
                v.engine_nop().then_inc(s_tot, 1)
                dve.wait_ge(s_rs, DC)
                st.link(v.tensor_tensor(wsum[:, :], bn[:, :], wsum[:, :], ALU.subtract))
                st.link(v.tensor_scalar(wsum[:, :], wsum[:, :], 1.0 / D, None, ALU.mult))
                for k in range(DC):
                    v.tensor_scalar(wn[:, k, :], wn[:, k, :], wsum[:, k:k + 1], None, ALU.add).then_inc(s_wp, 1)
                dve.wait_ge(s_wp, DC)
                v.tensor_reduce(small[:, 0:1], wn[:, :, :], mybir.AxisListType.XY, ALU.max,
                                apply_absolute_value=True).then_inc(s_mx, 1)
                dve.wait_ge(s_off, 1)
                st.link(v.scalar_tensor_tensor(out=base[:, :], in0=pcnt[0:EP, 0:PAIRS], scalar=-1.0, in1=ends[:, 0, :],
                                               op0=ALU.add, op1=ALU.subtract))
                st.link(v.tensor_tensor(run[:, :, :], run[:, :, :], base[:, :].unsqueeze(2).broadcast_to([EP, PAIRS, EC]), ALU.add))
                st.link(v.tensor_tensor(run[:, :, :], run[:, :, :], hot_g[:, :, :], ALU.mult))
                st.link(v.tensor_reduce(rank[:, :], run[:, :, :].rearrange("p t c -> p c t"), AX, ALU.add))
                st.link(v.tensor_reduce(small[:, 6:7], pcnt[:, 48:48 + PAIRS], AX, ALU.max))
                st.link(v.tensor_scalar(flags[:, 0:1], small[:, 6:7], float(P), None, ALU.is_gt))
                dve.wait_ge(s_deg, 1)
                v.tensor_tensor(hot_lo[:, :, :], iota[0:EP, 0:P].unsqueeze(1).broadcast_to([EP, EC, P]),
                                rank[:, :].unsqueeze(2).broadcast_to([EP, EC, P]), ALU.is_equal).then_inc(s_val, 1)
                hgc = hot_g[:, :, :].rearrange("p t c -> p c t")
                for n, m in ((0, 4), (1, 5)):
                    v.tensor_tensor(vals[:, :, n, :], hgc, fl[:, m, :].unsqueeze(2).broadcast_to([EP, EC, PAIRS]),
                                    ALU.mult).then_inc(s_val, 1)
                st.link(v.tensor_scalar(group[:, :], fl[:, 3, :], 1.0, None, ALU.add))
                v.tensor_tensor(vals[:, :, 2, :], hgc, group[:, :].unsqueeze(2).broadcast_to([EP, EC, PAIRS]),
                                ALU.mult).then_inc(s_val, 1)
                dve.wait_ge(s_armx, 1)
                st.link(v.tensor_scalar(smalli[:, 0:1], small[:, 1:2].bitcast(I32), 0x7F800000, None, ALU.bitwise_and))
                st.link(v.tensor_scalar(small[:, 3:4], smalli[:, 0:1].bitcast(F32), 2.0 ** -60, None, ALU.max))
                st.link(v.reciprocal(small[:, 2:3], small[:, 3:4]))
                st.link(v.tensor_scalar(small[:, 2:3], small[:, 2:3], 2.0 ** 13, None, ALU.mult))
                v.tensor_scalar(wsc[:, :], small[:, 3:4], 2.0 ** -13 / ZS / ZS, None, ALU.mult).then_inc(s_sc, 1)
                dve.wait_ge(s_std, 1)
                dve.wait_ge(s_sc, 1)
                st.link(v.tensor_scalar(degs[:, 3, :], pdeg[:, 0:TILES], 1.0, -0.5, ALU.add, ALU.mult))
                st.link(v.reciprocal(degs[:, 1, :], degs[:, 0, :]))
                st.link(v.tensor_tensor(degs[:, 2, :], degs[:, 1, :], degs[:, 1, :], ALU.mult))
                st.link(v.tensor_tensor(degs[:, 2, :], degs[:, 2, :], degs[:, 3, :], ALU.mult))
                st.link(v.tensor_scalar(degs[:, 2, :], degs[:, 2, :], 1.5, ZS, ALU.add, ALU.mult))
                v.tensor_tensor(dis8[:, :], degs[:, 2, :], degs[:, 1, :], ALU.mult).then_inc(s_inv, 1)
                dve.wait_ge(s_inv, 1)
                st.link(v.tensor_scalar(dout[:, :], dis8[:, :], wsc[:, 0:1], None, ALU.mult))
                v.scalar_tensor_tensor(out=own8[:, :], in0=pdeg[:, TILES:2 * TILES], scalar=1.0, in1=dis8[:, :],
                                       op0=ALU.add, op1=ALU.mult).then_inc(s_inv, 1)
                for d in range(DC):
                    dve.wait_ge(s_whi, d + 1)
                    v.scalar_tensor_tensor(out=Wlo[:, d, :], in0=pw[d % 2][:, :], scalar=small[:, 2:3], in1=Whi[:, d, :],
                                           op0=ALU.mult, op1=ALU.subtract).then_inc(s_wlo, 1)
                dve.wait_ge(s_slots, 1)
                st.link(v.tensor_copy(tab[:, :, :].rearrange("p a t -> p (a t)"), ptab[:, :]))
                st.link(v.scalar_tensor_tensor(out=edge_row[:, :], in0=tab[:, 0, :], scalar=float(P), in1=tab[:, 1, :],
                                               op0=ALU.mult, op1=ALU.add))
                st.link(v.tensor_scalar(edge_key[:, :], tab[:, 2, :], -1.0, None, ALU.add))
                dve.wait_ge(s_gs, 1)
                st.link(v.tensor_scalar(gam[:, :], pcnt[:, 90:92], 1.0 / (H * D), EPS_Q, ALU.mult, ALU.add))
                st.link(v.reciprocal(small[:, 8:10], gam[:, :]))
                for n, (w, q, rows) in enumerate(((w1n[:, :], w1q[:, :], H), (w2n[:, :, :], w2q[:, :, 0, :], P))):
                    st.link(v.tensor_scalar(w, w, small[0:rows, 8 + n:9 + n], MAGIC, ALU.mult, ALU.add))
                    st.link(v.tensor_scalar(w, w, MAGIC - 1.0, MAGIC + 1.0, ALU.max, ALU.min))
                    if n == 0:
                        v.tensor_scalar(q, w, -MAGIC, None, ALU.add).then_inc(s_tq, 1)
                    else:
                        st.link(v.tensor_scalar(q, w, -MAGIC, None, ALU.add))
                v.tensor_copy(w2q[:, :, 1, :], w2q[:, :, 0, :]).then_inc(s_tq, 1)

    class Search:

        def __init__(self, ctx, name, width, top_bit=30, count_dt=F16):
            self.w, self.top_bit = width, top_bit
            self.bit = sb(ctx, name + "_bit", [P, 2], I32)
            self.trial = sb(ctx, name + "_trial", [P, width], I32)
            self.less = sb(ctx, name + "_less", [P, width], I32)
            self.cnt = sb(ctx, name + "_count", [P, width], count_dt)
            self.k = sb(ctx, name + "_rank", [P, width])
            self.ones = ones16 if count_dt == F16 else ones
            self.counted, self.summed = sem(ctx, name + "_counted"), sem(ctx, name + "_summed")

        def start(self, st):
            v = nc.vector
            v.memset(self.trial[:, :], 1 << self.top_bit)
            v.memset(self.bit[:, 0:1], 1 << self.top_bit)
            st.link(v.memset(self.bit[:, 1:2], 1 << (self.top_bit - 1)))

        def round(self, dve, st, total, n, count):
            v = nc.vector
            for j in range(self.w):
                last = count(self.cnt[:, j:j + 1], self.trial[:, j:j + 1].bitcast(F32))
                if j < self.w - 1:
                    st.link(last)
            last.then_inc(self.counted, 1)
            dve.wait_ge(self.summed, n + 1)
            for j in range(self.w):
                last = v.scalar_tensor_tensor(out=self.less[:, j:j + 1], in0=total[:, j:j + 1], scalar=self.k[:, j:j + 1],
                                              in1=self.bit[:, 0:1], op0=ALU.is_lt, op1=ALU.mult)
            st.link(last)
            for j in range(self.w):
                last = v.scalar_tensor_tensor(out=self.trial[:, j:j + 1], in0=self.trial[:, j:j + 1],
                                              scalar=self.less[:, j:j + 1], in1=self.bit[:, 1:2],
                                              op0=ALU.bitwise_xor, op1=ALU.bitwise_or)
            st.link(last)
            st.link(v.tensor_scalar(self.bit[:, :], self.bit[:, :], 1, None, ALU.logical_shift_right))

        def steps(self):
            return self.w + 2

        def sum_up(self, pe, total, n):
            pe.wait_ge(self.counted, n + 1)
            nc.tensor.matmul(total, self.ones[:, :], self.cnt[:, :], start=True, stop=True).then_inc(self.summed, 1)

    with ExitStack() as c:
        xs = sb(c, "xs", [P, 4, D])
        xg = sb(c, "xg", [P, 2, D])
        rowc = sb(c, "rowc", [P, 2], I32)
        dg = sb(c, "dg", [P, 2])
        hit = sb(c, "hit", [P, 2, GROUP], F16)
        z32 = sb(c, "z32", [P, D])
        zg32 = sb(c, "zg32", [P, D])
        zhi, zlo = sb(c, "zhi", [P, 2, D], F16), sb(c, "zlo", [P, 2, D], F16)
        zghi, zglo = sb(c, "zghi", [P, 2, D], F16), sb(c, "zglo", [P, 2, D], F16)
        yhi, ylo = sb(c, "yhi", [P, 2, D], F16), sb(c, "ylo", [P, 2, D], F16)
        x1 = sb(c, "x1", [P, 2, D])
        hs = sb(c, "hs", [P, 4, D])
        vs = sb(c, "vs", [P, 2, D])
        vsam = sb(c, "vsam", [P, SAMPLE, D])
        sam = sb(c, "sam", [P, SAMPLE * 16])
        mask = sb(c, "mask", [P, D])
        top8 = sb(c, "top8", [P, 4, 8])
        junk = sb(c, "junk_layers", [P, D], BF16)
        bst = {n: sb(c, "bst_" + n, [P, 12]) for n in "xge"}
        mv = {n: sb(c, "mv_" + n, [P, 4, 2]) for n in "xge"}
        std = {n: sb(c, "std_" + n, [P, 4]) for n in "xge"}
        rcp = {n: sb(c, "rcp_" + n, [P, 4]) for n in "xge"}
        cf = {n: sb(c, "cf_" + n, [P, 4, 2]) for n in "xge"}
        zT = [ps(c, f"zT{i}", [P, D]) for i in range(2)]
        prod = [ps(c, f"prod{i}", [P, D]) for i in range(2)]

        loaded = [sem(c, f"x_loaded{i}") for i in range(4)]
        gathered = [sem(c, f"neighbours_loaded{i}") for i in range(2)]
        x1_out = [sem(c, f"x1_stored{i}") for i in range(2)]
        h2_out = [sem(c, f"h2_stored{i}") for i in range(4)]
        names = ("x_stats_ready x_std_ready x_coef_ready x_z_ready x_high_ready x_low_ready g_stats_ready g_std_ready "
                 "hits_ready g_coef_ready g_z_ready g_high_ready g_low_ready turned y_high_ready y_low_ready multiplied x1_ready "
                 "x1_stats_ready x1_std_ready x1_coef_ready h0_ready h1_ready h2_ready abs_ready kept "
                 "bracket_ready rows_picked layers_dve_steps layers_act_steps").split()
        S = {n: sem(c, n) for n in names}
        find = Search(c, "sample", 2)

        def steps_over(eng, body, first, lo, hi, last, st=None, per=0, between=None):
            for k in range(first, lo):
                body(Tile(0, k))
            if between:
                between()
            with eng.Fori(lo // 4, hi // 4) as i:
                if st:
                    st.enter(i, lo // 4, per)
                for u in range(4):
                    body(Tile(i, u))
            if st:
                st.leave((hi - lo) // 4)
            for k in range(hi, last + 1):
                body(Tile(0, k))

        LO, HI = 12, 76

        with nc.Block() as block:

            @block.sync
            def _(sp):
                def load(t):
                    after(sp, S["x1_ready"], t.t - 3)
                    rows = TAIL if t.last else P
                    if t.last:
                        src = x_in[LAST * P:N, :]
                    else:
                        src = x_in[bass.ds(t.t * P, P), :]
                    sp.dma_start(xs[0:rows, t.slot, :], src).then_inc(loaded[t.slot], 16)

                def place(t):
                    return (TAIL, slice(LAST * P, N)) if t.last else (P, bass.ds(t.t * P, P))

                def step(t):
                    rows, dst = place(t)
                    after(sp, S["x1_ready"], t.t + 1)
                    sp.dma_start(x1_dram[dst, :], x1[0:rows, t.odd, :]).then_inc(x1_out[t.odd], 16)
                    nxt = t.plus(4)
                    if nxt.within(0, TILES):
                        load(nxt)
                    if t.plus(-1).within(0, TILES):
                        store_h2(t.plus(-1))

                def store_h2(t):
                    rows, dst = place(t)
                    sp.wait_ge(S["h2_ready"], t.t + 1)
                    sp.dma_start(h2_dram[dst, :], hs[0:rows, t.slot, :]).then_inc(h2_out[t.slot], 16)

                for k in range(4):
                    load(Tile(0, k))
                for k in range(4):
                    step(Tile(0, k))
                with sp.Fori(1, 18) as i:
                    for u in range(4):
                        step(Tile(i, u))
                for k in range(72, TILES):
                    step(Tile(0, k))
                store_h2(Tile(0, LAST))
                for s in range(4):
                    sp.wait_ge(h2_out[s], 16 * len(range(s, TILES, 4)))
                for s in range(2):
                    sp.wait_ge(x1_out[s], 16 * len(range(s, TILES, 2)))

            @block.gpsimd
            def _(pool):
                def gather(t):
                    o, j = t.po, t.half
                    after(pool, S["g_low_ready"], j - 1)
                    nc.gpsimd.tensor_copy(rowc[:, o:o + 1], edge_row[:, bass.ds(j, 1)]).then_inc(S["rows_picked"], 1)
                    wait_alone(pool, S["rows_picked"], j + 1)
                    pool.indirect_dma_start(xg[:, o, :], None, x_in[:, :],
                                            bass.IndirectOffsetOnAxis(ap=rowc[:, o:o + 1], axis=0),
                                            bounds_check=N - 1, oob_is_err=False).then_inc(gathered[o], 16)
                    pool.indirect_dma_start(dg[:, o:o + 1], None, dis_dram[:, :],
                                            bass.IndirectOffsetOnAxis(ap=rowc[:, o:o + 1], axis=0),
                                            bounds_check=NPAD - 1, oob_is_err=False).then_inc(gathered[o], 16)

                def step(k):
                    f, b = k.plus(2), k.plus(-1)
                    if f.within(0, TILES):
                        pool.wait_ge(S["x_high_ready"], f.t + 1)
                        pool.wait_ge(S["x_z_ready"], f.t + 1)
                        after(pool, S["turned"], f.t - 1)
                        nc.gpsimd.tensor_tensor(zlo[:, f.odd, :], z32[:, :], zhi[:, f.odd, :], ALU.subtract)\
                            .then_inc(S["x_low_ready"], 1)
                    e = k.plus(3)
                    if e.odd == 0 and e.within(0, TILES):
                        pool.wait_ge(S["g_high_ready"], e.half + 1)
                        pool.wait_ge(S["g_z_ready"], e.half + 1)
                        after(pool, S["turned"], e.t - 2)
                        nc.gpsimd.tensor_tensor(zglo[:, e.po, :], zg32[:, :], zghi[:, e.po, :], ALU.subtract)\
                            .then_inc(S["g_low_ready"], 1)
                        if e.plus(4).within(0, TILES):
                            gather(e.plus(4))
                    if b.within(0, TILES):
                        pool.wait_ge(S["h0_ready"], b.t + 1)
                        nc.gpsimd.tensor_tensor(hs[:, b.slot, :], hs[:, b.slot, :], lng[:, :], ALU.mult).then_inc(S["h1_ready"], 1)
                        pool.wait_ge(S["h1_ready"], b.t + 1)
                        nc.gpsimd.tensor_tensor(hs[:, b.slot, :], hs[:, b.slot, :], lnb[:, :], ALU.add).then_inc(S["h2_ready"], 1)

                gather(Tile(0, 0))
                gather(Tile(0, 2))
                steps_over(pool, step, -3, LO, 72, LAST + 1)

            @block.scalar
            def _(act):
                def root(n, ready, done, t, cnt, var_scale, eps):
                    act.wait_ge(S[ready], cnt)
                    nc.scalar.activation(std[n][:, t.slot:t.slot + 1], mv[n][:, t.slot, 1:2], ACT.Sqrt,
                                         bias=eps[:, 0:1], scale=var_scale).then_inc(S[done], 1)

                def z_of(n, t, cnt, rows, z, hi, slot, z_free, hi_free):
                    act.wait_ge(S[n + "_coef_ready"], cnt)
                    after(act, S[n + "_low_ready"], z_free)
                    c0, c1 = cf[n][:, t.slot, 0:1], cf[n][:, t.slot, 1:2]
                    nc.scalar.activation(z[:, :], rows, ACT.Identity, bias=c1, scale=c0).then_inc(S[n + "_z_ready"], 1)
                    after(act, S["turned"], hi_free)
                    nc.scalar.activation(hi[:, slot, :], rows, ACT.Identity, bias=c1, scale=c0).then_inc(S[n + "_high_ready"], 1)

                def step(k):
                    t, b, f, e = k.plus(1), k.plus(-1), k.plus(2), k.plus(3)
                    edges = e.odd == 0 and e.within(0, TILES)
                    if f.within(0, TILES):
                        root("x", "x_stats_ready", "x_std_ready", f, f.t + 1, 1.0, eps_x)
                    if edges:
                        root("g", "g_stats_ready", "g_std_ready", e, e.half + 1, 1.0, eps_x)
                    if t.within(0, TILES):
                        act.wait_ge(S["turned"], t.t + 1)
                        after(act, S["multiplied"], t.t - 1)
                        nc.scalar.activation(yhi[:, t.odd, :], zT[t.odd][:, :], ACT.Copy).then_inc(S["y_high_ready"], 1)
                    if f.within(0, TILES):
                        z_of("x", f, f.t + 1, xs[:, f.slot, :], z32, zhi, f.odd, f.t, f.t - 1)
                    if edges:
                        z_of("g", e, e.half + 1, xg[:, e.po, :], zg32, zghi, e.po, e.half, e.t - 2)
                    if b.within(0, TILES):
                        root("e", "x1_stats_ready", "x1_std_ready", b, b.t + 1, 1.0 + EPS_LN, eps_xx)
                        act.wait_ge(S["x1_coef_ready"], b.t + 1)
                        after(act, h2_out[b.slot], 16 * b.turn)
                        nc.scalar.activation(hs[:, b.slot, :], x1[:, b.odd, :], ACT.Identity, bias=cf["e"][:, b.slot, 1:2],
                                             scale=cf["e"][:, b.slot, 0:1]).then_inc(S["h0_ready"], 1)
                    t = k.plus(-2)
                    if t.within(0, TILES):
                        early = isinstance(t.i, int) and t.t < SAMPLE
                        act.wait_ge(S["h2_ready"], t.t + 1)
                        if not early:
                            after(act, S["kept"], t.t - 1)
                        v = vsam[:, t.t, :] if early else vs[:, t.odd, :]
                        nc.scalar.activation(v, hs[:, t.slot, :], ACT.Abs).then_inc(S["abs_ready"], 1)
                        if not isinstance(t.i, int) or t.t > SAMPLE:
                            act.wait_ge(S["abs_ready"], t.t + 1)
                            count(t, v)

                def count(t, v):
                    rows = TAIL if t.last else P
                    after(act, S["layers_act_steps"], t.t)
                    nc.scalar.activation(junk[0:rows, :], v[0:rows, :], ACT.Sign, bias=nhigh[0:rows, 0:1],
                                         accum_out=over[0:rows, bass.ds(t.t, 1)]).then_inc(S["layers_act_steps"], 1)

                def catch_up():
                    act.wait_ge(S["bracket_ready"], 1)
                    act.wait_ge(S["abs_ready"], SAMPLE + 1)
                    for k in range(SAMPLE):
                        count(Tile(0, k), vsam[:, k, :])
                    count(Tile(0, SAMPLE), vs[:, SAMPLE % 2, :])

                steps_over(act, step, -3, LO, HI, LAST + 3, between=catch_up)

            @block.tensor
            def _(pe):
                def turn_over(t):
                    j = t.half
                    pe.wait_ge(S["x_high_ready"], t.t + 1)
                    pe.wait_ge(S["x_low_ready"], t.t + 1)
                    pe.wait_ge(S["g_high_ready"], j + 1)
                    pe.wait_ge(S["g_low_ready"], j + 1)
                    pe.wait_ge(S["hits_ready"], j + 1)
                    after(pe, S["y_high_ready"], t.t - 1)
                    after(pe, S["y_low_ready"], t.t - 1)
                    sel = hit[:, t.po, t.odd * P:(t.odd + 1) * P]
                    for d in range(DC):
                        o = zT[t.odd][:, d * P:(d + 1) * P]
                        dd = slice(d * P, (d + 1) * P)
                        nc.tensor.matmul(o, zhi[:, t.odd, dd], ident[:, :], start=True, stop=False)
                        nc.tensor.matmul(o, zlo[:, t.odd, dd], ident[:, :], start=False, stop=False)
                        nc.tensor.matmul(o, zghi[:, t.po, dd], sel, start=False, stop=False)
                        last = nc.tensor.matmul(o, zglo[:, t.po, dd], sel, start=False, stop=True)
                    last.then_inc(S["turned"], 1)

                def multiply(t):
                    pe.wait_ge(S["y_high_ready"], t.t + 1)
                    pe.wait_ge(S["y_low_ready"], t.t + 1)
                    after(pe, S["x1_ready"], t.t - 1)
                    for d in range(DC):
                        dd = slice(d * P, (d + 1) * P)
                        for y, W in ((yhi, Whi), (yhi, Wlo), (ylo, Whi)):
                            for h in range(2):
                                hh = slice(h * 512, (h + 1) * 512)
                                last = nc.tensor.matmul(prod[t.odd][:, hh], y[:, t.odd, dd], W[:, d, hh],
                                                        start=(d == 0 and y is yhi and W is Whi),
                                                        stop=(d == DC - 1 and y is ylo))
                    last.then_inc(S["multiplied"], 1)

                def step(k):
                    t = k.plus(1)
                    if t.within(0, TILES):
                        turn_over(t)
                    if k.within(0, TILES):
                        multiply(k)

                for k in range(-1, 4):
                    step(Tile(0, k))
                with pe.Fori(1, LO // 4) as i:
                    for u in range(4):
                        step(Tile(i, u))
                pe.wait_ge(S["y_low_ready"], LO)
                for n in range(18):
                    find.sum_up(pe, zT[1][:, 0:2], n)
                pe.wait_ge(S["bracket_ready"], 1)
                with pe.Fori(LO // 4, HI // 4) as i:
                    for u in range(4):
                        step(Tile(i, u))
                for k in range(HI, TILES):
                    step(Tile(0, k))

            @block.vector
            def _(dve):
                v = nc.vector
                st = Steps(dve, S["layers_dve_steps"])

                def stats(n, rows, slot, ready):
                    v.bn_stats(bst[n][:, 0:6], rows[:, 0:512])
                    st.link(v.bn_stats(bst[n][:, 6:12], rows[:, 512:1024]), alone=True)
                    v.bn_aggr(mv[n][:, slot, :], bst[n][:, :]).then_inc(S[ready], 1)

                def coef(n, s, weight, ready):
                    c1 = slice(s, s + 1)
                    st.link(v.reciprocal(rcp[n][:, c1], std[n][:, c1]))
                    st.link(v.tensor_tensor(cf[n][:, s, 0:1], rcp[n][:, c1], weight, ALU.mult))
                    v.scalar_tensor_tensor(out=cf[n][:, s, 1:2], in0=mv[n][:, s, 0:1], scalar=cf[n][:, s, 0:1], in1=weight,
                                           op0=ALU.mult, op1=ALU.subtract, reverse1=True).then_inc(S[ready], 1)

                def keep(t, v_in):
                    rows = TAIL if t.last else P
                    st.link(v.scalar_tensor_tensor(out=mask[0:rows, :], in0=v_in[0:rows, :], scalar=brk[0:rows, 1:2],
                                                   in1=v_in[0:rows, :], op0=ALU.is_le, op1=ALU.mult), alone=True)
                    st.link(v.max(top8[0:rows, t.slot, :], mask[0:rows, :]))
                    return v.tensor_copy(cand[0:rows, bass.ds(t.t * 8, 8)], top8[0:rows, t.slot, :])

                def step(k):
                    t, b, f, e = k.plus(1), k.plus(-1), k.plus(2), k.plus(3)
                    edges = e.odd == 0 and e.within(0, TILES)
                    if f.within(0, TILES):
                        dve.wait_ge(loaded[f.slot], 16 * f.turn + 16)
                        stats("x", xs[:, f.slot, :], f.slot, "x_stats_ready")
                    if edges:
                        dve.wait_ge(gathered[e.po], 32 * e.turn + 32)
                        stats("g", xg[:, e.po, :], e.slot, "g_stats_ready")
                        after(dve, S["turned"], e.t - 2)
                        v.tensor_scalar(hit[:, e.po, :], iota[:, :], edge_key[:, bass.ds(e.half, 1)], None, ALU.is_equal)\
                            .then_inc(S["hits_ready"], 1)
                    if b.within(0, TILES):
                        dve.wait_ge(S["multiplied"], b.t + 1)
                        after(dve, x1_out[b.odd], 16 * b.half)
                        after(dve, S["h0_ready"], b.t - 1)
                        v.scalar_tensor_tensor(out=x1[:, b.odd, :], in0=prod[b.odd][:, :], scalar=dout[:, bass.ds(b.t, 1)],
                                               in1=xs[:, b.slot, :], op0=ALU.mult, op1=ALU.add).then_inc(S["x1_ready"], 1)
                    if f.within(0, TILES):
                        dve.wait_ge(S["x_std_ready"], f.t + 1)
                        coef("x", f.slot, own8[:, bass.ds(f.t, 1)], "x_coef_ready")
                    if edges:
                        dve.wait_ge(S["g_std_ready"], e.half + 1)
                        coef("g", e.slot, dg[:, e.po:e.po + 1], "g_coef_ready")
                    if b.within(0, TILES):
                        dve.wait_ge(S["x1_ready"], b.t + 1)
                        stats("e", x1[:, b.odd, :], b.slot, "x1_stats_ready")
                    if t.within(0, TILES):
                        dve.wait_ge(S["y_high_ready"], t.t + 1)
                        after(dve, S["multiplied"], t.t - 1)
                        v.tensor_tensor(ylo[:, t.odd, :], zT[t.odd][:, :], yhi[:, t.odd, :], ALU.subtract)\
                            .then_inc(S["y_low_ready"], 1)
                    if b.within(0, TILES):
                        dve.wait_ge(S["x1_std_ready"], b.t + 1)
                        s = b.slot
                        st.link(v.reciprocal(cf["e"][:, s, 0:1], std["e"][:, s:s + 1]))
                        v.scalar_tensor_tensor(out=cf["e"][:, s, 1:2], in0=mv["e"][:, s, 0:1], scalar=-1.0,
                                               in1=cf["e"][:, s, 0:1], op0=ALU.mult, op1=ALU.mult)\
                            .then_inc(S["x1_coef_ready"], 1)
                    t = k.plus(-3)
                    if t.within(0, TILES):
                        dve.wait_ge(S["abs_ready"], t.t + 1)
                        if isinstance(t.i, int) and t.t < SAMPLE:
                            v.max(sam[:, t.t * 16:t.t * 16 + 8], vsam[:, t.t, 0:512])
                            v.max(sam[:, t.t * 16 + 8:t.t * 16 + 16], vsam[:, t.t, 512:1024]).then_inc(S["kept"], 1)
                        else:
                            keep(t, vs[:, t.odd, :]).then_inc(S["kept"], 1)

                def bracket():
                    dve.wait_ge(S["kept"], SAMPLE)
                    find.start(st)
                    st.link(v.memset(find.k[:, 0:1], SLO))
                    st.link(v.memset(find.k[:, 1:2], SHI))
                    for n in range(18):
                        find.round(dve, st, zT[1][:, 0:2], n, lambda cnt, thr: v.tensor_scalar(
                            mask[:, 0:SAMPLE * 16], sam[:, :], thr, None, ALU.is_ge, ALU.add, accum_out=cnt))
                    st.link(v.tensor_copy(brk[:, :], find.trial[:, :].bitcast(F32)))
                    v.tensor_scalar(nhigh[:, :], brk[:, 1:2], -1.0, None, ALU.mult).then_inc(S["bracket_ready"], 1)
                    for k in range(SAMPLE):
                        st.link(keep(Tile(0, k), vsam[:, k, :]))

                per = (2 * 4 + 2) + 4 + 2 * 4 + 2 * 2 + 2 * 4
                steps_over(dve, step, -3, LO, HI, LAST + 3, st=st, per=per, between=bracket)


    CT, CR = N // 125, 125
    with ExitStack() as c:
        ei = sb(c, "c_edges", [EP, 2, EC], I32)
        ef = sb(c, "c_edgef", [EP, 2, EC])
        own = sb(c, "c_loop", [EP, EC])
        rel = sb(c, "c_rel", [EP, 2, EC])
        hots = sb(c, "c_hots", [EP, 2, EC, CR], BF16)
        off = sb(c, "c_off", [P, 2])
        xr = sb(c, "c_x", [CR, 2, D])
        wt = sb(c, "c_w", [CR, 3])
        bst = sb(c, "c_bst", [CR, 12])
        mv = sb(c, "c_mv", [CR, 2])
        std = sb(c, "c_std", [CR, 1])
        cf = sb(c, "c_cf", [CR, 2])
        z = sb(c, "c_z", [CR, D])
        cnts = sb(c, "c_counts", [CR, CR])
        eye = sb(c, "c_eye", [P, P])
        yacc = sb(c, "c_y", [P, DC, CR])
        yh, yl = sb(c, "c_yhi", [P, DC, CR], F16), sb(c, "c_ylo", [P, DC, CR], F16)
        res = sb(c, "c_res", [CR, 2, D])
        pa = ps(c, "c_pa", [CR, CR])
        py = ps(c, "c_py", [P, DC, P])
        pp = ps(c, "c_pp", [CR, D])
        s_in, s_s, s_t, s_st, s_eye = (sem(c, "c_" + n) for n in ("edges_in", "s_in", "t_in", "stored", "eye_ready"))
        s_var, s_root, s_z, s_hot, s_a, s_as, s_y, s_ya, s_yt, s_yb, s_pp, s_res = (sem(c, "c_" + n) for n in (
            "stats_ready", "root_ready", "z_ready", "hots_ready", "counts_ready", "counts_copied", "part_ready",
            "part_added", "own_turned", "y_ready", "multiplied", "rows_ready"))
        s_dve = sem(c, "c_dve_steps")

        with nc.Block() as block:

            def crowded(eng):
                return eng.If(eng.value_load(flags[0:1, 0:1], min_val=0, max_val=1) > 0)

            @block.sync
            def _(sp):
                with crowded(sp):
                    sp.dma_start(ei[:, 0, :], src_in.rearrange("(p c) -> p c", c=EC)).then_inc(s_in, 16)
                    sp.dma_start(ei[:, 1, :], dst_in.rearrange("(p c) -> p c", c=EC)).then_inc(s_in, 16)
                    with sp.Fori(0, CT) as t:
                        sp.wait_ge(s_res, t)
                        sp.dma_start(xr[:, 0, :], x_in[bass.ds(t * CR, CR), :]).then_inc(s_t, 16)
                        sp.dma_start(wt[:, 0:1], own_dram[bass.ds(t * CR, CR), :]).then_inc(s_t, 16)
                        sp.dma_start(wt[:, 1:2], dis_dram[bass.ds(t * CR, CR), :]).then_inc(s_t, 16)
                        with sp.Fori(0, CT) as s:
                            sp.wait_ge(s_z, t * (CT + 1) + s)
                            sp.dma_start(xr[:, 1, :], x_in[bass.ds(s * CR, CR), :]).then_inc(s_s, 16)
                            sp.dma_start(wt[:, 2:3], dis_dram[bass.ds(s * CR, CR), :]).then_inc(s_s, 16)
                        sp.wait_ge(s_res, t + 1)
                        sp.dma_start(x1_dram[bass.ds(t * CR, CR), :], res[:, 0, :]).then_inc(s_st, 16)
                        sp.dma_start(h2_dram[bass.ds(t * CR, CR), :], res[:, 1, :]).then_inc(s_st, 16)
                        wait_alone(sp, s_st, 32 * t + 32)

            @block.gpsimd
            def _(pool):
                with crowded(pool):
                    nc.gpsimd.memset(eye[:, :], 0.0).then_inc(s_eye, 1)
                    pool.wait_ge(s_eye, 1)
                    nc.gpsimd.affine_select(out=eye[:, :], in_=eye[:, :], compare_op=ALU.not_equal, fill=1.0, base=0,
                                            pattern=[[-1, P]], channel_multiplier=1).then_inc(s_eye, 1)

            @block.scalar
            def _(act):
                with crowded(act):
                    with act.Fori(0, CT) as t:
                        with act.Fori(0, CT + 1) as s:
                            act.wait_ge(s_var, t * (CT + 2) + s + 1)
                            nc.scalar.activation(std[:, :], mv[:, 1:2], ACT.Sqrt, bias=eps_x[0:CR, 0:1]).then_inc(s_root, 1)
                        act.wait_ge(s_var, t * (CT + 2) + CT + 2)
                        nc.scalar.activation(std[:, :], mv[:, 1:2], ACT.Sqrt, bias=eps_xx[0:CR, 0:1],
                                             scale=1.0 + EPS_LN).then_inc(s_root, 1)

            @block.tensor
            def _(pe):
                with crowded(pe):
                    pe.wait_ge(s_eye, 2)
                    with pe.Fori(0, CT) as t:
                        with pe.Fori(0, CT) as s:
                            pe.wait_ge(s_hot, t * CT + s + 1)
                            for e in range(EC):
                                last = nc.tensor.matmul(pa[:, :], hots[:, 1, e, :], hots[:, 0, e, :],
                                                        start=(e == 0), stop=(e == EC - 1))
                            last.then_inc(s_a, 1)
                            pe.wait_ge(s_as, t * CT + s + 1)
                            for d in range(DC):
                                last = nc.tensor.matmul(py[:, d, 0:CR], z[:, d * P:(d + 1) * P], cnts[:, :],
                                                        start=True, stop=True)
                            last.then_inc(s_y, 1)
                        pe.wait_ge(s_z, (t + 1) * (CT + 1))
                        for d in range(DC):
                            last = nc.tensor.matmul(py[:, d, 0:CR], z[:, d * P:(d + 1) * P], eye[0:CR, 0:CR],
                                                    start=True, stop=True)
                        last.then_inc(s_yt, 1)
                        pe.wait_ge(s_yb, t + 1)
                        for d in range(DC):
                            for y, W in ((yh, Whi), (yh, Wlo), (yl, Whi)):
                                for h in range(2):
                                    hh = slice(h * 512, (h + 1) * 512)
                                    last = nc.tensor.matmul(pp[:, hh], y[:, d, :], W[:, d, hh],
                                                            start=(d == 0 and y is yh and W is Whi),
                                                            stop=(d == DC - 1 and y is yl))
                        last.then_inc(s_pp, 1)

            @block.vector
            def _(dve):
                v = nc.vector
                st = Steps(dve, s_dve)

                def stats(rows):
                    v.bn_stats(bst[:, 0:6], rows[:, 0:512])
                    st.link(v.bn_stats(bst[:, 6:12], rows[:, 512:1024]), alone=True)
                    v.bn_aggr(mv[:, :], bst[:, :]).then_inc(s_var, 1)

                def normalise(rows, weight, out_rows, n_root):
                    dve.wait_ge(s_root, n_root)
                    st.link(v.reciprocal(cf[:, 0:1], std[:, :]))
                    if weight is not None:
                        st.link(v.tensor_tensor(cf[:, 0:1], cf[:, 0:1], weight, ALU.mult))
                    st.link(v.scalar_tensor_tensor(out=cf[:, 1:2], in0=mv[:, 0:1], scalar=-1.0, in1=cf[:, 0:1],
                                                   op0=ALU.mult, op1=ALU.mult))
                    if weight is not None:
                        st.link(v.tensor_tensor(cf[:, 1:2], cf[:, 1:2], weight, ALU.add))
                    return v.tensor_scalar(out_rows, rows, cf[:, 0:1], cf[:, 1:2], ALU.mult, ALU.add)

                def hot(n):
                    st.link(v.tensor_scalar(rel[:, n, :], ef[:, n, :], off[0:EP, n:n + 1], None, ALU.subtract))
                    return v.tensor_tensor(hots[:, n, :, :], iota[0:EP, 0:CR].unsqueeze(1).broadcast_to([EP, EC, CR]),
                                           rel[:, n, :].unsqueeze(2).broadcast_to([EP, EC, CR]), ALU.is_equal)

                with crowded(dve):
                    dve.wait_ge(s_in, 32)
                    st.link(v.tensor_copy(ef[:, :, :], ei[:, :, :]))
                    st.link(v.tensor_tensor(own[:, :], ef[:, 0, :], ef[:, 1, :], ALU.is_equal))
                    st.link(v.scalar_tensor_tensor(out=ef[:, 0, :], in0=own[:, :], scalar=-2.0 * N, in1=ef[:, 0, :],
                                                   op0=ALU.mult, op1=ALU.add))
                    st.link(v.memset(off[:, 0:1], 0.0))
                    with dve.Fori(0, CT) as t:
                        st.enter(t, 0, 3 + CT * 8 + 16)
                        st.link(v.memset(off[:, 1:2], 0.0))
                        st.link(v.memset(yacc[:, :, :], 0.0))
                        st.link(hot(0), alone=True)
                        with dve.Fori(0, CT) as s:
                            st.enter(s, 0, 8)
                            dve.wait_ge(s_s, (t * CT + s) * 32 + 32)
                            stats(xr[:, 1, :])
                            normalise(xr[:, 1, :], wt[:, 2:3], z[:, :], t * (CT + 2) + s + 1).then_inc(s_z, 1)
                            dve.wait_ge(s_z, t * (CT + 1) + s + 1)
                            hot(1).then_inc(s_hot, 1)
                            dve.wait_ge(s_a, t * CT + s + 1)
                            v.tensor_copy(cnts[:, :], pa[:, :]).then_inc(s_as, 1)
                            dve.wait_ge(s_y, t * CT + s + 1)
                            st.link(v.tensor_tensor(yacc[:, :, :], py[:, :, 0:CR], yacc[:, :, :], ALU.add))
                            st.link(v.tensor_scalar(off[:, 1:2], off[:, 1:2], float(CR), None, ALU.add))
                        st.leave(CT)
                        dve.wait_ge(s_t, t * 48 + 48)
                        stats(xr[:, 0, :])
                        normalise(xr[:, 0, :], wt[:, 0:1], z[:, :], t * (CT + 2) + CT + 1).then_inc(s_z, 1)
                        dve.wait_ge(s_yt, t + 1)
                        st.link(v.tensor_tensor(yacc[:, :, :], py[:, :, 0:CR], yacc[:, :, :], ALU.add))
                        st.link(v.tensor_copy(yh[:, :, :], yacc[:, :, :]))
                        v.tensor_tensor(yl[:, :, :], yacc[:, :, :], yh[:, :, :], ALU.subtract).then_inc(s_yb, 1)
                        st.link(v.tensor_scalar(wt[:, 1:2], wt[:, 1:2], wsc[0:CR, 0:1], None, ALU.mult))
                        dve.wait_ge(s_pp, t + 1)
                        st.link(v.scalar_tensor_tensor(out=res[:, 0, :], in0=pp[:, :], scalar=wt[:, 1:2], in1=xr[:, 0, :],
                                                       op0=ALU.mult, op1=ALU.add))
                        stats(res[:, 0, :])
                        st.link(normalise(res[:, 0, :], None, res[:, 1, :], t * (CT + 2) + CT + 2))
                        st.link(v.tensor_tensor(res[:, 1, :], res[:, 1, :], lng[0:CR, :], ALU.mult))
                        st.link(v.tensor_scalar(off[:, 0:1], off[:, 0:1], float(CR), None, ALU.add))
                        v.tensor_tensor(res[:, 1, :], res[:, 1, :], lnb[0:CR, :], ALU.add).then_inc(s_res, 1)
                    st.leave(CT)

    with ExitStack() as c:
        part = sb(c, "part", [P, 4])
        tot = sb(c, "tot", [P, 4])
        chk = sb(c, "chk", [P, 6])
        junk = sb(c, "junk_range", [P, TILES * 8])
        find = Search(c, "range1", 1)
        psum = ps(c, "range1_sums", [P, 8])
        s_part, s_tot = sem(c, "range1_parts_ready"), sem(c, "range1_totals_ready")
        s_dve = sem(c, "range1_dve_steps")

        with nc.Block() as block:

            @block.tensor
            def _(pe):
                pe.wait_ge(s_part, 4)
                nc.tensor.matmul(psum[:, 0:4], ones[:, :], part[:, :], start=True, stop=True).then_inc(s_tot, 1)
                with pe.Fori(0, 31) as n:
                    find.sum_up(pe, psum[:, 4:5], n)

            @block.vector
            def _(dve):
                v = nc.vector
                st = Steps(dve, s_dve)
                v.tensor_reduce(part[:, 0:1], over[:, :], AX, ALU.add).then_inc(s_part, 1)
                dve.wait_ge(s_part, 1)
                v.tensor_scalar(junk[:, :], cand[:, :], brk[:, 1:2], None, ALU.is_equal, ALU.add,
                                accum_out=part[:, 1:2]).then_inc(s_part, 1)
                dve.wait_ge(s_part, 2)
                v.tensor_scalar(junk[:, :], cand[:, :], brk[:, 0:1], None, ALU.is_ge, ALU.add,
                                accum_out=part[:, 2:3]).then_inc(s_part, 1)
                dve.wait_ge(s_part, 3)
                v.tensor_scalar(junk[:, 0:TILES], cand[:, :].rearrange("p (t k) -> p t k", k=8)[:, :, 7], brk[:, 0:1], None,
                                ALU.is_ge, ALU.add, accum_out=part[:, 3:4]).then_inc(s_part, 1)
                dve.wait_ge(s_tot, 1)
                st.link(v.tensor_copy(tot[:, :], psum[:, 0:4]))
                st.link(v.tensor_tensor(chk[:, 0:1], tot[:, 0:1], tot[:, 1:2], ALU.subtract))
                st.link(v.tensor_scalar(chk[:, 0:1], chk[:, 0:1], float(N * D), 0.5, ALU.add, ALU.mult))
                st.link(v.tensor_scalar(find.k[:, :], chk[:, 0:1], -1.0, float(RANK1), ALU.mult, ALU.add))
                st.link(v.tensor_scalar(chk[:, 1:2], find.k[:, :], 1.0, None, ALU.is_lt))
                st.link(v.tensor_tensor(chk[:, 2:3], tot[:, 2:3], find.k[:, :], ALU.is_lt))
                st.link(v.tensor_scalar(chk[:, 3:4], tot[:, 3:4], 0.0, None, ALU.is_gt))
                st.link(v.tensor_copy(chk[:, 4:5], flags[:, 0:1]))
                st.link(v.tensor_reduce(flags[:, 1:2], chk[:, 1:5], AX, ALU.max))
                find.start(st)
                with dve.Fori(0, 31) as n:
                    st.enter(n, 0, find.steps())
                    find.round(dve, st, psum[:, 4:5], n, lambda cnt, thr: v.tensor_scalar(
                        junk[:, :], cand[:, :], thr, None, ALU.is_ge, ALU.add, accum_out=cnt))
                st.leave(31)
                st.link(v.tensor_copy(amax[:, 0:1], find.trial[:, 0:1].bitcast(F32)))

    with ExitStack() as c:
        hb = sb(c, "f_h2", [P, 2, D])
        junk = sb(c, "f_junk", [P, D])
        mask = sb(c, "f_mask", [P, D])
        find = Search(c, "full", 1, count_dt=F32)
        psum = ps(c, "full_sums", [P, 1])
        s_ld = [sem(c, f"full_loaded{i}") for i in range(2)]
        s_cnt, s_dve = sem(c, "full_counted_tiles"), sem(c, "full_dve_steps")

        with nc.Block() as block:

            def uncovered(eng):
                return eng.If(eng.value_load(flags[0:1, 1:2], min_val=0, max_val=1) > 0)

            @block.sync
            def _(sp):
                with uncovered(sp):
                    with sp.Fori(0, 31) as r:
                        with sp.Fori(0, LAST // 2) as i:
                            for u in range(2):
                                sp.wait_ge(s_cnt, r * TILES + i * 2 + u)
                                sp.dma_start(hb[:, u, :], h2_dram[bass.ds((i * 2 + u) * P, P), :]).then_inc(s_ld[u], 16)
                        sp.wait_ge(s_cnt, r * TILES + LAST)
                        sp.dma_start(hb[0:TAIL, 0, :], h2_dram[LAST * P:N, :]).then_inc(s_ld[0], 16)

            @block.tensor
            def _(pe):
                with uncovered(pe):
                    with pe.Fori(0, 31) as n:
                        find.sum_up(pe, psum[:, :], n)

            @block.vector
            def _(dve):
                v = nc.vector
                st = Steps(dve, s_dve)
                with uncovered(dve):
                    find.start(st)
                    st.link(v.memset(find.k[:, :], float(RANK1)))
                    st.link(v.memset(over[:, :], 0.0), alone=True)
                    with dve.Fori(0, 31) as r:
                        st.enter(r, 0, find.steps() + LAST + 1)
                        def count(u, rows, col):
                            st.link(v.scalar_tensor_tensor(out=junk[0:rows, :], in0=hb[0:rows, u, :], scalar=-1.0,
                                                           in1=hb[0:rows, u, :], op0=ALU.mult, op1=ALU.max))
                            v.tensor_scalar(mask[0:rows, :], junk[0:rows, :], find.trial[0:rows, 0:1].bitcast(F32), None,
                                            ALU.is_ge, ALU.add, accum_out=over[0:rows, col]).then_inc(s_cnt, 1)

                        with dve.Fori(0, LAST // 2) as i:
                            st.enter(i, 0, 2)
                            for u in range(2):
                                dve.wait_ge(s_ld[u], (r * (LAST // 2 + 1 - u) + i) * 16 + 16)
                                count(u, P, bass.ds(i * 2 + u, 1))
                        st.leave(LAST // 2)
                        dve.wait_ge(s_ld[0], (r * (LAST // 2 + 1) + LAST // 2) * 16 + 16)
                        count(0, TAIL, slice(LAST, TILES))
                        dve.wait_ge(s_cnt, r * TILES + TILES)
                        find.round(dve, st, psum[:, :], r, lambda cnt, thr: v.tensor_reduce(cnt, over[:, :], AX, ALU.add))
                    st.leave(31)
                    st.link(v.tensor_copy(amax[:, 0:1], find.trial[:, 0:1].bitcast(F32)))

    lay.close()

    GC = PAIRS * P
    with ExitStack() as top2:
        G = sb(top2, "G", [P, GC])
        GA = sb(top2, "GA", [P, GC])
        with ExitStack() as c:
            hb = sb(c, "h_in", [P, 4, D])
            qs = sb(c, "h_q", [P, 2, D], BF16)
            qt = sb(c, "h_qT", [P, 2, D], BF16)
            U = sb(c, "h_pre", [P, 2, P])
            identb = sb(c, "h_ident", [P, P], BF16)
            pT = [ps(c, f"h_pT{i}", [P, D], BF16) for i in range(2)]
            pu = [ps(c, f"h_pu{i}", [P, 512]) for i in range(2)]
            ld = [sem(c, f"h_loaded{i}") for i in range(4)]
            s_id, s_kap, s_q, s_T, s_qt, s_u, s_U, s_G, s_dve = (sem(c, "h_" + n) for n in (
                "ident_ready", "scales_ready", "q_ready", "turned", "qT_ready", "multiplied", "pre_ready",
                "gelu_ready", "dve_steps"))

            with nc.Block() as block:

                def tiles_over(eng, body, st=None, per=0):
                    for k in range(4):
                        body(Tile(0, k))
                    with eng.Fori(1, 19) as i:
                        if st:
                            st.enter(i, 1, per)
                        for u in range(4):
                            body(Tile(i, u))
                    if st:
                        st.leave(18)
                    for k in range(76, TILES):
                        body(Tile(0, k))

                @block.sync
                def _(sp):
                    def load(t):
                        after(sp, s_q, t.t - 3)
                        if t.last:
                            sp.dma_start(hb[0:TAIL, t.slot, :], h2_dram[LAST * P:N, :]).then_inc(ld[t.slot], 16)
                        else:
                            sp.dma_start(hb[:, t.slot, :], h2_dram[bass.ds(t.t * P, P), :]).then_inc(ld[t.slot], 16)

                    for k in range(4):
                        load(Tile(0, k))
                    with sp.Fori(1, 19) as i:
                        for u in range(4):
                            load(Tile(i, u))
                    for k in range(76, TILES):
                        load(Tile(0, k))

                @block.gpsimd
                def _(pool):
                    nc.gpsimd.memset(identb[:, :], 0.0).then_inc(s_id, 1)
                    nc.gpsimd.memset(GA[:, :], 0.0).then_inc(s_id, 1)
                    pool.wait_ge(s_id, 2)
                    nc.gpsimd.affine_select(out=identb[:, :], in_=identb[:, :], compare_op=ALU.not_equal, fill=1.0, base=0,
                                            pattern=[[-1, P]], channel_multiplier=1).then_inc(s_id, 1)

                @block.tensor
                def _(pe):
                    def step(t):
                        pe.wait_ge(s_q, t.t + 1)
                        after(pe, s_qt, t.t - 1)
                        for d in range(DC):
                            last = nc.tensor.matmul(pT[t.odd][:, d * P:(d + 1) * P], qs[:, t.odd, d * P:(d + 1) * P],
                                                    identb[:, :], start=True, stop=True, is_transpose=True)
                        last.then_inc(s_T, 1)

                    def hidden(t):
                        pe.wait_ge(s_qt, t.t + 1)
                        after(pe, s_U, t.half - 1)
                        rows = slice(t.odd * H, (t.odd + 1) * H)
                        for d in range(DC):
                            last = nc.tensor.matmul(pu[t.po][rows, 0:P], w1T[:, d, :], qt[:, t.odd, d * P:(d + 1) * P],
                                                    start=(d == 0), stop=(d == DC - 1))
                        last.then_inc(s_u, 1)

                    pe.wait_ge(s_id, 3)
                    def both(t):
                        if t.plus(1).within(0, TILES):
                            step(t.plus(1))
                        hidden(t)

                    step(Tile(0, 0))
                    tiles_over(pe, both)

                @block.scalar
                def _(act):
                    def step(t):
                        act.wait_ge(s_T, t.t + 1)
                        after(act, s_u, t.t - 1)
                        nc.scalar.activation(qt[:, t.odd, :], pT[t.odd][:, :], ACT.Copy).then_inc(s_qt, 1)
                        if t.odd or t.last:
                            rows, n = (H, TAIL) if t.last else (P, P)
                            act.wait_ge(s_U, t.half + 1)
                            nc.scalar.activation(G[0:rows, bass.ds(t.half * P, n)], U[0:rows, t.po, 0:n], ACT.Gelu)\
                                .then_inc(s_G, 1)

                    tiles_over(act, step)

                @block.vector
                def _(dve):
                    v = nc.vector
                    st = Steps(dve, s_dve)
                    st.link(v.tensor_scalar(kap[:, 2:3], amax[:, 0:1], EPS_Q, None, ALU.max))
                    st.link(v.reciprocal(kap[:, 3:4], kap[:, 2:3]))
                    st.link(v.tensor_scalar(kap[:, 0:1], kap[:, 3:4], QMAX, None, ALU.mult))
                    st.link(v.reciprocal(kap[:, 3:4], kap[:, 0:1]))
                    st.link(v.tensor_tensor(kap[:, 1:2], kap[:, 3:4], gam[:, 0:1], ALU.mult))
                    dve.wait_ge(s_id, 2)

                    def sizes(t, rows, n):
                        dve.wait_ge(s_G, t.half + 1)
                        g = G[0:rows, bass.ds(t.half * P, n)]
                        v.scalar_tensor_tensor(out=GA[0:rows, bass.ds(t.half * P, n)], in0=g, scalar=-1.0, in1=g,
                                               op0=ALU.mult, op1=ALU.max)

                    def step(t):
                        dve.wait_ge(ld[t.slot], 16 * t.turn + 16)
                        st.link(v.tensor_scalar(hb[:, t.slot, :], hb[:, t.slot, :], kap[:, 0:1], MAGIC, ALU.mult, ALU.add))
                        st.link(v.tensor_scalar(hb[:, t.slot, :], hb[:, t.slot, :], MAGIC - 128.0, MAGIC + 127.0,
                                                ALU.max, ALU.min))
                        after(dve, s_T, t.t - 1)
                        v.tensor_scalar(qs[:, t.odd, :], hb[:, t.slot, :], -MAGIC, None, ALU.add).then_inc(s_q, 1)
                        b = t.plus(-2)
                        if t.odd and b.within(0, TILES):
                            pre(b, P)
                        b = t.plus(-4)
                        if t.odd and b.within(0, TILES):
                            sizes(b, P, P)

                    def pre(t, rows):
                        dve.wait_ge(s_u, 2 * t.half + (2 if rows == P else 1))
                        after(dve, s_G, t.half - 1)
                        v.tensor_scalar(U[0:rows, t.po, :], pu[t.po][0:rows, 0:P], kap[0:rows, 1:2], None,
                                        ALU.mult).then_inc(s_U, 1)

                    tiles_over(dve, step, st, 8)
                    pre(Tile(0, 77), P)
                    sizes(Tile(0, 75), P, P)
                    pre(Tile(0, 78), H)
                    sizes(Tile(0, 77), P, P)
                    sizes(Tile(0, 78), H, TAIL)

        with ExitStack() as c:
            junk = sb(c, "r2_junk", [P, GC], BF16)
            find = Search(c, "range2", 1)
            psum = ps(c, "range2_sums", [P, 1])
            s_dve = sem(c, "range2_dve_steps")

            with nc.Block() as block:

                @block.tensor
                def _(pe):
                    with pe.Fori(0, 31) as n:
                        find.sum_up(pe, psum[:, :], n)

                @block.vector
                def _(dve):
                    v = nc.vector
                    st = Steps(dve, s_dve)
                    find.start(st)
                    st.link(v.memset(find.k[:, :], float(RANK2)))
                    with dve.Fori(0, 31) as n:
                        st.enter(n, 0, find.steps())
                        find.round(dve, st, psum[:, :], n, lambda cnt, thr: v.tensor_scalar(
                            junk[:, :], GA[:, :], thr, None, ALU.is_ge, ALU.add, accum_out=cnt))
                    st.leave(31)
                    st.link(v.tensor_scalar(kap[:, 2:3], find.trial[:, 0:1].bitcast(F32), EPS_Q, None, ALU.max))
                    st.link(v.reciprocal(kap[:, 3:4], kap[:, 2:3]))
                    st.link(v.tensor_scalar(kap[:, 4:5], kap[:, 3:4], QMAX, None, ALU.mult))
                    st.link(v.reciprocal(kap[:, 3:4], kap[:, 4:5]))
                    st.link(v.tensor_tensor(kap[:, 5:6], kap[:, 3:4], gam[:, 1:2], ALU.mult))

        with ExitStack() as c:
            xb = sb(c, "o_x1", [P, 4, D])
            ob = sb(c, "o_out", [P, 4, D])
            qf = sb(c, "o_qf", [P, P])
            q2 = sb(c, "o_q", [P, 2, P], BF16)
            po = [ps(c, f"o_po{i}", [P, D]) for i in range(4)]
            ld = [sem(c, f"o_loaded{i}") for i in range(4)]
            sd = [sem(c, f"o_stored{i}") for i in range(4)]
            s_q, s_m, s_o, s_dve = (sem(c, "o_" + n) for n in ("q_ready", "multiplied", "out_ready", "dve_steps"))

            with nc.Block() as block:

                @block.sync
                def _(sp):
                    def load(t):
                        after(sp, s_o, t.t - 3)
                        if t.last:
                            sp.dma_start(xb[0:TAIL, t.slot, :], x1_dram[LAST * P:N, :]).then_inc(ld[t.slot], 16)
                        else:
                            sp.dma_start(xb[:, t.slot, :], x1_dram[bass.ds(t.t * P, P), :]).then_inc(ld[t.slot], 16)

                    for k in range(4):
                        load(Tile(0, k))
                    with sp.Fori(1, 19) as i:
                        for u in range(4):
                            load(Tile(i, u))
                    for k in range(76, TILES):
                        load(Tile(0, k))

                @block.scalar
                def _(act):
                    def store(t):
                        act.wait_ge(s_o, t.t + 1)
                        if t.last:
                            act.dma_start(out[LAST * P:N, :], ob[0:TAIL, t.slot, :]).then_inc(sd[t.slot], 16)
                        else:
                            act.dma_start(out[bass.ds(t.t * P, P), :], ob[:, t.slot, :]).then_inc(sd[t.slot], 16)

                    with act.Fori(0, 19) as i:
                        for u in range(4):
                            store(Tile(i, u))
                    for k in range(76, TILES):
                        store(Tile(0, k))
                    for s in range(4):
                        act.wait_ge(sd[s], 16 * len(range(s, TILES, 4)))

                @block.tensor
                def _(pe):
                    def step(t):
                        pe.wait_ge(s_q, t.half + 1)
                        after(pe, s_o, t.t - 3)
                        rows = slice(t.odd * H, (t.odd + 1) * H)
                        for h in range(2):
                            last = nc.tensor.matmul(po[t.slot][:, h * 512:(h + 1) * 512], q2[rows, t.po, :],
                                                    w2T[rows, h * 512:(h + 1) * 512], start=True, stop=True)
                        last.then_inc(s_m, 1)

                    for k in range(4):
                        step(Tile(0, k))
                    with pe.Fori(1, 19) as i:
                        for u in range(4):
                            step(Tile(i, u))
                    for k in range(76, TILES):
                        step(Tile(0, k))

                @block.vector
                def _(dve):
                    v = nc.vector
                    st = Steps(dve, s_dve)

                    def quantise(t):
                        rows, n = (H, TAIL) if t.last else (P, P)
                        after(dve, s_q, t.half)
                        st.link(v.tensor_scalar(qf[0:rows, 0:n], G[0:rows, bass.ds(t.half * P, n)], kap[0:rows, 4:5], MAGIC,
                                                ALU.mult, ALU.add))
                        st.link(v.tensor_scalar(qf[0:rows, 0:n], qf[0:rows, 0:n], MAGIC - 128.0, MAGIC + 127.0, ALU.max, ALU.min))
                        after(dve, s_m, 2 * t.half - 2)
                        v.tensor_scalar(q2[0:rows, t.po, 0:n], qf[0:rows, 0:n], -MAGIC, None, ALU.add).then_inc(s_q, 1)

                    def step(t):
                        if t.odd == 0:
                            nxt = t.plus(2)
                            if nxt.within(0, TILES):
                                quantise(nxt)
                        dve.wait_ge(s_m, t.t + 1)
                        dve.wait_ge(ld[t.slot], 16 * t.turn + 16)
                        after(dve, sd[t.slot], 16 * t.turn)
                        v.scalar_tensor_tensor(out=ob[:, t.slot, :], in0=po[t.slot][:, :], scalar=kap[:, 5:6],
                                               in1=xb[:, t.slot, :], op0=ALU.mult, op1=ALU.add).then_inc(s_o, 1)

                    quantise(Tile(0, 0))
                    with dve.Fori(0, 19) as i:
                        st.enter(i, 0, 4)
                        for u in range(4):
                            step(Tile(i, u))
                    st.leave(19)
                    for k in range(76, TILES):
                        step(Tile(0, k))

    top.close()


def kernel(x, src, dst, L0_gnn_W, L0_gnn_b, L0_ffn_ln_g, L0_ffn_ln_b, L0_ffn_w1, L0_ffn_w2):
    import concourse.bacc as bacc
    import numpy as np
    from concourse.bass_utils import run_bass_kernel_spmd

    nc = bacc.Bacc("TRN2", target_bir_lowering=False, num_devices=1)
    given = {"x": x, "src": src, "dst": dst, "W": L0_gnn_W, "b": L0_gnn_b, "ln_g": L0_ffn_ln_g, "ln_b": L0_ffn_ln_b,
             "w1": L0_ffn_w1, "w2": L0_ffn_w2}
    arrays = {"in_" + k: np.ascontiguousarray(a) for k, a in given.items()}
    ins = [nc.dram_tensor(k, a.shape, mybir.dt.from_np(a.dtype), kind="ExternalInput").ap() for k, a in arrays.items()]
    out = nc.dram_tensor("out_rows", (N, D), F32, kind="ExternalOutput").ap()
    build(nc, *ins, out)
    return run_bass_kernel_spmd(nc, [arrays], core_ids=[0]).results[0]["out_rows"]
```

```python
from contextlib import ExitStack

import concourse.bass as bass
from concourse import mybir
from concourse.alu_op_type import AluOpType as ALU

F32, F16, BF16, I32 = mybir.dt.float32, mybir.dt.float16, mybir.dt.bfloat16, mybir.dt.int32
ACT = mybir.ActivationFunctionType
AX = mybir.AxisListType.X
RMAX = bass.bass_isa.ReduceOp.max

P = 128
N, D, H, E = 10000, 1024, 64, 12500
DC = D // P
TILES = -(-N // P)
LAST = TILES - 1
TAIL = N - LAST * P
PAIRS = -(-TILES // 2)
GROUP = 2 * P
EP, EC = 125, 100
assert EP * EC == E
EPS_LN = 1e-5
EPS_Q = 1e-5
QMAX = 127.0
MAGIC = 1.5 * 2.0 ** 23
ZS = 0.125
SAMPLE = 8
RANK1 = N * D - 10188799
RANK2 = N * H - 636799
SRANK = RANK1 * SAMPLE * P / N
SLO, SHI = float(round(SRANK * 1.08)), float(round(SRANK * 0.92))
SBITS = 16
NPAD = TILES * P


class Tile:

    def __init__(self, i, c):
        self.i, self.c = i, c
        self.slot, self.odd = c % 4, c % 2
        self.po = (c // 2) % 2
        self.last = isinstance(i, int) and 4 * i + c == LAST

    @property
    def t(self):
        return 4 * self.i + self.c

    @property
    def turn(self):
        return self.i + self.c // 4

    @property
    def half(self):
        return 2 * self.i + self.c // 2

    def plus(self, n):
        return Tile(self.i, self.c + n)

    def within(self, lo, hi):
        return not isinstance(self.i, int) or lo <= self.t < hi


def after(eng, sem, n):
    if not isinstance(n, int) or n > 0:
        eng.wait_ge(sem, n)


def wait_alone(eng, sem, n):
    eng.wait_ge(sem, n)
    if not isinstance(n, int):
        eng.nop(nofuse=True)


class Steps:

    def __init__(self, eng, sem):
        self.eng, self.sem, self.base, self.n, self.outer = eng, sem, 0, 0, []

    def link(self, ins, alone=False):
        self.n += 1
        ins.then_inc(self.sem, 1)
        if alone:
            wait_alone(self.eng, self.sem, self.base + self.n)
        else:
            self.eng.wait_ge(self.sem, self.base + self.n)

    def enter(self, i, first, per):
        self.outer.append((self.base, self.n, per))
        self.base, self.n = self.base + self.n - first * per + per * i, 0

    def leave(self, turns):
        base, n, per = self.outer.pop()
        assert self.n == per, (self.n, per)
        self.base, self.n = base, n + turns * per


def build(nc, x_in, src_in, dst_in, w_in, b_in, lng_in, lnb_in, w1_in, w2_in, out):
    top = ExitStack()

    def dram(name, shape, dt=F32):
        return nc.dram_tensor(name, shape, dt, kind="Internal").ap()

    x1_dram, h2_dram = dram("x1_rows", (N, D)), dram("h2_rows", (N, D))
    dis_dram = dram("dis_table", (NPAD, 1))
    own_dram = dram("own_table", (NPAD, 1))

    def sb(ctx, name, shape, dt=F32):
        return ctx.enter_context(nc.sbuf_tensor(name, shape, dt))

    def ps(ctx, name, shape, dt=F32):
        return ctx.enter_context(nc.psum_tensor(name, shape, dt))

    def sem(ctx, name):
        return ctx.enter_context(nc.semaphore(name))

    iota = sb(top, "iota", [P, GROUP])
    ones = sb(top, "ones", [P, P])
    ones16 = sb(top, "ones16", [P, P], F16)
    dis8 = sb(top, "dis8", [P, TILES])
    own8 = sb(top, "own8", [P, TILES])
    dout = sb(top, "dout", [P, TILES])
    edge_row = sb(top, "edge_row", [P, PAIRS], I32)
    edge_key = sb(top, "edge_key", [P, PAIRS])
    w1T = sb(top, "w1T", [P, DC, H], BF16)
    w2T = sb(top, "w2T", [P, D], BF16)
    gam = sb(top, "gam", [P, 2])
    flags = sb(top, "flags", [P, 3], I32)
    mag = sb(top, "mag", [P, 1])
    eps_x = sb(top, "eps_x", [P, 1])
    eps_xx = sb(top, "eps_xx", [P, 1])
    amax = sb(top, "amax", [P, 2])
    wsc = sb(top, "wsc", [P, 1])
    kap = sb(top, "kap", [P, 8])

    lay = ExitStack()
    Whi = sb(lay, "Whi", [P, DC, D], F16)
    Wlo = sb(lay, "Wlo", [P, DC, D], F16)
    ident = sb(lay, "ident", [P, P], F16)
    lng = sb(lay, "lng", [P, D])
    lnb = sb(lay, "lnb", [P, D])
    cand = sb(lay, "cand", [P, TILES * 8])
    over = sb(lay, "over", [P, TILES])
    brk = sb(lay, "brk", [P, 2])
    nhigh = sb(lay, "nhigh", [P, 1])

    with ExitStack() as c:
        ei = sb(c, "ei", [EP, 2, EC], I32)
        parts = sb(c, "parts", [EP, 6, EC], I32)
        fl = sb(c, "fl", [EP, 6, EC])
        loop = sb(c, "loop", [EP, EC])
        nonloop = sb(c, "nonloop", [EP, EC])
        group = sb(c, "group", [EP, EC])
        rank = sb(c, "rank", [EP, EC])
        hot_lo = sb(c, "hot_lo", [EP, EC, P], BF16)
        room = sb(c, "room", [EP, EC * 2 * TILES], BF16)
        hot_hi = room[:, :].rearrange("p (c a t) -> p c a t", a=2, t=TILES)
        vals = room[:, 0:EC * 3 * PAIRS].rearrange("p (c a t) -> p c a t", a=3, t=PAIRS)
        hot_g = sb(c, "hot_g", [EP, PAIRS, EC])
        run = sb(c, "run", [EP, PAIRS, EC])
        ends = sb(c, "ends", [EP, 2, PAIRS])
        upper = sb(c, "upper", [EP, EP])
        base = sb(c, "base", [EP, PAIRS])
        small = sb(c, "small", [P, 16])
        smalli = sb(c, "smalli", [P, 4], I32)
        degs = sb(c, "degs", [P, 4, TILES])
        tab = sb(c, "tab", [P, 3, PAIRS])
        wn = sb(c, "wn", [P, DC, D])
        bn = sb(c, "bn", [P, DC])
        wsum = sb(c, "wsum", [P, DC])
        wabs = sb(c, "wabs", [P, 2, DC])
        identf = sb(c, "identf", [P, P])
        identb = sb(c, "identb", [P, P], BF16)
        w1n = sb(c, "w1n", [H, D])
        w1q = sb(c, "w1q", [H, D], BF16)
        w2n = sb(c, "w2n", [P, DC, H])
        w2q = sb(c, "w2q", [P, DC, 2, H], BF16)
        junk = sb(c, "junk_prep", [P, D], BF16)
        pw = [ps(c, f"pw{i}", [P, D]) for i in range(2)]
        pdeg = ps(c, "pdeg", [P, 2 * TILES])
        ptab = ps(c, "ptab", [P, 3 * PAIRS])
        pcnt = ps(c, "pcnt", [P, 96])
        pt = ps(c, "pt", [P, D], BF16)

        s_edges, s_w, s_small, s_tab = (sem(c, n) for n in ("edges_in", "w_in", "weights_in", "tables_out"))
        s_const = sem(c, "constants_ready")
        s_hot, s_hh, s_deg = sem(c, "degree_low_hots_ready"), sem(c, "degree_high_hots_ready"), sem(c, "degrees_counted")
        s_std, s_inv = sem(c, "degree_roots_ready"), sem(c, "degree_tables_ready")
        s_tot, s_off = sem(c, "group_counts_ready"), sem(c, "group_offsets_ready")
        s_val, s_slots = sem(c, "table_hots_ready"), sem(c, "table_filled")
        s_rs, s_sh, s_wp = sem(c, "w_row_sums_ready"), sem(c, "w_shifts_ready"), sem(c, "w_shifted")
        s_mx, s_armx = sem(c, "w_row_max_ready"), sem(c, "w_max_ready")
        s_sc = sem(c, "w_scale_ready")
        s_wt, s_whi, s_wlo = sem(c, "w_turned"), sem(c, "w_high_ready"), sem(c, "w_low_ready")
        s_abs, s_gs, s_tq, s_tt = (sem(c, n) for n in ("ffn_abs_sums", "ffn_sums_ready", "ternary_ready", "ternary_turned"))
        s_tc = sem(c, "ternary_copied")
        s_parts, s_grp, s_rank = sem(c, "node_parts_ready"), sem(c, "group_hots_ready"), sem(c, "ranks_ready")
        s_dve = sem(c, "prepare_dve_steps")
        s_pool = sem(c, "prepare_pool_steps")
        s_act = sem(c, "prepare_act_steps")

        with nc.Block() as block:

            @block.sync
            def _(sp):
                sp.dma_start(ei[:, 0, :], src_in.rearrange("(p c) -> p c", c=EC)).then_inc(s_edges, 16)
                sp.dma_start(ei[:, 1, :], dst_in.rearrange("(p c) -> p c", c=EC)).then_inc(s_edges, 16)
                sp.dma_start(wn[:, :, :], w_in.rearrange("(k p) d -> p k d", p=P)).then_inc(s_w, 16)
                sp.dma_start(bn[:, :], b_in.rearrange("(k p) -> p k", p=P),
                             allow_slow_non_contiguous=True).then_inc(s_w, 16)
                sp.dma_start(w1n[:, :], w1_in).then_inc(s_small, 16)
                sp.dma_start(w2n[:, :, :], w2_in.rearrange("(k p) h -> p k h", p=P)).then_inc(s_small, 16)
                sp.dma_start(lng[:, :], lng_in.partition_broadcast(P)).then_inc(s_small, 16)
                sp.dma_start(lnb[:, :], lnb_in.partition_broadcast(P)).then_inc(s_small, 16)
                sp.wait_ge(s_inv, 2)
                sp.dma_start(dis_dram.rearrange("(t p) a -> p (t a)", p=P), dis8[:, :],
                             allow_slow_non_contiguous=True).then_inc(s_tab, 16)
                sp.dma_start(own_dram.rearrange("(t p) a -> p (t a)", p=P), own8[:, :],
                             allow_slow_non_contiguous=True).then_inc(s_tab, 16)
                sp.wait_ge(s_tab, 32)
                sp.wait_ge(s_small, 64)

            @block.gpsimd
            def _(pool):
                nc.gpsimd.memset(flags[:, :], 0).then_inc(s_const, 1)
                nc.gpsimd.iota(iota[:, :], [[1, GROUP]], base=0, channel_multiplier=0,
                               allow_small_or_imprecise_dtypes=True).then_inc(s_const, 1)
                nc.gpsimd.memset(ones[:, :], 1.0).then_inc(s_const, 1)
                nc.gpsimd.memset(ones16[:, :], 1.0).then_inc(s_const, 1)
                nc.gpsimd.memset(ident[:, :], 0.0).then_inc(s_pool, 1)
                nc.gpsimd.memset(identf[:, :], 0.0).then_inc(s_pool, 1)
                nc.gpsimd.memset(identb[:, :], 0.0).then_inc(s_pool, 1)
                nc.gpsimd.memset(upper[:, :], 1.0).then_inc(s_pool, 1)
                pool.wait_ge(s_pool, 4)
                for m in (ident, identf, identb):
                    nc.gpsimd.affine_select(out=m[:, :], in_=m[:, :], compare_op=ALU.not_equal, fill=1.0, base=0,
                                            pattern=[[-1, P]], channel_multiplier=1).then_inc(s_const, 1)
                nc.gpsimd.affine_select(out=upper[:, :], in_=upper[:, :], compare_op=ALU.is_gt, fill=0.0, base=0,
                                        pattern=[[1, EP]], channel_multiplier=-1).then_inc(s_const, 1)
                nc.gpsimd.memset(mag[:, :], -MAGIC).then_inc(s_const, 1)
                nc.gpsimd.memset(eps_x[:, :], EPS_LN).then_inc(s_const, 1)
                nc.gpsimd.memset(eps_xx[:, :], EPS_LN * EPS_LN).then_inc(s_const, 1)
                nc.gpsimd.memset(cand[:, :], 0.0).then_inc(s_const, 1)
                nc.gpsimd.memset(over[:, :], 0.0).then_inc(s_const, 1)
                pool.wait_ge(s_hh, 1)
                pool.wait_ge(s_parts, 2)
                nc.gpsimd.tensor_tensor(hot_hi[:, :, 1, :], hot_hi[:, :, 0, :],
                                        loop[:, :].unsqueeze(2).broadcast_to([EP, EC, TILES]), ALU.mult).then_inc(s_hh, 1)
                pool.wait_ge(s_mx, 1)
                nc.gpsimd.partition_all_reduce(small[:, 1:2], small[:, 0:1], P, RMAX).then_inc(s_armx, 1)
                pool.wait_ge(s_deg, 1)
                hgc = hot_g[:, :, :].rearrange("p t c -> p c t")
                pool.wait_ge(s_grp, 1)
                for n, m in ((0, 4), (1, 5)):
                    nc.gpsimd.tensor_tensor(vals[:, :, n, :], hgc, fl[:, m, :].unsqueeze(2).broadcast_to([EP, EC, PAIRS]),
                                            ALU.mult).then_inc(s_val, 1)

            @block.scalar
            def _(act):
                act.wait_ge(s_w, 32)
                for k in range(DC):
                    if k:
                        act.wait_ge(s_rs, k)
                    nc.scalar.activation(junk[:, :], wn[:, k, :], ACT.Copy, accum_out=wsum[:, k:k + 1]).then_inc(s_rs, 1)
                for k in range(DC):
                    act.wait_ge(s_rs, DC + k)
                    nc.scalar.activation(junk[:, :], wn[:, k, :], ACT.Abs, accum_out=wabs[:, 0, k:k + 1]).then_inc(s_rs, 1)
                act.wait_ge(s_rs, 2 * DC)
                act.wait_ge(s_sh, 1)
                for k in range(DC):
                    nc.scalar.activation(wn[:, k, :], wn[:, k, :], ACT.Identity, bias=wsum[:, k:k + 1]).then_inc(s_wp, 1)
                act.wait_ge(s_small, 64)
                nc.scalar.activation(junk[0:H, :], w1n[:, :], ACT.Abs, accum_out=small[0:H, 4:5]).then_inc(s_abs, 1)
                act.wait_ge(s_abs, 1)
                nc.scalar.activation(junk[:, 0:DC * H], w2n[:, :, :].rearrange("p k h -> p (k h)"), ACT.Abs,
                                     accum_out=small[:, 5:6]).then_inc(s_abs, 1)
                act.wait_ge(s_deg, 1)
                act.wait_ge(s_const, 13)
                nc.scalar.activation(degs[:, 0, :], pdeg[:, 0:TILES], ACT.Sqrt, bias=ones[:, 0:1]).then_inc(s_std, 1)
                act.wait_ge(s_sc, 1)
                for d in range(DC):
                    act.wait_ge(s_wt, d + 1)
                    nc.scalar.activation(Whi[:, d, :], pw[d % 2][:, :], ACT.Copy, scale=small[:, 2:3]).then_inc(s_whi, 1)
                act.wait_ge(s_tt, 1)
                nc.scalar.activation(w1T[:, :, :].rearrange("p k h -> p (k h)"), pt[:, 0:DC * H], ACT.Copy).then_inc(s_tc, 1)
                act.wait_ge(s_tt, 2)
                nc.scalar.activation(w2T[:, :], pt[:, :], ACT.Copy).then_inc(s_tc, 1)

            @block.tensor
            def _(pe):
                def fill_table():
                    pe.wait_ge(s_val, 4)
                    for e in range(EC):
                        last = nc.tensor.matmul(ptab[:, :], hot_lo[:, e, :], vals[:, e, :, :].rearrange("p a t -> p (a t)"),
                                                start=(e == 0), stop=(e == EC - 1))
                    last.then_inc(s_slots, 1)

                pe.wait_ge(s_const, 13)
                pe.wait_ge(s_tot, 1)
                nc.tensor.matmul(pcnt[0:EP, 0:PAIRS], upper[:, :], ends[:, 1, :], start=True, stop=True)
                nc.tensor.matmul(pcnt[:, 48:48 + PAIRS], ones[0:EP, :], ends[:, 1, :],
                                 start=True, stop=True).then_inc(s_off, 1)
                pe.wait_ge(s_hot, 1)
                pe.wait_ge(s_hh, 2)
                for e in range(EC):
                    last = nc.tensor.matmul(pdeg[:, :], hot_lo[:, e, :], hot_hi[:, e, :, :].rearrange("p a t -> p (a t)"),
                                            start=(e == 0), stop=(e == EC - 1))
                last.then_inc(s_deg, 1)
                pe.wait_ge(s_abs, 2)
                pe.wait_ge(s_rank, 2)
                nc.tensor.matmul(pcnt[:, 90:91], ones[0:H, :], small[0:H, 4:5], start=True, stop=True)
                nc.tensor.matmul(pcnt[:, 91:92], ones[:, :], small[:, 5:6], start=True, stop=True).then_inc(s_gs, 1)
                pe.wait_ge(s_wp, DC)
                for d in range(DC):
                    if d == 2:
                        fill_table()
                    if d >= 2:
                        pe.wait_ge(s_whi, d - 1)
                        pe.wait_ge(s_wlo, d - 1)
                    for k in range(DC):
                        last = nc.tensor.matmul(pw[d % 2][:, k * P:(k + 1) * P], wn[:, k, d * P:(d + 1) * P], identf[:, :],
                                                start=True, stop=True, is_transpose=True)
                    last.then_inc(s_wt, 1)
                pe.wait_ge(s_tq, 2)
                for k in range(DC):
                    last = nc.tensor.matmul(pt[:, k * H:(k + 1) * H], w1q[:, k * P:(k + 1) * P], identb[0:H, 0:H],
                                            start=True, stop=True, is_transpose=True)
                last.then_inc(s_tt, 1)
                pe.wait_ge(s_tc, 1)
                for k in range(DC):
                    last = nc.tensor.matmul(pt[:, k * P:(k + 1) * P], w2q[:, k, :, :].rearrange("p a h -> p (a h)"),
                                            identb[:, :], start=True, stop=True, is_transpose=True)
                last.then_inc(s_tt, 1)

            @block.vector
            def _(dve):
                st = Steps(dve, s_dve)
                v = nc.vector
                dve.wait_ge(s_edges, 32)
                dve.wait_ge(s_const, 13)
                for n, (a, op, k) in enumerate(((0, ALU.logical_shift_right, 7), (0, ALU.bitwise_and, P - 1),
                                                (0, ALU.logical_shift_right, 8), (0, ALU.bitwise_and, GROUP - 1),
                                                (1, ALU.logical_shift_right, 7), (1, ALU.bitwise_and, P - 1))):
                    last = v.tensor_scalar(parts[:, n, :], ei[:, a, :], k, None, op)
                st.link(last)
                v.tensor_copy(fl[:, :, :], parts[:, :, :]).then_inc(s_parts, 1)
                dve.wait_ge(s_parts, 1)
                v.tensor_tensor(loop[:, :], ei[:, 0, :], ei[:, 1, :], ALU.is_equal).then_inc(s_parts, 1)
                dve.wait_ge(s_parts, 2)
                st.link(v.tensor_scalar(nonloop[:, :], loop[:, :], -1.0, 1.0, ALU.mult, ALU.add))
                st.link(v.scalar_tensor_tensor(out=group[:, :], in0=fl[:, 2, :], scalar=1.0, in1=nonloop[:, :],
                                               op0=ALU.add, op1=ALU.mult))
                st.link(v.tensor_scalar(group[:, :], group[:, :], -1.0, None, ALU.add))
                v.tensor_tensor(hot_g[:, :, :], iota[0:EP, 0:PAIRS].unsqueeze(2).broadcast_to([EP, PAIRS, EC]),
                                group[:, :].unsqueeze(1).broadcast_to([EP, PAIRS, EC]), ALU.is_equal).then_inc(s_grp, 1)
                dve.wait_ge(s_grp, 1)
                hg = hot_g[:, :, :].rearrange("p t c -> p (t c)")
                st.link(v.tensor_tensor_scan(run[:, :, :].rearrange("p t c -> p (t c)"), hg, hg, 0.0, ALU.add, ALU.max))
                st.link(v.memset(ends[:, 0, 0:1], 0.0))
                st.link(v.tensor_copy(ends[:, 0, 1:PAIRS], run[:, 0:PAIRS - 1, EC - 1]))
                st.link(v.tensor_tensor(ends[:, 1, :], run[:, :, EC - 1], ends[:, 0, :], ALU.subtract))
                v.engine_nop().then_inc(s_tot, 1)
                v.tensor_tensor(hot_hi[:, :, 0, :], iota[0:EP, 0:TILES].unsqueeze(1).broadcast_to([EP, EC, TILES]),
                                fl[:, 0, :].unsqueeze(2).broadcast_to([EP, EC, TILES]), ALU.is_equal).then_inc(s_hh, 1)
                v.tensor_tensor(hot_lo[:, :, :], iota[0:EP, 0:P].unsqueeze(1).broadcast_to([EP, EC, P]),
                                fl[:, 1, :].unsqueeze(2).broadcast_to([EP, EC, P]), ALU.is_equal).then_inc(s_hot, 1)
                dve.wait_ge(s_rs, 2 * DC)
                st.link(v.tensor_tensor(wsum[:, :], bn[:, :], wsum[:, :], ALU.subtract))
                v.tensor_scalar(wsum[:, :], wsum[:, :], 1.0 / D, None, ALU.mult).then_inc(s_sh, 1)
                dve.wait_ge(s_sh, 1)
                st.link(v.scalar_tensor_tensor(out=wabs[:, 1, :], in0=wsum[:, :], scalar=-1.0, in1=wsum[:, :],
                                               op0=ALU.mult, op1=ALU.max))
                st.link(v.tensor_tensor(wabs[:, 0, :], wabs[:, 0, :], wabs[:, 1, :], ALU.add))
                v.tensor_reduce(small[:, 0:1], wabs[:, 0, :], AX, ALU.max).then_inc(s_mx, 1)
                dve.wait_ge(s_off, 1)
                st.link(v.scalar_tensor_tensor(out=base[:, :], in0=pcnt[0:EP, 0:PAIRS], scalar=-1.0, in1=ends[:, 0, :],
                                               op0=ALU.add, op1=ALU.subtract))
                st.link(v.tensor_tensor(run[:, :, :], run[:, :, :], base[:, :].unsqueeze(2).broadcast_to([EP, PAIRS, EC]), ALU.add))
                st.link(v.tensor_tensor(run[:, :, :], run[:, :, :], hot_g[:, :, :], ALU.mult))
                v.tensor_reduce(rank[:, :], run[:, :, :].rearrange("p t c -> p c t"), AX, ALU.add).then_inc(s_rank, 1)
                v.tensor_reduce(small[:, 6:7], pcnt[:, 48:48 + PAIRS], AX, ALU.max).then_inc(s_rank, 1)
                dve.wait_ge(s_rank, 2)
                st.link(v.tensor_scalar(flags[:, 0:1], small[:, 6:7], float(P), None, ALU.is_gt))
                dve.wait_ge(s_armx, 1)
                st.link(v.tensor_scalar(smalli[:, 0:1], small[:, 1:2].bitcast(I32), 0x7F800000, None, ALU.bitwise_and))
                st.link(v.tensor_scalar(small[:, 3:4], smalli[:, 0:1].bitcast(F32), 2.0 ** -60, None, ALU.max))
                st.link(v.reciprocal(small[:, 2:3], small[:, 3:4]))
                st.link(v.tensor_scalar(small[:, 2:3], small[:, 2:3], 2.0 ** 14, None, ALU.mult))
                v.tensor_scalar(wsc[:, :], small[:, 3:4], 2.0 ** -14 / ZS / ZS, None, ALU.mult).then_inc(s_sc, 1)
                dve.wait_ge(s_deg, 1)
                v.tensor_tensor(hot_lo[:, :, :], iota[0:EP, 0:P].unsqueeze(1).broadcast_to([EP, EC, P]),
                                rank[:, :].unsqueeze(2).broadcast_to([EP, EC, P]), ALU.is_equal).then_inc(s_val, 1)
                st.link(v.tensor_scalar(group[:, :], fl[:, 3, :], 1.0, None, ALU.add))
                v.tensor_tensor(vals[:, :, 2, :], hot_g[:, :, :].rearrange("p t c -> p c t"),
                                group[:, :].unsqueeze(2).broadcast_to([EP, EC, PAIRS]), ALU.mult).then_inc(s_val, 1)
                dve.wait_ge(s_std, 1)
                dve.wait_ge(s_sc, 1)
                st.link(v.tensor_scalar(degs[:, 3, :], pdeg[:, 0:TILES], 1.0, -0.5, ALU.add, ALU.mult))
                st.link(v.reciprocal(degs[:, 1, :], degs[:, 0, :]))
                st.link(v.tensor_tensor(degs[:, 2, :], degs[:, 1, :], degs[:, 1, :], ALU.mult))
                st.link(v.tensor_tensor(degs[:, 2, :], degs[:, 2, :], degs[:, 3, :], ALU.mult))
                st.link(v.tensor_scalar(degs[:, 2, :], degs[:, 2, :], 1.5, ZS, ALU.add, ALU.mult))
                v.tensor_tensor(dis8[:, :], degs[:, 2, :], degs[:, 1, :], ALU.mult).then_inc(s_inv, 1)
                dve.wait_ge(s_inv, 1)
                st.link(v.tensor_scalar(dout[:, :], dis8[:, :], wsc[:, 0:1], None, ALU.mult))
                v.scalar_tensor_tensor(out=own8[:, :], in0=pdeg[:, TILES:2 * TILES], scalar=1.0, in1=dis8[:, :],
                                       op0=ALU.add, op1=ALU.mult).then_inc(s_inv, 1)
                dve.wait_ge(s_gs, 1)
                st.link(v.tensor_scalar(gam[:, :], pcnt[:, 90:92], 1.0 / (H * D), EPS_Q, ALU.mult, ALU.add))
                st.link(v.reciprocal(small[:, 8:10], gam[:, :]))
                for n, (w, q, rows) in enumerate(((w1n[:, :], w1q[:, :], H), (w2n[:, :, :], w2q[:, :, 0, :], P))):
                    st.link(v.tensor_scalar(w, w, small[0:rows, 8 + n:9 + n], MAGIC, ALU.mult, ALU.add))
                    st.link(v.tensor_scalar(w, w, MAGIC - 1.0, MAGIC + 1.0, ALU.max, ALU.min))
                    if n == 0:
                        v.tensor_scalar(q, w, -MAGIC, None, ALU.add).then_inc(s_tq, 1)
                    else:
                        st.link(v.tensor_scalar(q, w, -MAGIC, None, ALU.add))
                v.tensor_copy(w2q[:, :, 1, :], w2q[:, :, 0, :]).then_inc(s_tq, 1)
                for d in range(DC):
                    dve.wait_ge(s_whi, d + 1)
                    v.scalar_tensor_tensor(out=Wlo[:, d, :], in0=pw[d % 2][:, :], scalar=small[:, 2:3], in1=Whi[:, d, :],
                                           op0=ALU.mult, op1=ALU.subtract).then_inc(s_wlo, 1)
                dve.wait_ge(s_slots, 1)
                st.link(v.tensor_copy(tab[:, :, :].rearrange("p a t -> p (a t)"), ptab[:, :]))
                st.link(v.scalar_tensor_tensor(out=edge_row[:, :], in0=tab[:, 0, :], scalar=float(P), in1=tab[:, 1, :],
                                               op0=ALU.mult, op1=ALU.add))
                st.link(v.tensor_scalar(edge_key[:, :], tab[:, 2, :], -1.0, None, ALU.add))

    class Search:

        def __init__(self, ctx, name, width, top_bit=30, count_dt=F16):
            self.w, self.top_bit = width, top_bit
            self.bit = sb(ctx, name + "_bit", [P, 2], I32)
            self.trial = sb(ctx, name + "_trial", [P, width], I32)
            self.less = sb(ctx, name + "_less", [P, width], I32)
            self.cnt = sb(ctx, name + "_count", [P, width], count_dt)
            self.k = sb(ctx, name + "_rank", [P, width])
            self.ones = ones16 if count_dt == F16 else ones
            self.counted, self.summed = sem(ctx, name + "_counted"), sem(ctx, name + "_summed")

        def start(self, st):
            v = nc.vector
            v.memset(self.trial[:, :], 1 << self.top_bit)
            v.memset(self.bit[:, 0:1], 1 << self.top_bit)
            st.link(v.memset(self.bit[:, 1:2], 1 << (self.top_bit - 1)))

        def round(self, dve, st, total, n, count, first=False):
            v = nc.vector
            for j in range(self.w):
                last = count(self.cnt[:, j:j + 1], self.trial[:, j:j + 1].bitcast(F32))
                if j < self.w - 1:
                    st.link(last)
            last.then_inc(self.counted, 1)
            if not first:
                st.link(v.tensor_scalar(self.bit[:, :], self.bit[:, :], 1, None, ALU.logical_shift_right))
            dve.wait_ge(self.summed, n + 1)
            for j in range(self.w):
                last = v.scalar_tensor_tensor(out=self.less[:, j:j + 1], in0=total[:, j:j + 1], scalar=self.k[:, j:j + 1],
                                              in1=self.bit[:, 0:1], op0=ALU.is_lt, op1=ALU.mult)
            st.link(last)
            for j in range(self.w):
                last = v.scalar_tensor_tensor(out=self.trial[:, j:j + 1], in0=self.trial[:, j:j + 1],
                                              scalar=self.less[:, j:j + 1], in1=self.bit[:, 1:2],
                                              op0=ALU.bitwise_xor, op1=ALU.bitwise_or)
            st.link(last)

        def steps(self):
            return self.w + 2

        def rounds(self, dve, st, total, count):
            for n in range(31):
                self.round(dve, st, total, n, count, first=(n == 0))

        def sums(self, pe, total):
            for n in range(31):
                self.sum_up(pe, total, n)

        def sum_up(self, pe, total, n):
            pe.wait_ge(self.counted, n + 1)
            nc.tensor.matmul(total, self.ones[:, :], self.cnt[:, :], start=True, stop=True).then_inc(self.summed, 1)

    with ExitStack() as c:
        xs = sb(c, "xs", [P, 4, D])
        xg = sb(c, "xg", [P, 2, D])
        rowc = sb(c, "rowc", [P, 2], I32)
        dg = sb(c, "dg", [P, 2])
        hit = sb(c, "hit", [P, 2, GROUP], F16)
        z32 = sb(c, "z32", [P, D])
        zg32 = sb(c, "zg32", [P, D])
        zhi, zlo = sb(c, "zhi", [P, 2, D], F16), sb(c, "zlo", [P, 2, D], F16)
        zghi, zglo = sb(c, "zghi", [P, 2, D], F16), sb(c, "zglo", [P, 2, D], F16)
        yhi, ylo = sb(c, "yhi", [P, 2, D], F16), sb(c, "ylo", [P, 2, D], F16)
        x1 = sb(c, "x1", [P, 2, D])
        hs = sb(c, "hs", [P, 4, D])
        vs = sb(c, "vs", [P, 2, D])
        vsam = sb(c, "vsam", [P, SAMPLE, D])
        sam = sb(c, "sam", [P, SAMPLE * 16])
        mask = sb(c, "mask", [P, D])
        top8 = sb(c, "top8", [P, 4, 8])
        junk = sb(c, "junk_layers", [P, D], BF16)
        bst = {n: sb(c, "bst_" + n, [P, 12]) for n in "xge"}
        mv = {n: sb(c, "mv_" + n, [P, 4, 2]) for n in "xge"}
        std = {n: sb(c, "std_" + n, [P, 4]) for n in "xge"}
        rcp = {n: sb(c, "rcp_" + n, [P, 4]) for n in "xge"}
        cf = {n: sb(c, "cf_" + n, [P, 4, 2]) for n in "xge"}
        zT = [ps(c, f"zT{i}", [P, D]) for i in range(2)]
        prod = [ps(c, f"prod{i}", [P, D]) for i in range(2)]

        loaded = [sem(c, f"x_loaded{i}") for i in range(4)]
        gathered = [sem(c, f"neighbours_loaded{i}") for i in range(2)]
        x1_out = [sem(c, f"x1_stored{i}") for i in range(2)]
        h2_out = [sem(c, f"h2_stored{i}") for i in range(4)]
        names = ("x_stats_ready x_std_ready x_coef_ready x_z_ready x_high_ready x_low_ready g_stats_ready g_std_ready "
                 "hits_ready g_coef_ready g_z_ready g_high_ready g_low_ready turned y_high_ready y_low_ready multiplied x1_ready "
                 "x1_stats_ready x1_std_ready x1_coef_ready h0_ready h1_ready h2_ready abs_ready kept "
                 "bracket_ready rows_picked layers_dve_steps layers_act_steps").split()
        S = {n: sem(c, n) for n in names}
        find = Search(c, "sample", 2)

        def steps_over(eng, body, first, lo, hi, last, st=None, per=0, between=None, late=None, late_per=0):
            for k in range(first, lo):
                if between and k == SAMPLE + 3:
                    between()
                body(Tile(0, k))
            if late:
                with eng.Fori(lo // 4, (lo + SAMPLE) // 4) as i:
                    if st:
                        st.enter(i, lo // 4, per + late_per)
                    for u in range(4):
                        late(Tile(i, u))
                if st:
                    st.leave(SAMPLE // 4)
                lo += SAMPLE
            with eng.Fori(lo // 4, hi // 4) as i:
                if st:
                    st.enter(i, lo // 4, per)
                for u in range(4):
                    body(Tile(i, u))
            if st:
                st.leave((hi - lo) // 4)
            for k in range(hi, last + 1):
                body(Tile(0, k))

        LO, HI = 12, 76
        assert SAMPLE + 3 <= LO and SAMPLE % 4 == 0
        SUMS = SAMPLE % 2

        with nc.Block() as block:

            @block.sync
            def _(sp):
                def load(t):
                    after(sp, S["x1_ready"], t.t - 3)
                    rows = TAIL if t.last else P
                    if t.last:
                        src = x_in[LAST * P:N, :]
                    else:
                        src = x_in[bass.ds(t.t * P, P), :]
                    sp.dma_start(xs[0:rows, t.slot, :], src).then_inc(loaded[t.slot], 16)

                def place(t):
                    return (TAIL, slice(LAST * P, N)) if t.last else (P, bass.ds(t.t * P, P))

                def step(t):
                    rows, dst = place(t)
                    after(sp, S["x1_ready"], t.t + 1)
                    sp.dma_start(x1_dram[dst, :], x1[0:rows, t.odd, :]).then_inc(x1_out[t.odd], 16)
                    nxt = t.plus(4)
                    if nxt.within(0, TILES):
                        load(nxt)
                    if t.plus(-1).within(0, TILES):
                        store_h2(t.plus(-1))

                def store_h2(t):
                    rows, dst = place(t)
                    sp.wait_ge(S["h2_ready"], t.t + 1)
                    sp.dma_start(h2_dram[dst, :], hs[0:rows, t.slot, :]).then_inc(h2_out[t.slot], 16)

                for k in range(4):
                    load(Tile(0, k))
                for k in range(4):
                    step(Tile(0, k))
                with sp.Fori(1, 18) as i:
                    for u in range(4):
                        step(Tile(i, u))
                for k in range(72, TILES):
                    step(Tile(0, k))
                store_h2(Tile(0, LAST))
                for s in range(4):
                    sp.wait_ge(h2_out[s], 16 * len(range(s, TILES, 4)))
                for s in range(2):
                    sp.wait_ge(x1_out[s], 16 * len(range(s, TILES, 2)))

            @block.gpsimd
            def _(pool):
                def gather(t):
                    o, j = t.po, t.half
                    after(pool, S["g_low_ready"], j - 1)
                    nc.gpsimd.tensor_copy(rowc[:, o:o + 1], edge_row[:, bass.ds(j, 1)]).then_inc(S["rows_picked"], 1)
                    wait_alone(pool, S["rows_picked"], j + 1)
                    pool.indirect_dma_start(xg[:, o, :], None, x_in[:, :],
                                            bass.IndirectOffsetOnAxis(ap=rowc[:, o:o + 1], axis=0),
                                            bounds_check=N - 1, oob_is_err=False).then_inc(gathered[o], 16)
                    pool.indirect_dma_start(dg[:, o:o + 1], None, dis_dram[:, :],
                                            bass.IndirectOffsetOnAxis(ap=rowc[:, o:o + 1], axis=0),
                                            bounds_check=NPAD - 1, oob_is_err=False).then_inc(gathered[o], 16)

                def step(k):
                    f, b = k.plus(2), k.plus(-1)
                    if f.within(0, TILES):
                        pool.wait_ge(S["x_high_ready"], f.t + 1)
                        pool.wait_ge(S["x_z_ready"], f.t + 1)
                        after(pool, S["turned"], f.t - 1)
                        nc.gpsimd.tensor_tensor(zlo[:, f.odd, :], z32[:, :], zhi[:, f.odd, :], ALU.subtract)\
                            .then_inc(S["x_low_ready"], 1)
                    e = k.plus(3)
                    if e.odd == 0 and e.within(0, TILES):
                        pool.wait_ge(S["g_high_ready"], e.half + 1)
                        pool.wait_ge(S["g_z_ready"], e.half + 1)
                        after(pool, S["turned"], e.t - 2)
                        nc.gpsimd.tensor_tensor(zglo[:, e.po, :], zg32[:, :], zghi[:, e.po, :], ALU.subtract)\
                            .then_inc(S["g_low_ready"], 1)
                        if e.plus(4).within(0, TILES):
                            gather(e.plus(4))
                    if b.within(0, TILES):
                        pool.wait_ge(S["h0_ready"], b.t + 1)
                        nc.gpsimd.tensor_tensor(hs[:, b.slot, :], hs[:, b.slot, :], lng[:, :], ALU.mult).then_inc(S["h1_ready"], 1)
                        pool.wait_ge(S["h1_ready"], b.t + 1)
                        nc.gpsimd.tensor_tensor(hs[:, b.slot, :], hs[:, b.slot, :], lnb[:, :], ALU.add).then_inc(S["h2_ready"], 1)

                gather(Tile(0, 0))
                gather(Tile(0, 2))
                steps_over(pool, step, -3, LO, 72, LAST + 1)

            @block.scalar
            def _(act):
                def root(n, ready, done, t, cnt, var_scale, eps):
                    act.wait_ge(S[ready], cnt)
                    nc.scalar.activation(std[n][:, t.slot:t.slot + 1], mv[n][:, t.slot, 1:2], ACT.Sqrt,
                                         bias=eps[:, 0:1], scale=var_scale).then_inc(S[done], 1)

                def z_of(n, t, cnt, rows, z, hi, slot, z_free, hi_free):
                    act.wait_ge(S[n + "_coef_ready"], cnt)
                    after(act, S[n + "_low_ready"], z_free)
                    c0, c1 = cf[n][:, t.slot, 0:1], cf[n][:, t.slot, 1:2]
                    nc.scalar.activation(z[:, :], rows, ACT.Identity, bias=c1, scale=c0).then_inc(S[n + "_z_ready"], 1)
                    after(act, S["turned"], hi_free)
                    nc.scalar.activation(hi[:, slot, :], rows, ACT.Identity, bias=c1, scale=c0).then_inc(S[n + "_high_ready"], 1)

                def step(k, late=False):
                    t, b, f, e = k.plus(1), k.plus(-1), k.plus(2), k.plus(3)
                    edges = e.odd == 0 and e.within(0, TILES)
                    if f.within(0, TILES):
                        root("x", "x_stats_ready", "x_std_ready", f, f.t + 1, 1.0, eps_x)
                    if edges:
                        root("g", "g_stats_ready", "g_std_ready", e, e.half + 1, 1.0, eps_x)
                    if t.within(0, TILES):
                        act.wait_ge(S["turned"], t.t + 1)
                        after(act, S["multiplied"], t.t - 1)
                        nc.scalar.activation(yhi[:, t.odd, :], zT[t.odd][:, :], ACT.Copy).then_inc(S["y_high_ready"], 1)
                    if f.within(0, TILES):
                        z_of("x", f, f.t + 1, xs[:, f.slot, :], z32, zhi, f.odd, f.t, f.t - 1)
                    if edges:
                        z_of("g", e, e.half + 1, xg[:, e.po, :], zg32, zghi, e.po, e.half, e.t - 2)
                    if b.within(0, TILES):
                        root("e", "x1_stats_ready", "x1_std_ready", b, b.t + 1, 1.0 + EPS_LN, eps_xx)
                        act.wait_ge(S["x1_coef_ready"], b.t + 1)
                        after(act, h2_out[b.slot], 16 * b.turn)
                        nc.scalar.activation(hs[:, b.slot, :], x1[:, b.odd, :], ACT.Identity, bias=cf["e"][:, b.slot, 1:2],
                                             scale=cf["e"][:, b.slot, 0:1]).then_inc(S["h0_ready"], 1)
                    t = k.plus(-2)
                    if t.within(0, TILES):
                        early = isinstance(t.i, int) and t.t < SAMPLE
                        act.wait_ge(S["h2_ready"], t.t + 1)
                        if not early:
                            after(act, S["kept"], t.t - 1)
                        v = vsam[:, t.t, :] if early else vs[:, t.odd, :]
                        nc.scalar.activation(v, hs[:, t.slot, :], ACT.Abs).then_inc(S["abs_ready"], 1)
                        if not isinstance(t.i, int) or t.t > SAMPLE:
                            act.wait_ge(S["abs_ready"], t.t + 1)
                            if late:
                                before = 2 * k.t - (2 * LO - 3)
                            elif isinstance(t.i, int) and k.t < LO:
                                before = t.t - SAMPLE
                            else:
                                before = t.t
                            count(t, v, before)

                def count(t, v, before):
                    rows = TAIL if t.last else P
                    after(act, S["layers_act_steps"], before)
                    nc.scalar.activation(junk[0:rows, :], v[0:rows, :], ACT.Sign, bias=nhigh[0:rows, 0:1],
                                         accum_out=over[0:rows, bass.ds(t.t, 1)]).then_inc(S["layers_act_steps"], 1)

                def catch_up():
                    act.wait_ge(S["bracket_ready"], 1)
                    act.wait_ge(S["abs_ready"], SAMPLE + 1)
                    count(Tile(0, SAMPLE), vs[:, SAMPLE % 2, :], 0)

                def late(k):
                    t = k.plus(-LO)
                    count(t, vsam[:, bass.ds(t.t, 1), :].rearrange("p a d -> p (a d)"), 2 * k.t - (2 * LO - 2))
                    step(k, True)

                steps_over(act, step, -3, LO, HI, LAST + 3, between=catch_up, late=late)

            @block.tensor
            def _(pe):
                def turn_over(t):
                    j = t.half
                    pe.wait_ge(S["x_high_ready"], t.t + 1)
                    pe.wait_ge(S["x_low_ready"], t.t + 1)
                    pe.wait_ge(S["g_high_ready"], j + 1)
                    pe.wait_ge(S["g_low_ready"], j + 1)
                    pe.wait_ge(S["hits_ready"], j + 1)
                    after(pe, S["y_high_ready"], t.t - 1)
                    after(pe, S["y_low_ready"], t.t - 1)
                    sel = hit[:, t.po, t.odd * P:(t.odd + 1) * P]
                    for d in range(DC):
                        o = zT[t.odd][:, d * P:(d + 1) * P]
                        dd = slice(d * P, (d + 1) * P)
                        nc.tensor.matmul(o, zhi[:, t.odd, dd], ident[:, :], start=True, stop=False)
                        nc.tensor.matmul(o, zlo[:, t.odd, dd], ident[:, :], start=False, stop=False)
                        nc.tensor.matmul(o, zghi[:, t.po, dd], sel, start=False, stop=False)
                        last = nc.tensor.matmul(o, zglo[:, t.po, dd], sel, start=False, stop=True)
                    last.then_inc(S["turned"], 1)

                def multiply(t, chunks=range(DC)):
                    if chunks[0] == 0:
                        pe.wait_ge(S["y_high_ready"], t.t + 1)
                        pe.wait_ge(S["y_low_ready"], t.t + 1)
                        after(pe, S["x1_ready"], t.t - 1)
                    for d in chunks:
                        dd = slice(d * P, (d + 1) * P)
                        for y, W in ((yhi, Whi), (yhi, Wlo), (ylo, Whi)):
                            for h in range(2):
                                hh = slice(h * 512, (h + 1) * 512)
                                last = nc.tensor.matmul(prod[t.odd][:, hh], y[:, t.odd, dd], W[:, d, hh],
                                                        start=(d == 0 and y is yhi and W is Whi),
                                                        stop=(d == DC - 1 and y is ylo))
                    if d == DC - 1:
                        last.then_inc(S["multiplied"], 1)

                def step(k):
                    t = k.plus(1)
                    if t.within(0, TILES):
                        turn_over(t)
                    if k.within(0, TILES):
                        multiply(k)

                for k in range(-1, SAMPLE + 3):
                    step(Tile(0, k))
                pe.wait_ge(S["y_low_ready"], SAMPLE + 3)
                for n in range(DC):
                    find.sum_up(pe, zT[SUMS][:, 0:2], n)
                    multiply(Tile(0, SAMPLE + 3), [n])
                for n in range(DC, SBITS):
                    find.sum_up(pe, zT[SUMS][:, 0:2], n)
                pe.wait_ge(S["bracket_ready"], 1)
                turn_over(Tile(0, SAMPLE + 4))
                for k in range(SAMPLE + 4, LO):
                    step(Tile(0, k))
                with pe.Fori(LO // 4, HI // 4) as i:
                    for u in range(4):
                        step(Tile(i, u))
                for k in range(HI, TILES):
                    step(Tile(0, k))

            @block.vector
            def _(dve):
                v = nc.vector
                st = Steps(dve, S["layers_dve_steps"])

                def stats(n, rows, slot, ready):
                    v.bn_stats(bst[n][:, 0:6], rows[:, 0:512])
                    st.link(v.bn_stats(bst[n][:, 6:12], rows[:, 512:1024]), alone=True)
                    v.bn_aggr(mv[n][:, slot, :], bst[n][:, :]).then_inc(S[ready], 1)

                def coef(n, s, weight, ready):
                    c1 = slice(s, s + 1)
                    st.link(v.reciprocal(rcp[n][:, c1], std[n][:, c1]))
                    st.link(v.tensor_tensor(cf[n][:, s, 0:1], rcp[n][:, c1], weight, ALU.mult))
                    v.scalar_tensor_tensor(out=cf[n][:, s, 1:2], in0=mv[n][:, s, 0:1], scalar=cf[n][:, s, 0:1], in1=weight,
                                           op0=ALU.mult, op1=ALU.subtract, reverse1=True).then_inc(S[ready], 1)

                def keep(t, v_in):
                    rows = TAIL if t.last else P
                    st.link(v.scalar_tensor_tensor(out=mask[0:rows, :], in0=v_in[0:rows, :], scalar=brk[0:rows, 1:2],
                                                   in1=v_in[0:rows, :], op0=ALU.is_le, op1=ALU.mult), alone=True)
                    st.link(v.max(top8[0:rows, t.slot, :], mask[0:rows, :]))
                    return v.tensor_copy(cand[0:rows, bass.ds(t.t * 8, 8)], top8[0:rows, t.slot, :])

                def step(k):
                    t, b, f, e = k.plus(1), k.plus(-1), k.plus(2), k.plus(3)
                    edges = e.odd == 0 and e.within(0, TILES)
                    if f.within(0, TILES):
                        dve.wait_ge(loaded[f.slot], 16 * f.turn + 16)
                        stats("x", xs[:, f.slot, :], f.slot, "x_stats_ready")
                    if edges:
                        dve.wait_ge(gathered[e.po], 32 * e.turn + 32)
                        stats("g", xg[:, e.po, :], e.slot, "g_stats_ready")
                        after(dve, S["turned"], e.t - 2)
                        v.tensor_scalar(hit[:, e.po, :], iota[:, :], edge_key[:, bass.ds(e.half, 1)], None, ALU.is_equal)\
                            .then_inc(S["hits_ready"], 1)
                    if b.within(0, TILES):
                        dve.wait_ge(S["multiplied"], b.t + 1)
                        after(dve, x1_out[b.odd], 16 * b.half)
                        after(dve, S["h0_ready"], b.t - 1)
                        v.scalar_tensor_tensor(out=x1[:, b.odd, :], in0=prod[b.odd][:, :], scalar=dout[:, bass.ds(b.t, 1)],
                                               in1=xs[:, b.slot, :], op0=ALU.mult, op1=ALU.add).then_inc(S["x1_ready"], 1)
                    if f.within(0, TILES):
                        dve.wait_ge(S["x_std_ready"], f.t + 1)
                        coef("x", f.slot, own8[:, bass.ds(f.t, 1)], "x_coef_ready")
                    if edges:
                        dve.wait_ge(S["g_std_ready"], e.half + 1)
                        coef("g", e.slot, dg[:, e.po:e.po + 1], "g_coef_ready")
                    if b.within(0, TILES):
                        dve.wait_ge(S["x1_ready"], b.t + 1)
                        stats("e", x1[:, b.odd, :], b.slot, "x1_stats_ready")
                    if t.within(0, TILES):
                        dve.wait_ge(S["y_high_ready"], t.t + 1)
                        after(dve, S["multiplied"], t.t - 1)
                        v.tensor_tensor(ylo[:, t.odd, :], zT[t.odd][:, :], yhi[:, t.odd, :], ALU.subtract)\
                            .then_inc(S["y_low_ready"], 1)
                    if b.within(0, TILES):
                        dve.wait_ge(S["x1_std_ready"], b.t + 1)
                        s = b.slot
                        st.link(v.reciprocal(cf["e"][:, s, 0:1], std["e"][:, s:s + 1]))
                        v.scalar_tensor_tensor(out=cf["e"][:, s, 1:2], in0=mv["e"][:, s, 0:1], scalar=-1.0,
                                               in1=cf["e"][:, s, 0:1], op0=ALU.mult, op1=ALU.mult)\
                            .then_inc(S["x1_coef_ready"], 1)
                    t = k.plus(-3)
                    if t.within(0, TILES):
                        dve.wait_ge(S["abs_ready"], t.t + 1)
                        if isinstance(t.i, int) and t.t < SAMPLE:
                            v.max(sam[:, t.t * 16:t.t * 16 + 8], vsam[:, t.t, 0:512])
                            v.max(sam[:, t.t * 16 + 8:t.t * 16 + 16], vsam[:, t.t, 512:1024]).then_inc(S["kept"], 1)
                        else:
                            keep(t, vs[:, t.odd, :]).then_inc(S["kept"], 1)

                def bracket():
                    dve.wait_ge(S["kept"], SAMPLE)
                    find.start(st)
                    st.link(v.memset(find.k[:, 0:1], SLO))
                    st.link(v.memset(find.k[:, 1:2], SHI))
                    for n in range(SBITS):
                        find.round(dve, st, zT[SUMS][:, 0:2], n, lambda cnt, thr: v.tensor_scalar(
                            mask[:, 0:SAMPLE * 16], sam[:, :], thr, None, ALU.is_ge, ALU.add, accum_out=cnt), first=(n == 0))
                    st.link(v.tensor_scalar(find.trial[:, 1:2], find.trial[:, 1:2], (1 << (31 - SBITS)) - 1, None, ALU.bitwise_or))
                    st.link(v.tensor_copy(brk[:, :], find.trial[:, :].bitcast(F32)))
                    v.tensor_scalar(nhigh[:, :], brk[:, 1:2], -1.0, None, ALU.mult).then_inc(S["bracket_ready"], 1)

                per = (2 * 4 + 2) + 4 + 2 * 4 + 2 * 2 + 2 * 4
                def late(k):
                    step(k)
                    t = k.plus(-LO)
                    st.link(keep(t, vsam[:, bass.ds(t.t, 1), :].rearrange("p a d -> p (a d)")))

                steps_over(dve, step, -3, LO, HI, LAST + 3, st=st, per=per, between=bracket, late=late, late_per=3 * 4)

    CT, CR = N // 125, 125
    with ExitStack() as c:
        ei = sb(c, "c_edges", [EP, 2, EC], I32)
        ef = sb(c, "c_edgef", [EP, 2, EC])
        own = sb(c, "c_loop", [EP, EC])
        rel = sb(c, "c_rel", [EP, 2, EC])
        hots = sb(c, "c_hots", [EP, 2, EC, CR], BF16)
        off = sb(c, "c_off", [P, 2])
        xr = sb(c, "c_x", [CR, 2, D])
        wt = sb(c, "c_w", [CR, 3])
        bst = sb(c, "c_bst", [CR, 12])
        mv = sb(c, "c_mv", [CR, 2])
        std = sb(c, "c_std", [CR, 1])
        cf = sb(c, "c_cf", [CR, 2])
        z = sb(c, "c_z", [CR, D])
        cnts = sb(c, "c_counts", [CR, CR])
        eye = sb(c, "c_eye", [P, P])
        yacc = sb(c, "c_y", [P, DC, CR])
        yh, yl = sb(c, "c_yhi", [P, DC, CR], F16), sb(c, "c_ylo", [P, DC, CR], F16)
        res = sb(c, "c_res", [CR, 2, D])
        pa = ps(c, "c_pa", [CR, CR])
        py = ps(c, "c_py", [P, DC, P])
        pp = ps(c, "c_pp", [CR, D])
        s_in, s_s, s_t, s_st, s_eye = (sem(c, "c_" + n) for n in ("edges_in", "s_in", "t_in", "stored", "eye_ready"))
        s_var, s_root, s_z, s_hot, s_a, s_as, s_y, s_ya, s_yt, s_yb, s_pp, s_res = (sem(c, "c_" + n) for n in (
            "stats_ready", "root_ready", "z_ready", "hots_ready", "counts_ready", "counts_copied", "part_ready",
            "part_added", "own_turned", "y_ready", "multiplied", "rows_ready"))
        s_dve = sem(c, "c_dve_steps")

        with nc.Block() as block:

            def crowded(eng):
                return eng.If(eng.value_load(flags[0:1, 0:1], min_val=0, max_val=1) > 0)

            @block.sync
            def _(sp):
                with crowded(sp):
                    sp.dma_start(ei[:, 0, :], src_in.rearrange("(p c) -> p c", c=EC)).then_inc(s_in, 16)
                    sp.dma_start(ei[:, 1, :], dst_in.rearrange("(p c) -> p c", c=EC)).then_inc(s_in, 16)
                    with sp.Fori(0, CT) as t:
                        sp.wait_ge(s_res, t + 1)
                        sp.dma_start(xr[:, 0, :], x_in[bass.ds(t * CR, CR), :]).then_inc(s_t, 16)
                        sp.dma_start(wt[:, 0:1], own_dram[bass.ds(t * CR, CR), :]).then_inc(s_t, 16)
                        sp.dma_start(wt[:, 1:2], dis_dram[bass.ds(t * CR, CR), :]).then_inc(s_t, 16)
                        with sp.Fori(0, CT) as s:
                            sp.wait_ge(s_z, t * (CT + 1) + s + 1)
                            sp.dma_start(xr[:, 1, :], x_in[bass.ds(s * CR, CR), :]).then_inc(s_s, 16)
                            sp.dma_start(wt[:, 2:3], dis_dram[bass.ds(s * CR, CR), :]).then_inc(s_s, 16)
                        sp.wait_ge(s_res, t + 2)
                        sp.dma_start(x1_dram[bass.ds(t * CR, CR), :], res[:, 0, :]).then_inc(s_st, 16)
                        sp.dma_start(h2_dram[bass.ds(t * CR, CR), :], res[:, 1, :]).then_inc(s_st, 16)
                        wait_alone(sp, s_st, 32 * t + 32)

            @block.gpsimd
            def _(pool):
                with crowded(pool):
                    nc.gpsimd.memset(eye[:, :], 0.0).then_inc(s_eye, 1)
                    pool.wait_ge(s_eye, 1)
                    nc.gpsimd.affine_select(out=eye[:, :], in_=eye[:, :], compare_op=ALU.not_equal, fill=1.0, base=0,
                                            pattern=[[-1, P]], channel_multiplier=1).then_inc(s_eye, 1)

            @block.scalar
            def _(act):
                with crowded(act):
                    with act.Fori(0, CT) as t:
                        with act.Fori(0, CT + 1) as s:
                            act.wait_ge(s_var, t * (CT + 2) + s + 1)
                            nc.scalar.activation(std[:, :], mv[:, 1:2], ACT.Sqrt, bias=eps_x[0:CR, 0:1]).then_inc(s_root, 1)
                        act.wait_ge(s_var, t * (CT + 2) + CT + 2)
                        nc.scalar.activation(std[:, :], mv[:, 1:2], ACT.Sqrt, bias=eps_xx[0:CR, 0:1],
                                             scale=1.0 + EPS_LN).then_inc(s_root, 1)

            @block.tensor
            def _(pe):
                with crowded(pe):
                    pe.wait_ge(s_eye, 2)
                    with pe.Fori(0, CT) as t:
                        with pe.Fori(0, CT) as s:
                            pe.wait_ge(s_hot, t * CT + s + 1)
                            for e in range(EC):
                                last = nc.tensor.matmul(pa[:, :], hots[:, 1, e, :], hots[:, 0, e, :],
                                                        start=(e == 0), stop=(e == EC - 1))
                            last.then_inc(s_a, 1)
                            pe.wait_ge(s_as, t * CT + s + 1)
                            for d in range(DC):
                                last = nc.tensor.matmul(py[:, d, 0:CR], z[:, d * P:(d + 1) * P], cnts[:, :],
                                                        start=True, stop=True)
                            last.then_inc(s_y, 1)
                        pe.wait_ge(s_z, (t + 1) * (CT + 1) + 1)
                        for d in range(DC):
                            last = nc.tensor.matmul(py[:, d, 0:CR], z[:, d * P:(d + 1) * P], eye[0:CR, 0:CR],
                                                    start=True, stop=True)
                        last.then_inc(s_yt, 1)
                        pe.wait_ge(s_yb, t + 1)
                        for d in range(DC):
                            for y, W in ((yh, Whi), (yh, Wlo), (yl, Whi)):
                                for h in range(2):
                                    hh = slice(h * 512, (h + 1) * 512)
                                    last = nc.tensor.matmul(pp[:, hh], y[:, d, :], W[:, d, hh],
                                                            start=(d == 0 and y is yh and W is Whi),
                                                            stop=(d == DC - 1 and y is yl))
                        last.then_inc(s_pp, 1)

            @block.vector
            def _(dve):
                v = nc.vector
                st = Steps(dve, s_dve)

                def stats(rows):
                    v.bn_stats(bst[:, 0:6], rows[:, 0:512])
                    st.link(v.bn_stats(bst[:, 6:12], rows[:, 512:1024]), alone=True)
                    v.bn_aggr(mv[:, :], bst[:, :]).then_inc(s_var, 1)

                def normalise(rows, weight, out_rows, n_root):
                    dve.wait_ge(s_root, n_root)
                    st.link(v.reciprocal(cf[:, 0:1], std[:, :]))
                    if weight is not None:
                        st.link(v.tensor_tensor(cf[:, 0:1], cf[:, 0:1], weight, ALU.mult))
                    st.link(v.scalar_tensor_tensor(out=cf[:, 1:2], in0=mv[:, 0:1], scalar=-1.0, in1=cf[:, 0:1],
                                                   op0=ALU.mult, op1=ALU.mult))
                    if weight is not None:
                        st.link(v.tensor_tensor(cf[:, 1:2], cf[:, 1:2], weight, ALU.add))
                    return v.tensor_scalar(out_rows, rows, cf[:, 0:1], cf[:, 1:2], ALU.mult, ALU.add)

                def hot(n):
                    st.link(v.tensor_scalar(rel[:, n, :], ef[:, n, :], off[0:EP, n:n + 1], None, ALU.subtract))
                    return v.tensor_tensor(hots[:, n, :, :], iota[0:EP, 0:CR].unsqueeze(1).broadcast_to([EP, EC, CR]),
                                           rel[:, n, :].unsqueeze(2).broadcast_to([EP, EC, CR]), ALU.is_equal)

                with crowded(dve):
                    v.engine_nop().then_inc(s_z, 1)
                    v.engine_nop().then_inc(s_res, 1)
                    dve.wait_ge(s_in, 32)
                    st.link(v.tensor_copy(ef[:, :, :], ei[:, :, :]))
                    st.link(v.tensor_tensor(own[:, :], ef[:, 0, :], ef[:, 1, :], ALU.is_equal))
                    st.link(v.scalar_tensor_tensor(out=ef[:, 0, :], in0=own[:, :], scalar=-2.0 * N, in1=ef[:, 0, :],
                                                   op0=ALU.mult, op1=ALU.add))
                    st.link(v.memset(off[:, 0:1], 0.0))
                    with dve.Fori(0, CT) as t:
                        st.enter(t, 0, 3 + CT * 8 + 16)
                        st.link(v.memset(off[:, 1:2], 0.0))
                        st.link(v.memset(yacc[:, :, :], 0.0))
                        st.link(hot(0), alone=True)
                        with dve.Fori(0, CT) as s:
                            st.enter(s, 0, 8)
                            dve.wait_ge(s_s, (t * CT + s) * 32 + 32)
                            stats(xr[:, 1, :])
                            normalise(xr[:, 1, :], wt[:, 2:3], z[:, :], t * (CT + 2) + s + 1).then_inc(s_z, 1)
                            dve.wait_ge(s_z, t * (CT + 1) + s + 2)
                            hot(1).then_inc(s_hot, 1)
                            dve.wait_ge(s_a, t * CT + s + 1)
                            v.tensor_copy(cnts[:, :], pa[:, :]).then_inc(s_as, 1)
                            dve.wait_ge(s_y, t * CT + s + 1)
                            st.link(v.tensor_tensor(yacc[:, :, :], py[:, :, 0:CR], yacc[:, :, :], ALU.add))
                            st.link(v.tensor_scalar(off[:, 1:2], off[:, 1:2], float(CR), None, ALU.add))
                        st.leave(CT)
                        dve.wait_ge(s_t, t * 48 + 48)
                        stats(xr[:, 0, :])
                        normalise(xr[:, 0, :], wt[:, 0:1], z[:, :], t * (CT + 2) + CT + 1).then_inc(s_z, 1)
                        dve.wait_ge(s_yt, t + 1)
                        st.link(v.tensor_tensor(yacc[:, :, :], py[:, :, 0:CR], yacc[:, :, :], ALU.add))
                        st.link(v.tensor_copy(yh[:, :, :], yacc[:, :, :]))
                        v.tensor_tensor(yl[:, :, :], yacc[:, :, :], yh[:, :, :], ALU.subtract).then_inc(s_yb, 1)
                        st.link(v.tensor_scalar(wt[:, 1:2], wt[:, 1:2], wsc[0:CR, 0:1], None, ALU.mult))
                        dve.wait_ge(s_pp, t + 1)
                        st.link(v.scalar_tensor_tensor(out=res[:, 0, :], in0=pp[:, :], scalar=wt[:, 1:2], in1=xr[:, 0, :],
                                                       op0=ALU.mult, op1=ALU.add))
                        stats(res[:, 0, :])
                        st.link(normalise(res[:, 0, :], None, res[:, 1, :], t * (CT + 2) + CT + 2))
                        st.link(v.tensor_tensor(res[:, 1, :], res[:, 1, :], lng[0:CR, :], ALU.mult))
                        st.link(v.tensor_scalar(off[:, 0:1], off[:, 0:1], float(CR), None, ALU.add))
                        v.tensor_tensor(res[:, 1, :], res[:, 1, :], lnb[0:CR, :], ALU.add).then_inc(s_res, 1)
                    st.leave(CT)

    with ExitStack() as c:
        part = sb(c, "part", [P, 4])
        tot = sb(c, "tot", [P, 4])
        chk = sb(c, "chk", [P, 6])
        junk = sb(c, "junk_range", [P, TILES * 8])
        find = Search(c, "range1", 1)
        psum = ps(c, "range1_sums", [P, 8])
        s_part, s_tot = sem(c, "range1_parts_ready"), sem(c, "range1_totals_ready")
        s_dve = sem(c, "range1_dve_steps")

        with nc.Block() as block:

            @block.tensor
            def _(pe):
                pe.wait_ge(s_part, 4)
                nc.tensor.matmul(psum[:, 0:4], ones[:, :], part[:, :], start=True, stop=True).then_inc(s_tot, 1)
                find.sums(pe, psum[:, 4:5])

            @block.vector
            def _(dve):
                v = nc.vector
                st = Steps(dve, s_dve)
                v.tensor_reduce(part[:, 0:1], over[:, :], AX, ALU.add).then_inc(s_part, 1)
                dve.wait_ge(s_part, 1)
                v.tensor_scalar(junk[:, :], cand[:, :], brk[:, 1:2], None, ALU.is_equal, ALU.add,
                                accum_out=part[:, 1:2]).then_inc(s_part, 1)
                dve.wait_ge(s_part, 2)
                v.tensor_scalar(junk[:, :], cand[:, :], brk[:, 0:1], None, ALU.is_ge, ALU.add,
                                accum_out=part[:, 2:3]).then_inc(s_part, 1)
                dve.wait_ge(s_part, 3)
                v.tensor_scalar(junk[:, 0:TILES], cand[:, :].rearrange("p (t k) -> p t k", k=8)[:, :, 7], brk[:, 0:1], None,
                                ALU.is_ge, ALU.add, accum_out=part[:, 3:4]).then_inc(s_part, 1)
                dve.wait_ge(s_tot, 1)
                st.link(v.tensor_copy(tot[:, :], psum[:, 0:4]))
                st.link(v.tensor_tensor(chk[:, 0:1], tot[:, 0:1], tot[:, 1:2], ALU.subtract))
                st.link(v.tensor_scalar(chk[:, 0:1], chk[:, 0:1], float(N * D), 0.5, ALU.add, ALU.mult))
                st.link(v.tensor_scalar(find.k[:, :], chk[:, 0:1], -1.0, float(RANK1), ALU.mult, ALU.add))
                st.link(v.tensor_scalar(chk[:, 1:2], find.k[:, :], 1.0, None, ALU.is_lt))
                st.link(v.tensor_tensor(chk[:, 2:3], tot[:, 2:3], find.k[:, :], ALU.is_lt))
                st.link(v.tensor_scalar(chk[:, 3:4], tot[:, 3:4], 0.0, None, ALU.is_gt))
                st.link(v.tensor_copy(chk[:, 4:5], flags[:, 0:1]))
                st.link(v.tensor_reduce(flags[:, 1:2], chk[:, 1:5], AX, ALU.max))
                st.link(v.tensor_scalar(find.k[:, :], find.k[:, :], 1.0, None, ALU.max))
                find.start(st)
                find.rounds(dve, st, psum[:, 4:5], lambda cnt, thr: v.tensor_scalar(
                    junk[:, :], cand[:, :], thr, None, ALU.is_ge, ALU.add, accum_out=cnt))
                st.link(v.tensor_copy(amax[:, 0:1], find.trial[:, 0:1].bitcast(F32)))

    with ExitStack() as c:
        hb = sb(c, "f_h2", [P, 2, D])
        junk = sb(c, "f_junk", [P, D])
        mask = sb(c, "f_mask", [P, D])
        find = Search(c, "full", 1, count_dt=F32)
        psum = ps(c, "full_sums", [P, 1])
        s_ld = [sem(c, f"full_loaded{i}") for i in range(2)]
        s_cnt, s_dve = sem(c, "full_counted_tiles"), sem(c, "full_dve_steps")

        with nc.Block() as block:

            def uncovered(eng):
                return eng.If(eng.value_load(flags[0:1, 1:2], min_val=0, max_val=1) > 0)

            @block.sync
            def _(sp):
                with uncovered(sp):
                    with sp.Fori(0, 31) as r:
                        with sp.Fori(0, LAST // 2) as i:
                            for u in range(2):
                                sp.wait_ge(s_cnt, r * TILES + i * 2 + (u + 1))
                                sp.dma_start(hb[:, u, :], h2_dram[bass.ds((i * 2 + u) * P, P), :]).then_inc(s_ld[u], 16)
                        sp.wait_ge(s_cnt, r * TILES + (LAST + 1))
                        sp.dma_start(hb[0:TAIL, 0, :], h2_dram[LAST * P:N, :]).then_inc(s_ld[0], 16)

            @block.tensor
            def _(pe):
                with uncovered(pe):
                    find.sums(pe, psum[:, :])

            @block.vector
            def _(dve):
                v = nc.vector
                st = Steps(dve, s_dve)
                with uncovered(dve):
                    find.start(st)
                    st.link(v.memset(find.k[:, :], float(RANK1)))
                    st.link(v.memset(over[:, :], 0.0), alone=True)
                    v.engine_nop().then_inc(s_cnt, 1)

                    def scan(r, first):
                        def count(u, rows, col):
                            st.link(v.scalar_tensor_tensor(out=junk[0:rows, :], in0=hb[0:rows, u, :], scalar=-1.0,
                                                           in1=hb[0:rows, u, :], op0=ALU.mult, op1=ALU.max))
                            v.tensor_scalar(mask[0:rows, :], junk[0:rows, :], find.trial[0:rows, 0:1].bitcast(F32), None,
                                            ALU.is_ge, ALU.add, accum_out=over[0:rows, col]).then_inc(s_cnt, 1)

                        with dve.Fori(0, LAST // 2) as i:
                            st.enter(i, 0, 2)
                            for u in range(2):
                                dve.wait_ge(s_ld[u], (r * (LAST // 2 + 1 - u) + i) * 16 + 16)
                                count(u, P, bass.ds(i * 2 + u, 1))
                        st.leave(LAST // 2)
                        dve.wait_ge(s_ld[0], (r * (LAST // 2 + 1) + LAST // 2) * 16 + 16)
                        count(0, TAIL, slice(LAST, TILES))
                        dve.wait_ge(s_cnt, r * TILES + (TILES + 1))
                        find.round(dve, st, psum[:, :], r, lambda cnt, thr: v.tensor_reduce(cnt, over[:, :], AX, ALU.add),
                                   first=first)

                    scan(0, True)
                    with dve.Fori(1, 31) as r:
                        st.enter(r, 1, find.steps() + LAST + 1)
                        scan(r, False)
                    st.leave(30)
                    st.link(v.tensor_copy(amax[:, 0:1], find.trial[:, 0:1].bitcast(F32)))

    lay.close()

    GC = PAIRS * P
    HALF = P // 2
    with ExitStack() as top2:
        G = sb(top2, "G", [P, GC])
        cand2 = sb(top2, "cand2", [P, PAIRS * 16])
        with ExitStack() as c:
            hb = sb(c, "h_in", [P, 4, D])
            qs = sb(c, "h_q", [P, 2, D], BF16)
            qt = sb(c, "h_qT", [P, 2, D], BF16)
            ga = sb(c, "h_abs", [P, 2, P])
            top16 = sb(c, "h_top", [P, 2, 16])
            identb = sb(c, "h_ident", [P, P], BF16)
            w1sum = sb(c, "h_w1sum", [P, H], BF16)
            w1sumf = sb(c, "h_w1sumf", [P, H])
            neg = sb(c, "h_neg", [P, P], BF16)
            pos = sb(c, "h_pos", [P, 1])
            pT = [ps(c, f"h_pT{i}", [P, D], BF16) for i in range(2)]
            pu = [ps(c, f"h_pu{i}", [P, 512]) for i in range(2)]
            ld = [sem(c, f"h_loaded{i}") for i in range(4)]
            s_id, s_kap, s_r, s_q, s_T, s_qt, s_u, s_G, s_A, s_c, s_dve = (sem(c, "h_" + n) for n in (
                "constants_ready", "scales_ready", "rounded", "q_ready", "turned", "qT_ready", "multiplied",
                "gelu_ready", "abs_ready", "kept", "dve_steps"))

            with nc.Block() as block:

                def tiles_over(eng, body, st=None, per=0):
                    for k in range(4):
                        body(Tile(0, k))
                    with eng.Fori(1, 19) as i:
                        if st:
                            st.enter(i, 1, per)
                        for u in range(4):
                            body(Tile(i, u))
                    if st:
                        st.leave(18)
                    for k in range(76, TILES):
                        body(Tile(0, k))

                @block.sync
                def _(sp):
                    def load(t):
                        after(sp, s_q, t.t - 3)
                        if t.last:
                            sp.dma_start(hb[0:TAIL, t.slot, :], h2_dram[LAST * P:N, :]).then_inc(ld[t.slot], 16)
                        else:
                            sp.dma_start(hb[:, t.slot, :], h2_dram[bass.ds(t.t * P, P), :]).then_inc(ld[t.slot], 16)

                    tiles_over(sp, load)

                @block.gpsimd
                def _(pool):
                    nc.gpsimd.memset(identb[:, :], 0.0).then_inc(s_id, 1)
                    nc.gpsimd.memset(cand2[:, :], 0.0).then_inc(s_id, 1)
                    nc.gpsimd.memset(G[:, GC - P:GC], 0.0).then_inc(s_id, 1)
                    nc.gpsimd.memset(neg[:, :], -128.0).then_inc(s_id, 1)
                    nc.gpsimd.memset(pos[:, :], 128.0).then_inc(s_id, 1)
                    pool.wait_ge(s_id, 5)
                    nc.gpsimd.affine_select(out=identb[:, :], in_=identb[:, :], compare_op=ALU.not_equal, fill=1.0, base=0,
                                            pattern=[[-1, P]], channel_multiplier=1).then_inc(s_id, 1)

                @block.tensor
                def _(pe):
                    def turn(t):
                        pe.wait_ge(s_q, t.t + 1)
                        after(pe, s_qt, t.t - 1)
                        for d in range(DC):
                            last = nc.tensor.matmul(pT[t.odd][:, d * P:(d + 1) * P], qs[:, t.odd, d * P:(d + 1) * P],
                                                    identb[:, :], start=True, stop=True, is_transpose=True)
                        last.then_inc(s_T, 1)

                    def hidden(t):
                        pe.wait_ge(s_qt, t.t + 1)
                        after(pe, s_G, t.half - 1)
                        rows = slice(t.odd * H, (t.odd + 1) * H)
                        nc.tensor.matmul(pu[t.po][rows, 0:P], w1sum[:, :], neg[:, :], start=True, stop=False)
                        for d in range(DC):
                            last = nc.tensor.matmul(pu[t.po][rows, 0:P], w1T[:, d, :], qt[:, t.odd, d * P:(d + 1) * P],
                                                    start=False, stop=(d == DC - 1))
                        last.then_inc(s_u, 1)

                    def both(t):
                        if t.plus(1).within(0, TILES):
                            turn(t.plus(1))
                        hidden(t)

                    pe.wait_ge(s_id, 6)
                    pe.wait_ge(s_kap, 1)
                    turn(Tile(0, 0))
                    tiles_over(pe, both)

                @block.scalar
                def _(act):
                    def gelu(t):
                        rows, n = (H, TAIL) if t.last else (P, P)
                        wait_alone(act, s_u, 2 * t.half + (1 if t.last else 2))
                        g = G[0:rows, bass.ds(t.half * P, n)]
                        nc.scalar.activation(g, pu[t.po][0:rows, 0:n], ACT.Gelu, scale=kap[0:rows, 1:2]).then_inc(s_G, 1)
                        after(act, s_c, t.half - 1)
                        wait_alone(act, s_G, t.half + 1)
                        nc.scalar.activation(ga[0:rows, t.po, 0:n], g, ACT.Abs).then_inc(s_A, 1)

                    def step(t):
                        act.wait_ge(s_T, t.t + 1)
                        after(act, s_u, t.t - 1)
                        nc.scalar.activation(qt[:, t.odd, :], pT[t.odd][:, :], ACT.Relu, bias=pos[:, 0:1]).then_inc(s_qt, 1)
                        if t.odd and t.plus(-2).within(0, TILES):
                            gelu(t.plus(-2))

                    act.wait_ge(s_id, 6)
                    act.wait_ge(s_kap, 1)
                    tiles_over(act, step)
                    gelu(Tile(0, 77))
                    gelu(Tile(0, 78))

                @block.vector
                def _(dve):
                    v = nc.vector
                    st = Steps(dve, s_dve)
                    st.link(v.tensor_scalar(kap[:, 2:3], amax[:, 0:1], EPS_Q, None, ALU.max))
                    st.link(v.reciprocal(kap[:, 3:4], kap[:, 2:3]))
                    st.link(v.tensor_scalar(kap[:, 0:1], kap[:, 3:4], QMAX, None, ALU.mult))
                    st.link(v.reciprocal(kap[:, 3:4], kap[:, 0:1]))
                    st.link(v.tensor_tensor(kap[:, 1:2], kap[:, 3:4], gam[:, 0:1], ALU.mult))
                    st.link(v.tensor_reduce(w1sumf[:, :], w1T[:, :, :].rearrange("p k h -> p h k"), AX, ALU.add))
                    v.tensor_copy(w1sum[:, :], w1sumf[:, :]).then_inc(s_kap, 1)
                    dve.wait_ge(s_id, 6)

                    def rounded(t):
                        dve.wait_ge(ld[t.slot], 16 * t.turn + 16)
                        v.tensor_scalar(hb[:, t.slot, :], hb[:, t.slot, :], kap[:, 0:1], MAGIC, ALU.mult, ALU.add)\
                            .then_inc(s_r, 1)

                    def bounded(t):
                        dve.wait_ge(s_r, t.t + 1)
                        after(dve, s_T, t.t - 1)
                        v.tensor_scalar(qs[:, t.odd, :], hb[:, t.slot, :], -MAGIC, QMAX, ALU.add, ALU.min).then_inc(s_q, 1)

                    def largest(t):
                        rows = H if t.last else P
                        wait_alone(dve, s_A, t.half + 1)
                        if t.last:
                            st.link(v.max(top16[0:rows, t.po, 0:8], ga[0:rows, t.po, 0:TAIL]))
                        else:
                            v.max(top16[:, t.po, 0:8], ga[:, t.po, 0:HALF])
                            st.link(v.max(top16[:, t.po, 8:16], ga[:, t.po, HALF:P]), alone=True)
                        n = 8 if t.last else 16
                        v.tensor_copy(cand2[0:rows, bass.ds(t.half * 16, n)], top16[0:rows, t.po, 0:n]).then_inc(s_c, 1)

                    def step(t):
                        if t.plus(1).within(0, TILES):
                            rounded(t.plus(1))
                        bounded(t)
                        if t.odd and t.plus(-4).within(0, TILES):
                            largest(t.plus(-4))

                    rounded(Tile(0, 0))
                    tiles_over(dve, step, st, 2)
                    for k in (75, 77, 78):
                        largest(Tile(0, k))

        RES = 32
        xres = sb(top2, "x1_resident", [P, RES, D])
        with ExitStack() as c:
            junk = sb(c, "r2_junk", [P, PAIRS * 16], BF16)
            chk = sb(c, "r2_chk", [P, 2])
            find = Search(c, "range2", 1)
            psum = ps(c, "range2_sums", [P, 2])
            s_res, s_chk, s_tot, s_dve = (sem(c, "range2_" + n) for n in ("x1_loaded", "full_chunks", "full_total", "dve_steps"))

            with nc.Block() as block:

                @block.sync
                def _(sp):
                    for k in range(RES):
                        sp.dma_start(xres[:, k, :], x1_dram[k * P:(k + 1) * P, :]).then_inc(s_res, 16)
                    sp.wait_ge(s_res, 16 * RES)

                @block.tensor
                def _(pe):
                    find.sums(pe, psum[:, 0:1])
                    pe.wait_ge(s_chk, 1)
                    nc.tensor.matmul(psum[:, 1:2], ones[:, :], chk[:, 0:1], start=True, stop=True).then_inc(s_tot, 1)

                @block.vector
                def _(dve):
                    v = nc.vector
                    st = Steps(dve, s_dve)
                    find.start(st)
                    st.link(v.memset(find.k[:, :], float(RANK2)))
                    find.rounds(dve, st, psum[:, 0:1], lambda cnt, thr: v.tensor_scalar(
                        junk[:, :], cand2[:, :], thr, None, ALU.is_ge, ALU.add, accum_out=cnt))
                    st.link(v.tensor_copy(amax[:, 1:2], find.trial[:, 0:1].bitcast(F32)))
                    v.tensor_scalar(junk[:, 0:2 * PAIRS], cand2[:, :].rearrange("p (t k) -> p t k", k=8)[:, :, 7], amax[:, 1:2],
                                    None, ALU.is_ge, ALU.add, accum_out=chk[:, 0:1]).then_inc(s_chk, 1)
                    dve.wait_ge(s_tot, 1)
                    st.link(v.tensor_scalar(flags[:, 2:3], psum[:, 1:2], 0.0, None, ALU.is_gt))

        with ExitStack() as c:
            junk = sb(c, "g_junk", [P, D])
            hits = sb(c, "g_hits", [P, D], BF16)
            part = sb(c, "g_parts", [P, GC // D])
            find = Search(c, "fullg", 1, count_dt=F32)
            psum = ps(c, "fullg_sums", [P, 1])
            s_dve = sem(c, "fullg_dve_steps")

            with nc.Block() as block:

                def uncovered2(eng):
                    return eng.If(eng.value_load(flags[0:1, 2:3], min_val=0, max_val=1) > 0)

                @block.tensor
                def _(pe):
                    with uncovered2(pe):
                        find.sums(pe, psum[:, 0:1])

                @block.vector
                def _(dve):
                    v = nc.vector
                    st = Steps(dve, s_dve)
                    with uncovered2(dve):
                        find.start(st)
                        st.link(v.memset(find.k[:, :], float(RANK2)))

                        def scan(n, first):
                            for k in range(GC // D):
                                g = G[:, k * D:(k + 1) * D]
                                st.link(v.scalar_tensor_tensor(out=junk[:, :], in0=g, scalar=-1.0, in1=g,
                                                               op0=ALU.mult, op1=ALU.max))
                                st.link(v.tensor_scalar(hits[:, :], junk[:, :], find.trial[:, 0:1].bitcast(F32), None,
                                                        ALU.is_ge, ALU.add, accum_out=part[:, k:k + 1]))
                            find.round(dve, st, psum[:, :], n, lambda cnt, thr: v.tensor_reduce(cnt, part[:, :], AX, ALU.add),
                                       first=first)

                        scan(0, True)
                        with dve.Fori(1, 31) as n:
                            st.enter(n, 1, find.steps() + 2 * (GC // D))
                            scan(n, False)
                        st.leave(30)
                        st.link(v.tensor_copy(amax[:, 1:2], find.trial[:, 0:1].bitcast(F32)))

        with ExitStack() as c:
            xb = sb(c, "o_x1", [P, 2, D])
            ob = sb(c, "o_out", [P, 4, D])
            qf = sb(c, "o_qf", [P, P])
            q2 = sb(c, "o_q", [P, 2, P], BF16)
            po = [ps(c, f"o_po{i}", [P, D]) for i in range(4)]
            ld = [sem(c, f"o_loaded{i}") for i in range(2)]
            MIXED = RES // 2
            TURNS = -(-TILES // 4)
            ldt = [sem(c, f"o_tail_loaded{i}") for i in range(2 * (TURNS - MIXED))]
            sd = [sem(c, f"o_stored{i}") for i in range(4)]
            s_q, s_m, s_o, s_dve = (sem(c, "o_" + n) for n in ("q_ready", "multiplied", "out_ready", "dve_steps"))

            def tail(j):
                return isinstance(j, int) and j >= MIXED

            def pair_of(j, h):
                return 2 * j + h if tail(j) else j + MIXED * h

            def tile_of(j, u):
                return pair_of(j, u // 2) * 2 + u % 2

            def rows_of(j, u):
                t = tile_of(j, u)
                return (TAIL, slice(LAST * P, N)) if isinstance(t, int) and t == LAST else (P, bass.ds(t * P, P))

            def turns_over(eng, body, st=None, per=0):
                for u in range(4):
                    body(0, u)
                with eng.Fori(1, MIXED - 1) as j:
                    if st:
                        st.enter(j, 1, per)
                    for u in range(4):
                        body(j, u)
                if st:
                    st.leave(MIXED - 2)
                for n in range(4 * (MIXED - 1), TILES):
                    body(n // 4, n % 4)

            with nc.Block() as block:

                @block.sync
                def _(sp):
                    def load(j, u):
                        rows, src = rows_of(j, u)
                        if tail(j):
                            n = 4 * (j - MIXED) + u
                            if n == 0:
                                sp.wait_ge(s_o, RES)
                            sp.dma_start(xres[0:rows, n, :], x1_dram[src, :]).then_inc(ldt[n // 2], 16)
                        elif u >= 2:
                            after(sp, s_o, 4 * j + u - 3)
                            sp.dma_start(xb[:, u - 2, :], x1_dram[src, :]).then_inc(ld[u - 2], 16)

                    turns_over(sp, load)

                @block.scalar
                def _(act):
                    def store(j, u):
                        act.wait_ge(s_o, 4 * j + u + 1)
                        rows, dst = rows_of(j, u)
                        act.dma_start(out[dst, :], ob[0:rows, u, :]).then_inc(sd[u], 16)

                    turns_over(act, store)
                    for s in range(4):
                        act.wait_ge(sd[s], 16 * len(range(s, TILES, 4)))

                @block.tensor
                def _(pe):
                    def step(j, u):
                        h = u // 2
                        pe.wait_ge(s_q, 2 * j + h + 1)
                        after(pe, s_o, 4 * j + u - 3)
                        rows = slice((u % 2) * H, (u % 2 + 1) * H)
                        for n in range(2):
                            last = nc.tensor.matmul(po[u][:, n * 512:(n + 1) * 512], q2[rows, h, :],
                                                    w2T[rows, n * 512:(n + 1) * 512], start=True, stop=True)
                        last.then_inc(s_m, 1)

                    turns_over(pe, step)

                @block.vector
                def _(dve):
                    v = nc.vector
                    st = Steps(dve, s_dve)
                    st.link(v.tensor_scalar(kap[:, 2:3], amax[:, 1:2], EPS_Q, None, ALU.max))
                    st.link(v.reciprocal(kap[:, 3:4], kap[:, 2:3]))
                    st.link(v.tensor_scalar(kap[:, 4:5], kap[:, 3:4], QMAX, None, ALU.mult))
                    st.link(v.reciprocal(kap[:, 3:4], kap[:, 4:5]))
                    st.link(v.tensor_tensor(kap[:, 5:6], kap[:, 3:4], gam[:, 1:2], ALU.mult))

                    def quantise(j, h):
                        pair = pair_of(j, h)
                        last = isinstance(pair, int) and pair == PAIRS - 1
                        rows, n = (H, TAIL) if last else (P, P)
                        after(dve, s_q, 2 * j + h)
                        st.link(v.tensor_scalar(qf[0:rows, 0:n], G[0:rows, bass.ds(pair * P, n)], kap[0:rows, 4:5], MAGIC,
                                                ALU.mult, ALU.add))
                        st.link(v.tensor_scalar(qf[0:rows, 0:n], qf[0:rows, 0:n], MAGIC - 128.0, MAGIC + 127.0, ALU.max, ALU.min))
                        after(dve, s_m, 4 * j + 2 * h - 2)
                        v.tensor_scalar(q2[0:rows, h, 0:n], qf[0:rows, 0:n], -MAGIC, None, ALU.add).then_inc(s_q, 1)

                    def step(j, u):
                        if u == 0 and not (isinstance(j, int) and 2 * j + 1 >= PAIRS):
                            quantise(j, 1)
                        if u == 2 and not (isinstance(j, int) and 2 * j + 2 >= PAIRS):
                            quantise(j + 1, 0)
                        dve.wait_ge(s_m, 4 * j + u + 1)
                        if tail(j):
                            n = 4 * (j - MIXED) + u
                            both = 2 if tile_of(j, u) // 2 * 2 + 1 < TILES else 1
                            dve.wait_ge(ldt[n // 2], 16 * both)
                            x = xres[:, n, :]
                        elif u >= 2:
                            dve.wait_ge(ld[u - 2], 16 * j + 16)
                            x = xb[:, u - 2, :]
                        else:
                            x = xres[:, bass.ds(2 * j + u, 1), :].rearrange("p a d -> p (a d)")
                        after(dve, sd[u], 16 * j)
                        v.scalar_tensor_tensor(out=ob[:, u, :], in0=po[u][:, :], scalar=kap[:, 5:6],
                                               in1=x, op0=ALU.mult, op1=ALU.add).then_inc(s_o, 1)

                    quantise(0, 0)
                    turns_over(dve, step, st, 4)


    top.close()


def kernel(x, src, dst, L0_gnn_W, L0_gnn_b, L0_ffn_ln_g, L0_ffn_ln_b, L0_ffn_w1, L0_ffn_w2):
    import concourse.bacc as bacc
    import numpy as np
    from concourse.bass_utils import run_bass_kernel_spmd

    nc = bacc.Bacc("TRN2", target_bir_lowering=False, num_devices=1)
    given = {"x": x, "src": src, "dst": dst, "W": L0_gnn_W, "b": L0_gnn_b, "ln_g": L0_ffn_ln_g, "ln_b": L0_ffn_ln_b,
             "w1": L0_ffn_w1, "w2": L0_ffn_w2}
    arrays = {"in_" + k: np.ascontiguousarray(a) for k, a in given.items()}
    ins = [nc.dram_tensor(k, a.shape, mybir.dt.from_np(a.dtype), kind="ExternalInput").ap() for k, a in arrays.items()]
    out = nc.dram_tensor("out_rows", (N, D), F32, kind="ExternalOutput").ap()
    build(nc, *ins, out)
    return run_bass_kernel_spmd(nc, [arrays], core_ids=[0]).results[0]["out_rows"]
```

```python
from contextlib import ExitStack

import concourse.bass as bass
from concourse import mybir
from concourse.alu_op_type import AluOpType as ALU

F32, F16, BF16, I32 = mybir.dt.float32, mybir.dt.float16, mybir.dt.bfloat16, mybir.dt.int32
ACT = mybir.ActivationFunctionType
AX = mybir.AxisListType.X
RMAX = bass.bass_isa.ReduceOp.max

P = 128
N, D, H, E = 10000, 1024, 64, 12500
DC = D // P
TILES = -(-N // P)
LAST = TILES - 1
TAIL = N - LAST * P
PAIRS = -(-TILES // 2)
GROUP = 2 * P
EP, EC = 125, 100
assert EP * EC == E
EPS_LN = 1e-5
EPS_Q = 1e-5
QMAX = 127.0
MAGIC = 1.5 * 2.0 ** 23
ZS = 0.125
SAMPLE = 4
RANK1 = N * D - 10188799
RANK2 = N * H - 636799
SRANK = RANK1 * SAMPLE * P / N
SLO, SHI = float(round(SRANK * 1.08)), float(round(SRANK * 0.92))
SBITS = 16
NPAD = TILES * P
GC = PAIRS * P


class Tile:

    def __init__(self, i, c, m=4):
        self.i, self.c, self.m = i, c, m
        self.slot, self.odd = c % 4, c % 2
        self.po = (c // 2) % 2
        self.last = isinstance(i, int) and m * i + c == LAST

    @property
    def t(self):
        return self.m * self.i + self.c

    @property
    def turn(self):
        return self.m // 4 * self.i + self.c // 4

    @property
    def half(self):
        return self.m // 2 * self.i + self.c // 2

    def plus(self, n):
        return Tile(self.i, self.c + n, self.m)

    def within(self, lo, hi):
        return not isinstance(self.i, int) or lo <= self.t < hi


def after(eng, sem, n):
    if not isinstance(n, int) or n > 0:
        eng.wait_ge(sem, n)


def wait_alone(eng, sem, n):
    eng.wait_ge(sem, n)
    if not isinstance(n, int):
        eng.nop(nofuse=True)


class Steps:

    def __init__(self, eng, sem):
        self.eng, self.sem, self.base, self.n, self.outer = eng, sem, 0, 0, []

    def link(self, ins, alone=False):
        self.n += 1
        ins.then_inc(self.sem, 1)
        if alone:
            wait_alone(self.eng, self.sem, self.base + self.n)
        else:
            self.eng.wait_ge(self.sem, self.base + self.n)

    def enter(self, i, first, per):
        self.outer.append((self.base, self.n, per))
        self.base, self.n = self.base + self.n - first * per + per * i, 0

    def leave(self, turns):
        base, n, per = self.outer.pop()
        assert self.n == per, (self.n, per)
        self.base, self.n = base, n + turns * per


def build(nc, x_in, src_in, dst_in, w_in, b_in, lng_in, lnb_in, w1_in, w2_in, out):
    top = ExitStack()

    def dram(name, shape, dt=F32):
        return nc.dram_tensor(name, shape, dt, kind="Internal").ap()

    x1_dram, h2_dram = dram("x1_rows", (N, D)), dram("h2_rows", (N, D))
    dis_dram = dram("dis_table", (NPAD, 1))
    own_dram = dram("own_table", (NPAD, 1))

    def sb(ctx, name, shape, dt=F32):
        return ctx.enter_context(nc.sbuf_tensor(name, shape, dt))

    def ps(ctx, name, shape, dt=F32):
        return ctx.enter_context(nc.psum_tensor(name, shape, dt))

    def sem(ctx, name):
        return ctx.enter_context(nc.semaphore(name))

    iota = sb(top, "iota", [P, GROUP])
    ones = sb(top, "ones", [P, P])
    ones16 = sb(top, "ones16", [P, P], F16)
    dis8 = sb(top, "dis8", [P, TILES])
    own8 = sb(top, "own8", [P, TILES])
    dout = sb(top, "dout", [P, TILES])
    edge_row = sb(top, "edge_row", [P, PAIRS], I32)
    edge_key = sb(top, "edge_key", [P, PAIRS])
    w1T = sb(top, "w1T", [P, DC, H], BF16)
    w2T = sb(top, "w2T", [P, D], BF16)
    gam = sb(top, "gam", [P, 2])
    flags = sb(top, "flags", [P, 3], I32)
    eps_x = sb(top, "eps_x", [P, 1])
    eps_xx = sb(top, "eps_xx", [P, 1])
    amax = sb(top, "amax", [P, 2])
    wsc = sb(top, "wsc", [P, 1])
    kap = sb(top, "kap", [P, 8])

    G = sb(top, "G", [P, GC])
    cand2 = sb(top, "cand2", [P, PAIRS * 16])

    lay = ExitStack()
    Whi = sb(lay, "Whi", [P, DC, D], F16)
    Wlo = sb(lay, "Wlo", [P, DC, D], F16)
    ident = sb(lay, "ident", [P, P], F16)
    lng = sb(lay, "lng", [P, D])
    lnb = sb(lay, "lnb", [P, D])
    cand = sb(lay, "cand", [P, TILES * 8])
    over = sb(lay, "over", [P, TILES])
    brk = sb(lay, "brk", [P, 2])
    nhigh = sb(lay, "nhigh", [P, 1])

    with ExitStack() as c:
        ei = sb(c, "ei", [EP, 2, EC], I32)
        parts = sb(c, "parts", [EP, 6, EC], I32)
        fl = sb(c, "fl", [EP, 6, EC])
        loop = sb(c, "loop", [EP, EC])
        nonloop = sb(c, "nonloop", [EP, EC])
        group = sb(c, "group", [EP, EC])
        rank = sb(c, "rank", [EP, EC])
        hot_lo = sb(c, "hot_lo", [EP, EC, P], BF16)
        room = sb(c, "room", [EP, EC * 2 * TILES], BF16)
        hot_hi = room[:, :].rearrange("p (c a t) -> p c a t", a=2, t=TILES)
        vals = room[:, 0:EC * 3 * PAIRS].rearrange("p (c a t) -> p c a t", a=3, t=PAIRS)
        hot_g = sb(c, "hot_g", [EP, PAIRS, EC], BF16)
        run = sb(c, "run", [EP, PAIRS, EC])
        ends = sb(c, "ends", [EP, 2, PAIRS])
        upper = sb(c, "upper", [EP, EP])
        base = sb(c, "base", [EP, PAIRS])
        small = sb(c, "small", [P, 16])
        smalli = sb(c, "smalli", [P, 4], I32)
        degs = sb(c, "degs", [P, 4, TILES])
        tab = sb(c, "tab", [P, 3, PAIRS])
        wn = sb(c, "wn", [P, DC, D])
        bn = sb(c, "bn", [P, DC])
        wsum = sb(c, "wsum", [P, DC])
        wabs = sb(c, "wabs", [P, 2, DC])
        identf = sb(c, "identf", [P, P])
        identb = sb(c, "identb", [P, P], BF16)
        w1n = sb(c, "w1n", [H, D])
        w1q = sb(c, "w1q", [H, D], BF16)
        w2n = sb(c, "w2n", [P, DC, H])
        w2q = sb(c, "w2q", [P, DC, 2, H], BF16)
        junk = sb(c, "junk_prep", [P, D], BF16)
        pw = [ps(c, f"pw{i}", [P, D]) for i in range(2)]
        pdeg = ps(c, "pdeg", [P, 2 * TILES])
        ptab = ps(c, "ptab", [P, 3 * PAIRS])
        pcnt = ps(c, "pcnt", [P, 96])
        pt = ps(c, "pt", [P, D], BF16)

        s_edges, s_w, s_small, s_tab = (sem(c, n) for n in ("edges_in", "w_in", "weights_in", "tables_out"))
        s_const = sem(c, "constants_ready")
        s_hot, s_hh, s_deg = sem(c, "degree_low_hots_ready"), sem(c, "degree_high_hots_ready"), sem(c, "degrees_counted")
        s_std, s_inv = sem(c, "degree_roots_ready"), sem(c, "degree_tables_ready")
        s_tot, s_off = sem(c, "group_counts_ready"), sem(c, "group_offsets_ready")
        s_val, s_slots = sem(c, "table_hots_ready"), sem(c, "table_filled")
        s_rs, s_sh, s_wp = sem(c, "w_row_sums_ready"), sem(c, "w_shifts_ready"), sem(c, "w_shifted")
        s_mx, s_armx = sem(c, "w_row_max_ready"), sem(c, "w_max_ready")
        s_sc = sem(c, "w_scale_ready")
        s_wt, s_whi, s_wlo = sem(c, "w_turned"), sem(c, "w_high_ready"), sem(c, "w_low_ready")
        s_abs, s_gs, s_tq, s_tt = (sem(c, n) for n in ("ffn_abs_sums", "ffn_sums_ready", "ternary_ready", "ternary_turned"))
        s_tc = sem(c, "ternary_copied")
        s_parts, s_grp, s_rank = sem(c, "node_parts_ready"), sem(c, "group_hots_ready"), sem(c, "ranks_ready")
        s_dve = sem(c, "prepare_dve_steps")
        s_pool = sem(c, "prepare_pool_steps")

        with nc.Block() as block:

            @block.sync
            def _(sp):
                sp.dma_start(ei[:, 0, :], src_in.rearrange("(p c) -> p c", c=EC)).then_inc(s_edges, 16)
                sp.dma_start(ei[:, 1, :], dst_in.rearrange("(p c) -> p c", c=EC)).then_inc(s_edges, 16)
                sp.dma_start(wn[:, :, :], w_in.rearrange("(k p) d -> p k d", p=P)).then_inc(s_w, 16)
                sp.dma_start(bn[:, :], b_in.rearrange("(k p) -> p k", p=P),
                             allow_slow_non_contiguous=True).then_inc(s_w, 16)
                sp.dma_start(w1n[:, :], w1_in).then_inc(s_small, 16)
                sp.dma_start(w2n[:, :, :], w2_in.rearrange("(k p) h -> p k h", p=P)).then_inc(s_small, 16)
                sp.dma_start(lng[:, :], lng_in.partition_broadcast(P)).then_inc(s_small, 16)
                sp.dma_start(lnb[:, :], lnb_in.partition_broadcast(P)).then_inc(s_small, 16)
                sp.wait_ge(s_inv, 2)
                sp.dma_start(dis_dram.rearrange("(t p) a -> p (t a)", p=P), dis8[:, :],
                             allow_slow_non_contiguous=True).then_inc(s_tab, 16)
                sp.dma_start(own_dram.rearrange("(t p) a -> p (t a)", p=P), own8[:, :],
                             allow_slow_non_contiguous=True).then_inc(s_tab, 16)
                sp.wait_ge(s_tab, 32)
                sp.wait_ge(s_small, 64)

            @block.gpsimd
            def _(pool):
                nc.gpsimd.memset(flags[:, :], 0).then_inc(s_const, 1)
                nc.gpsimd.iota(iota[:, :], [[1, GROUP]], base=0, channel_multiplier=0,
                               allow_small_or_imprecise_dtypes=True).then_inc(s_const, 1)
                nc.gpsimd.memset(ones[:, :], 1.0).then_inc(s_const, 1)
                nc.gpsimd.memset(ones16[:, :], 1.0).then_inc(s_const, 1)
                nc.gpsimd.memset(ident[:, :], 0.0).then_inc(s_pool, 1)
                nc.gpsimd.memset(identf[:, :], 0.0).then_inc(s_pool, 1)
                nc.gpsimd.memset(identb[:, :], 0.0).then_inc(s_pool, 1)
                nc.gpsimd.memset(upper[:, :], 1.0).then_inc(s_pool, 1)
                pool.wait_ge(s_pool, 4)
                for m in (ident, identf, identb):
                    nc.gpsimd.affine_select(out=m[:, :], in_=m[:, :], compare_op=ALU.not_equal, fill=1.0, base=0,
                                            pattern=[[-1, P]], channel_multiplier=1).then_inc(s_const, 1)
                nc.gpsimd.affine_select(out=upper[:, :], in_=upper[:, :], compare_op=ALU.is_gt, fill=0.0, base=0,
                                        pattern=[[1, EP]], channel_multiplier=-1).then_inc(s_const, 1)
                nc.gpsimd.memset(eps_x[:, :], EPS_LN).then_inc(s_const, 1)
                nc.gpsimd.memset(eps_xx[:, :], EPS_LN * EPS_LN).then_inc(s_const, 1)
                nc.gpsimd.memset(cand[:, :], 0.0).then_inc(s_const, 1)
                nc.gpsimd.memset(over[:, :], 0.0).then_inc(s_const, 1)
                pool.wait_ge(s_hh, 1)
                pool.wait_ge(s_parts, 2)
                nc.gpsimd.tensor_tensor(hot_hi[:, :, 1, :], hot_hi[:, :, 0, :],
                                        loop[:, :].unsqueeze(2).broadcast_to([EP, EC, TILES]), ALU.mult).then_inc(s_hh, 1)
                pool.wait_ge(s_mx, 1)
                nc.gpsimd.partition_all_reduce(small[:, 1:2], small[:, 0:1], P, RMAX).then_inc(s_armx, 1)
                pool.wait_ge(s_deg, 1)
                hgc = hot_g[:, :, :].rearrange("p t c -> p c t")
                pool.wait_ge(s_grp, 1)
                for n, m in ((0, 4), (1, 5)):
                    nc.gpsimd.tensor_tensor(vals[:, :, n, :], hgc, fl[:, m, :].unsqueeze(2).broadcast_to([EP, EC, PAIRS]),
                                            ALU.mult).then_inc(s_val, 1)

            @block.scalar
            def _(act):
                act.wait_ge(s_w, 32)
                for k in range(DC):
                    if k:
                        act.wait_ge(s_rs, k)
                    nc.scalar.activation(junk[:, :], wn[:, k, :], ACT.Copy, accum_out=wsum[:, k:k + 1]).then_inc(s_rs, 1)
                for k in range(DC):
                    act.wait_ge(s_rs, DC + k)
                    nc.scalar.activation(junk[:, :], wn[:, k, :], ACT.Abs, accum_out=wabs[:, 0, k:k + 1]).then_inc(s_rs, 1)
                act.wait_ge(s_rs, 2 * DC)
                act.wait_ge(s_sh, 1)
                for k in range(DC):
                    nc.scalar.activation(wn[:, k, :], wn[:, k, :], ACT.Identity, bias=wsum[:, k:k + 1]).then_inc(s_wp, 1)
                act.wait_ge(s_small, 64)
                nc.scalar.activation(junk[0:H, :], w1n[:, :], ACT.Abs, accum_out=small[0:H, 4:5]).then_inc(s_abs, 1)
                act.wait_ge(s_abs, 1)
                nc.scalar.activation(junk[:, 0:DC * H], w2n[:, :, :].rearrange("p k h -> p (k h)"), ACT.Abs,
                                     accum_out=small[:, 5:6]).then_inc(s_abs, 1)
                act.wait_ge(s_deg, 1)
                act.wait_ge(s_const, 12)
                nc.scalar.activation(degs[:, 0, :], pdeg[:, 0:TILES], ACT.Sqrt, bias=ones[:, 0:1]).then_inc(s_std, 1)
                act.wait_ge(s_sc, 1)
                for d in range(DC):
                    act.wait_ge(s_wt, d + 1)
                    nc.scalar.activation(Whi[:, d, :], pw[d % 2][:, :], ACT.Copy, scale=small[:, 2:3]).then_inc(s_whi, 1)
                act.wait_ge(s_tt, 1)
                nc.scalar.activation(w1T[:, :, :].rearrange("p k h -> p (k h)"), pt[:, 0:DC * H], ACT.Copy).then_inc(s_tc, 1)
                act.wait_ge(s_tt, 2)
                nc.scalar.activation(w2T[:, :], pt[:, :], ACT.Copy).then_inc(s_tc, 1)

            @block.tensor
            def _(pe):
                def fill_table():
                    pe.wait_ge(s_val, 4)
                    for e in range(EC):
                        last = nc.tensor.matmul(ptab[:, :], hot_lo[:, e, :], vals[:, e, :, :].rearrange("p a t -> p (a t)"),
                                                start=(e == 0), stop=(e == EC - 1))
                    last.then_inc(s_slots, 1)

                pe.wait_ge(s_const, 12)
                pe.wait_ge(s_tot, 1)
                nc.tensor.matmul(pcnt[0:EP, 0:PAIRS], upper[:, :], ends[:, 1, :], start=True, stop=True)
                nc.tensor.matmul(pcnt[:, 48:48 + PAIRS], ones[0:EP, :], ends[:, 1, :],
                                 start=True, stop=True).then_inc(s_off, 1)
                pe.wait_ge(s_hot, 1)
                pe.wait_ge(s_hh, 2)
                for e in range(EC):
                    last = nc.tensor.matmul(pdeg[:, :], hot_lo[:, e, :], hot_hi[:, e, :, :].rearrange("p a t -> p (a t)"),
                                            start=(e == 0), stop=(e == EC - 1))
                last.then_inc(s_deg, 1)
                pe.wait_ge(s_abs, 2)
                pe.wait_ge(s_rank, 2)
                nc.tensor.matmul(pcnt[:, 90:91], ones[0:H, :], small[0:H, 4:5], start=True, stop=True)
                nc.tensor.matmul(pcnt[:, 91:92], ones[:, :], small[:, 5:6], start=True, stop=True).then_inc(s_gs, 1)
                pe.wait_ge(s_wp, DC)
                for d in range(DC):
                    if d == 2:
                        fill_table()
                    if d >= 2:
                        pe.wait_ge(s_whi, d - 1)
                        pe.wait_ge(s_wlo, d - 1)
                    for k in range(DC):
                        last = nc.tensor.matmul(pw[d % 2][:, k * P:(k + 1) * P], wn[:, k, d * P:(d + 1) * P], identf[:, :],
                                                start=True, stop=True, is_transpose=True)
                    last.then_inc(s_wt, 1)
                pe.wait_ge(s_tq, 2)
                for k in range(DC):
                    last = nc.tensor.matmul(pt[:, k * H:(k + 1) * H], w1q[:, k * P:(k + 1) * P], identb[0:H, 0:H],
                                            start=True, stop=True, is_transpose=True)
                last.then_inc(s_tt, 1)
                pe.wait_ge(s_tc, 1)
                for k in range(DC):
                    last = nc.tensor.matmul(pt[:, k * P:(k + 1) * P], w2q[:, k, :, :].rearrange("p a h -> p (a h)"),
                                            identb[:, :], start=True, stop=True, is_transpose=True)
                last.then_inc(s_tt, 1)

            @block.vector
            def _(dve):
                st = Steps(dve, s_dve)
                v = nc.vector
                dve.wait_ge(s_edges, 32)
                dve.wait_ge(s_const, 12)
                for n, (a, op, k) in enumerate(((0, ALU.logical_shift_right, 7), (0, ALU.bitwise_and, P - 1),
                                                (0, ALU.logical_shift_right, 8), (0, ALU.bitwise_and, GROUP - 1),
                                                (1, ALU.logical_shift_right, 7), (1, ALU.bitwise_and, P - 1))):
                    last = v.tensor_scalar(parts[:, n, :], ei[:, a, :], k, None, op)
                st.link(last)
                v.tensor_copy(fl[:, :, :], parts[:, :, :]).then_inc(s_parts, 1)
                dve.wait_ge(s_parts, 1)
                v.tensor_tensor(loop[:, :], ei[:, 0, :], ei[:, 1, :], ALU.is_equal).then_inc(s_parts, 1)
                dve.wait_ge(s_parts, 2)
                st.link(v.tensor_scalar(nonloop[:, :], loop[:, :], -1.0, 1.0, ALU.mult, ALU.add))
                st.link(v.scalar_tensor_tensor(out=group[:, :], in0=fl[:, 2, :], scalar=1.0, in1=nonloop[:, :],
                                               op0=ALU.add, op1=ALU.mult))
                st.link(v.tensor_scalar(group[:, :], group[:, :], -1.0, None, ALU.add))
                v.tensor_tensor(hot_g[:, :, :], iota[0:EP, 0:PAIRS].unsqueeze(2).broadcast_to([EP, PAIRS, EC]),
                                group[:, :].unsqueeze(1).broadcast_to([EP, PAIRS, EC]), ALU.is_equal).then_inc(s_grp, 1)
                dve.wait_ge(s_grp, 1)
                hg = hot_g[:, :, :].rearrange("p t c -> p (t c)")
                st.link(v.tensor_tensor_scan(run[:, :, :].rearrange("p t c -> p (t c)"), hg, hg, 0.0, ALU.add, ALU.max))
                st.link(v.memset(ends[:, 0, 0:1], 0.0))
                st.link(v.tensor_copy(ends[:, 0, 1:PAIRS], run[:, 0:PAIRS - 1, EC - 1]))
                st.link(v.tensor_tensor(ends[:, 1, :], run[:, :, EC - 1], ends[:, 0, :], ALU.subtract))
                v.engine_nop().then_inc(s_tot, 1)
                v.tensor_tensor(hot_hi[:, :, 0, :], iota[0:EP, 0:TILES].unsqueeze(1).broadcast_to([EP, EC, TILES]),
                                fl[:, 0, :].unsqueeze(2).broadcast_to([EP, EC, TILES]), ALU.is_equal).then_inc(s_hh, 1)
                v.tensor_tensor(hot_lo[:, :, :], iota[0:EP, 0:P].unsqueeze(1).broadcast_to([EP, EC, P]),
                                fl[:, 1, :].unsqueeze(2).broadcast_to([EP, EC, P]), ALU.is_equal).then_inc(s_hot, 1)
                dve.wait_ge(s_rs, 2 * DC)
                st.link(v.tensor_tensor(wsum[:, :], bn[:, :], wsum[:, :], ALU.subtract))
                v.tensor_scalar(wsum[:, :], wsum[:, :], 1.0 / D, None, ALU.mult).then_inc(s_sh, 1)
                dve.wait_ge(s_sh, 1)
                st.link(v.scalar_tensor_tensor(out=wabs[:, 1, :], in0=wsum[:, :], scalar=-1.0, in1=wsum[:, :],
                                               op0=ALU.mult, op1=ALU.max))
                st.link(v.tensor_tensor(wabs[:, 0, :], wabs[:, 0, :], wabs[:, 1, :], ALU.add))
                v.tensor_reduce(small[:, 0:1], wabs[:, 0, :], AX, ALU.max).then_inc(s_mx, 1)
                dve.wait_ge(s_off, 1)
                st.link(v.scalar_tensor_tensor(out=base[:, :], in0=pcnt[0:EP, 0:PAIRS], scalar=-1.0, in1=ends[:, 0, :],
                                               op0=ALU.add, op1=ALU.subtract))
                st.link(v.tensor_tensor(run[:, :, :], run[:, :, :], base[:, :].unsqueeze(2).broadcast_to([EP, PAIRS, EC]), ALU.add))
                st.link(v.tensor_tensor(run[:, :, :], run[:, :, :], hot_g[:, :, :], ALU.mult))
                v.tensor_reduce(rank[:, :], run[:, :, :].rearrange("p t c -> p c t"), AX, ALU.add).then_inc(s_rank, 1)
                v.tensor_reduce(small[:, 6:7], pcnt[:, 48:48 + PAIRS], AX, ALU.max).then_inc(s_rank, 1)
                dve.wait_ge(s_rank, 2)
                st.link(v.tensor_scalar(flags[:, 0:1], small[:, 6:7], float(P), None, ALU.is_gt))
                dve.wait_ge(s_armx, 1)
                st.link(v.tensor_scalar(smalli[:, 0:1], small[:, 1:2].bitcast(I32), 0x7F800000, None, ALU.bitwise_and))
                st.link(v.tensor_scalar(small[:, 3:4], smalli[:, 0:1].bitcast(F32), 2.0 ** -60, None, ALU.max))
                st.link(v.reciprocal(small[:, 2:3], small[:, 3:4]))
                st.link(v.tensor_scalar(small[:, 2:3], small[:, 2:3], 2.0 ** 14, None, ALU.mult))
                v.tensor_scalar(wsc[:, :], small[:, 3:4], 2.0 ** -14 / ZS / ZS, None, ALU.mult).then_inc(s_sc, 1)
                dve.wait_ge(s_deg, 1)
                v.tensor_tensor(hot_lo[:, :, :], iota[0:EP, 0:P].unsqueeze(1).broadcast_to([EP, EC, P]),
                                rank[:, :].unsqueeze(2).broadcast_to([EP, EC, P]), ALU.is_equal).then_inc(s_val, 1)
                st.link(v.tensor_scalar(group[:, :], fl[:, 3, :], 1.0, None, ALU.add))
                v.tensor_tensor(vals[:, :, 2, :], hot_g[:, :, :].rearrange("p t c -> p c t"),
                                group[:, :].unsqueeze(2).broadcast_to([EP, EC, PAIRS]), ALU.mult).then_inc(s_val, 1)
                dve.wait_ge(s_std, 1)
                dve.wait_ge(s_sc, 1)
                st.link(v.tensor_scalar(degs[:, 3, :], pdeg[:, 0:TILES], 1.0, -0.5, ALU.add, ALU.mult))
                st.link(v.reciprocal(degs[:, 1, :], degs[:, 0, :]))
                st.link(v.tensor_tensor(degs[:, 2, :], degs[:, 1, :], degs[:, 1, :], ALU.mult))
                st.link(v.tensor_tensor(degs[:, 2, :], degs[:, 2, :], degs[:, 3, :], ALU.mult))
                st.link(v.tensor_scalar(degs[:, 2, :], degs[:, 2, :], 1.5, ZS, ALU.add, ALU.mult))
                v.tensor_tensor(dis8[:, :], degs[:, 2, :], degs[:, 1, :], ALU.mult).then_inc(s_inv, 1)
                dve.wait_ge(s_inv, 1)
                st.link(v.tensor_scalar(dout[:, :], dis8[:, :], wsc[:, 0:1], None, ALU.mult))
                v.scalar_tensor_tensor(out=own8[:, :], in0=pdeg[:, TILES:2 * TILES], scalar=1.0, in1=dis8[:, :],
                                       op0=ALU.add, op1=ALU.mult).then_inc(s_inv, 1)
                dve.wait_ge(s_gs, 1)
                st.link(v.tensor_scalar(gam[:, :], pcnt[:, 90:92], 1.0 / (H * D), EPS_Q, ALU.mult, ALU.add))
                st.link(v.reciprocal(small[:, 8:10], gam[:, :]))
                for n, (w, q, rows) in enumerate(((w1n[:, :], w1q[:, :], H), (w2n[:, :, :], w2q[:, :, 0, :], P))):
                    st.link(v.tensor_scalar(w, w, small[0:rows, 8 + n:9 + n], MAGIC, ALU.mult, ALU.add))
                    st.link(v.tensor_scalar(w, w, MAGIC - 1.0, MAGIC + 1.0, ALU.max, ALU.min))
                    if n == 0:
                        v.tensor_scalar(q, w, -MAGIC, None, ALU.add).then_inc(s_tq, 1)
                    else:
                        st.link(v.tensor_scalar(q, w, -MAGIC, None, ALU.add))
                v.tensor_copy(w2q[:, :, 1, :], w2q[:, :, 0, :]).then_inc(s_tq, 1)
                for d in range(DC):
                    dve.wait_ge(s_whi, d + 1)
                    v.scalar_tensor_tensor(out=Wlo[:, d, :], in0=pw[d % 2][:, :], scalar=small[:, 2:3], in1=Whi[:, d, :],
                                           op0=ALU.mult, op1=ALU.subtract).then_inc(s_wlo, 1)
                dve.wait_ge(s_slots, 1)
                st.link(v.tensor_copy(tab[:, :, :].rearrange("p a t -> p (a t)"), ptab[:, :]))
                st.link(v.scalar_tensor_tensor(out=edge_row[:, :], in0=tab[:, 0, :], scalar=float(P), in1=tab[:, 1, :],
                                               op0=ALU.mult, op1=ALU.add))
                st.link(v.tensor_scalar(edge_key[:, :], tab[:, 2, :], -1.0, None, ALU.add))

    class Search:

        def __init__(self, ctx, name, width, top_bit=30, count_dt=F16, whole=False):
            self.w, self.top_bit, self.whole = width, top_bit, whole
            dt = F32 if whole else I32
            self.bit = sb(ctx, name + "_bit", [P, 2], dt)
            self.trial = sb(ctx, name + "_trial", [P, width], dt)
            self.less = sb(ctx, name + "_less", [P, width], dt)
            self.cnt = sb(ctx, name + "_count", [P, width], count_dt)
            self.k = sb(ctx, name + "_rank", [P, width])
            self.ones = ones16 if count_dt == F16 else ones
            self.counted, self.summed = sem(ctx, name + "_counted"), sem(ctx, name + "_summed")

        def start(self, st):
            v = nc.vector
            kind = float if self.whole else int
            v.memset(self.trial[:, :], kind(1 << self.top_bit))
            v.memset(self.bit[:, 0:1], kind(1 << self.top_bit))
            st.link(v.memset(self.bit[:, 1:2], kind(1 << (self.top_bit - 1))))

        def round(self, dve, st, total, n, count, first=False):
            v = nc.vector
            for j in range(self.w):
                thr = self.trial[:, j:j + 1]
                last = count(self.cnt[:, j:j + 1], thr if self.whole else thr.bitcast(F32))
                if j < self.w - 1:
                    st.link(last)
            last.then_inc(self.counted, 1)
            if not first:
                if self.whole:
                    st.link(v.tensor_scalar(self.bit[:, :], self.bit[:, :], 0.5, None, ALU.mult))
                else:
                    st.link(v.tensor_scalar(self.bit[:, :], self.bit[:, :], 1, None, ALU.logical_shift_right))
            dve.wait_ge(self.summed, n + 1)
            for j in range(self.w):
                last = v.scalar_tensor_tensor(out=self.less[:, j:j + 1], in0=total[:, j:j + 1], scalar=self.k[:, j:j + 1],
                                              in1=self.bit[:, 0:1], op0=ALU.is_lt, op1=ALU.mult)
            st.link(last)
            for j in range(self.w):
                last = v.scalar_tensor_tensor(out=self.trial[:, j:j + 1], in0=self.trial[:, j:j + 1],
                                              scalar=self.less[:, j:j + 1], in1=self.bit[:, 1:2],
                                              op0=ALU.subtract if self.whole else ALU.bitwise_xor,
                                              op1=ALU.add if self.whole else ALU.bitwise_or)
            st.link(last)

        def steps(self):
            return self.w + 2

        def rounds(self, dve, st, total, count):
            for n in range(self.top_bit + 1):
                self.round(dve, st, total, n, count, first=(n == 0))

        def sums(self, pe, total):
            for n in range(self.top_bit + 1):
                self.sum_up(pe, total, n)

        def sum_up(self, pe, total, n):
            pe.wait_ge(self.counted, n + 1)
            nc.tensor.matmul(total, self.ones[:, :], self.cnt[:, :], start=True, stop=True).then_inc(self.summed, 1)

    with ExitStack() as c:
        xs = sb(c, "xs", [P, 4, D])
        xg = sb(c, "xg", [P, 2, D])
        rowc = sb(c, "rowc", [P, 2], I32)
        dg = sb(c, "dg", [P, 2])
        hit = sb(c, "hit", [P, 2, GROUP], F16)
        z32 = sb(c, "z32", [P, D])
        zg32 = sb(c, "zg32", [P, D])
        zhi, zlo = sb(c, "zhi", [P, 2, D], F16), sb(c, "zlo", [P, 2, D], F16)
        zghi, zglo = sb(c, "zghi", [P, 2, D], F16), sb(c, "zglo", [P, 2, D], F16)
        yhi, ylo = sb(c, "yhi", [P, 2, D], F16), sb(c, "ylo", [P, 2, D], F16)
        x1 = sb(c, "x1", [P, 2, D])
        hs = sb(c, "hs", [P, 4, D])
        vs = sb(c, "vs", [P, 2, D])
        vsam = sb(c, "vsam", [P, SAMPLE, D])
        sam = sb(c, "sam", [P, SAMPLE * 16])
        mask = sb(c, "mask", [P, D])
        top8 = sb(c, "top8", [P, 4, 8])
        junk = sb(c, "junk_layers", [P, D], BF16)
        bst = {n: sb(c, "bst_" + n, [P, 12]) for n in "xge"}
        mv = {n: sb(c, "mv_" + n, [P, 4, 2]) for n in "xge"}
        std = {n: sb(c, "std_" + n, [P, 4]) for n in "xge"}
        rcp = {n: sb(c, "rcp_" + n, [P, 4]) for n in "xge"}
        cf = {n: sb(c, "cf_" + n, [P, 4, 2]) for n in "xge"}
        zT = [ps(c, f"zT{i}", [P, D]) for i in range(2)]
        prod = [ps(c, f"prod{i}", [P, D]) for i in range(2)]

        loaded = [sem(c, f"x_loaded{i}") for i in range(4)]
        gathered = [sem(c, f"neighbours_loaded{i}") for i in range(2)]
        x1_out = [sem(c, f"x1_stored{i}") for i in range(2)]
        h2_out = [sem(c, f"h2_stored{i}") for i in range(4)]
        names = ("x_stats_ready x_std_ready x_coef_ready x_z_ready x_high_ready x_low_ready g_stats_ready g_std_ready "
                 "hits_ready g_coef_ready g_z_ready g_high_ready g_low_ready turned y_high_ready y_low_ready multiplied x1_ready "
                 "x1_stats_ready x1_std_ready x1_coef_ready h0_ready h1_ready h2_ready abs_ready kept "
                 "bracket_ready rows_picked layers_dve_steps layers_act_steps").split()
        S = {n: sem(c, n) for n in names}
        find = Search(c, "sample", 2)

        def steps_over(eng, body, first, lo, hi, last, st=None, per=0, between=None, late=None, late_per=0):
            for k in range(first, lo):
                if between and k == SAMPLE + 3:
                    between()
                body(Tile(0, k))
            if late:
                with eng.Fori(lo // 4, (lo + SAMPLE) // 4) as i:
                    if st:
                        st.enter(i, lo // 4, per + late_per)
                    for u in range(4):
                        late(Tile(i, u))
                if st:
                    st.leave(SAMPLE // 4)
                lo += SAMPLE
            with eng.Fori(lo // 4, hi // 4) as i:
                if st:
                    st.enter(i, lo // 4, per)
                for u in range(4):
                    body(Tile(i, u))
            if st:
                st.leave((hi - lo) // 4)
            for k in range(hi, last + 1):
                body(Tile(0, k))

        LO, HI = 8, 76
        assert SAMPLE + 3 <= LO and SAMPLE % 4 == 0
        SUMS = SAMPLE % 2

        with nc.Block() as block:

            @block.sync
            def _(sp):
                def load(t):
                    after(sp, S["x1_ready"], t.t - 3)
                    rows = TAIL if t.last else P
                    if t.last:
                        src = x_in[LAST * P:N, :]
                    else:
                        src = x_in[bass.ds(t.t * P, P), :]
                    sp.dma_start(xs[0:rows, t.slot, :], src).then_inc(loaded[t.slot], 16)

                def place(t):
                    return (TAIL, slice(LAST * P, N)) if t.last else (P, bass.ds(t.t * P, P))

                def step(t):
                    rows, dst = place(t)
                    after(sp, S["x1_ready"], t.t + 1)
                    sp.dma_start(x1_dram[dst, :], x1[0:rows, t.odd, :]).then_inc(x1_out[t.odd], 16)
                    nxt = t.plus(4)
                    if nxt.within(0, TILES):
                        load(nxt)
                    if t.plus(-1).within(0, TILES):
                        store_h2(t.plus(-1))

                def store_h2(t):
                    rows, dst = place(t)
                    sp.wait_ge(S["h2_ready"], t.t + 1)
                    sp.dma_start(h2_dram[dst, :], hs[0:rows, t.slot, :]).then_inc(h2_out[t.slot], 16)

                for k in range(4):
                    load(Tile(0, k))
                for k in range(4):
                    step(Tile(0, k))
                with sp.Fori(1, 18) as i:
                    for u in range(4):
                        step(Tile(i, u))
                for k in range(72, TILES):
                    step(Tile(0, k))
                store_h2(Tile(0, LAST))
                for s in range(4):
                    sp.wait_ge(h2_out[s], 16 * len(range(s, TILES, 4)))
                for s in range(2):
                    sp.wait_ge(x1_out[s], 16 * len(range(s, TILES, 2)))

            @block.gpsimd
            def _(pool):
                def gather(t):
                    o, j = t.po, t.half
                    after(pool, S["g_low_ready"], j - 1)
                    nc.gpsimd.tensor_copy(rowc[:, o:o + 1], edge_row[:, bass.ds(j, 1)]).then_inc(S["rows_picked"], 1)
                    wait_alone(pool, S["rows_picked"], j + 1)
                    pool.indirect_dma_start(xg[:, o, :], None, x_in[:, :],
                                            bass.IndirectOffsetOnAxis(ap=rowc[:, o:o + 1], axis=0),
                                            bounds_check=N - 1, oob_is_err=False).then_inc(gathered[o], 16)
                    pool.indirect_dma_start(dg[:, o:o + 1], None, dis_dram[:, :],
                                            bass.IndirectOffsetOnAxis(ap=rowc[:, o:o + 1], axis=0),
                                            bounds_check=NPAD - 1, oob_is_err=False).then_inc(gathered[o], 16)

                def step(k):
                    f, b = k.plus(2), k.plus(-1)
                    if f.within(0, TILES):
                        pool.wait_ge(S["x_high_ready"], f.t + 1)
                        pool.wait_ge(S["x_z_ready"], f.t + 1)
                        after(pool, S["turned"], f.t - 1)
                        nc.gpsimd.tensor_tensor(zlo[:, f.odd, :], z32[:, :], zhi[:, f.odd, :], ALU.subtract)\
                            .then_inc(S["x_low_ready"], 1)
                    e = k.plus(3)
                    if e.odd == 0 and e.within(0, TILES):
                        pool.wait_ge(S["g_high_ready"], e.half + 1)
                        pool.wait_ge(S["g_z_ready"], e.half + 1)
                        after(pool, S["turned"], e.t - 2)
                        nc.gpsimd.tensor_tensor(zglo[:, e.po, :], zg32[:, :], zghi[:, e.po, :], ALU.subtract)\
                            .then_inc(S["g_low_ready"], 1)
                        if e.plus(4).within(0, TILES):
                            gather(e.plus(4))
                    if b.within(0, TILES):
                        pool.wait_ge(S["h0_ready"], b.t + 1)
                        nc.gpsimd.tensor_tensor(hs[:, b.slot, :], hs[:, b.slot, :], lng[:, :], ALU.mult).then_inc(S["h1_ready"], 1)
                        pool.wait_ge(S["h1_ready"], b.t + 1)
                        nc.gpsimd.tensor_tensor(hs[:, b.slot, :], hs[:, b.slot, :], lnb[:, :], ALU.add).then_inc(S["h2_ready"], 1)

                gather(Tile(0, 0))
                gather(Tile(0, 2))
                steps_over(pool, step, -3, LO, 72, LAST + 1)

            @block.scalar
            def _(act):
                def root(n, ready, done, t, cnt, var_scale, eps):
                    act.wait_ge(S[ready], cnt)
                    nc.scalar.activation(std[n][:, t.slot:t.slot + 1], mv[n][:, t.slot, 1:2], ACT.Sqrt,
                                         bias=eps[:, 0:1], scale=var_scale).then_inc(S[done], 1)

                def z_of(n, t, cnt, rows, z, hi, slot, z_free, hi_free):
                    act.wait_ge(S[n + "_coef_ready"], cnt)
                    after(act, S[n + "_low_ready"], z_free)
                    c0, c1 = cf[n][:, t.slot, 0:1], cf[n][:, t.slot, 1:2]
                    nc.scalar.activation(z[:, :], rows, ACT.Identity, bias=c1, scale=c0).then_inc(S[n + "_z_ready"], 1)
                    after(act, S["turned"], hi_free)
                    nc.scalar.activation(hi[:, slot, :], rows, ACT.Identity, bias=c1, scale=c0).then_inc(S[n + "_high_ready"], 1)

                def step(k, late=False):
                    t, b, f, e = k.plus(1), k.plus(-1), k.plus(2), k.plus(3)
                    early = isinstance(k.i, int) and k.t == -1
                    edges = e.odd == 0 and e.within(0, TILES)
                    if f.within(0, TILES):
                        root("x", "x_stats_ready", "x_std_ready", f, f.t + 1, 1.0, eps_x)
                    if edges:
                        root("g", "g_stats_ready", "g_std_ready", e, e.half + 1, 1.0, eps_x)
                    if early:
                        z_of("x", f, f.t + 1, xs[:, f.slot, :], z32, zhi, f.odd, f.t, f.t - 1)
                    if t.within(0, TILES):
                        act.wait_ge(S["turned"], t.t + 1)
                        after(act, S["multiplied"], t.t - 1)
                        nc.scalar.activation(yhi[:, t.odd, :], zT[t.odd][:, :], ACT.Copy).then_inc(S["y_high_ready"], 1)
                    if f.within(0, TILES) and not early:
                        z_of("x", f, f.t + 1, xs[:, f.slot, :], z32, zhi, f.odd, f.t, f.t - 1)
                    if edges:
                        z_of("g", e, e.half + 1, xg[:, e.po, :], zg32, zghi, e.po, e.half, e.t - 2)
                    if b.within(0, TILES):
                        root("e", "x1_stats_ready", "x1_std_ready", b, b.t + 1, 1.0 + EPS_LN, eps_xx)
                        act.wait_ge(S["x1_coef_ready"], b.t + 1)
                        after(act, h2_out[b.slot], 16 * b.turn)
                        nc.scalar.activation(hs[:, b.slot, :], x1[:, b.odd, :], ACT.Identity, bias=cf["e"][:, b.slot, 1:2],
                                             scale=cf["e"][:, b.slot, 0:1]).then_inc(S["h0_ready"], 1)
                    t = k.plus(-2)
                    if t.within(0, TILES):
                        sample = isinstance(t.i, int) and t.t < SAMPLE
                        act.wait_ge(S["h2_ready"], t.t + 1)
                        if not sample:
                            after(act, S["kept"], t.t - 1)
                        v = vsam[:, t.t, :] if sample else vs[:, t.odd, :]
                        nc.scalar.activation(v, hs[:, t.slot, :], ACT.Abs).then_inc(S["abs_ready"], 1)
                        if not isinstance(t.i, int) or t.t > SAMPLE:
                            act.wait_ge(S["abs_ready"], t.t + 1)
                            if late:
                                before = 2 * k.t - (2 * LO - 3)
                            elif isinstance(t.i, int) and k.t < LO:
                                before = t.t - SAMPLE
                            else:
                                before = t.t
                            count(t, v, before)

                def count(t, v, before):
                    rows = TAIL if t.last else P
                    after(act, S["layers_act_steps"], before)
                    nc.scalar.activation(junk[0:rows, :], v[0:rows, :], ACT.Sign, bias=nhigh[0:rows, 0:1],
                                         accum_out=over[0:rows, bass.ds(t.t, 1)]).then_inc(S["layers_act_steps"], 1)

                def catch_up():
                    act.wait_ge(S["bracket_ready"], 1)
                    act.wait_ge(S["abs_ready"], SAMPLE + 1)
                    count(Tile(0, SAMPLE), vs[:, SAMPLE % 2, :], 0)

                def late(k):
                    t = k.plus(-LO)
                    count(t, vsam[:, bass.ds(t.t, 1), :].rearrange("p a d -> p (a d)"), 2 * k.t - (2 * LO - 2))
                    step(k, True)

                steps_over(act, step, -3, LO, HI, LAST + 3, between=catch_up, late=late)

            @block.tensor
            def _(pe):
                def turn_over(t):
                    j = t.half
                    pe.wait_ge(S["x_high_ready"], t.t + 1)
                    pe.wait_ge(S["x_low_ready"], t.t + 1)
                    pe.wait_ge(S["g_high_ready"], j + 1)
                    pe.wait_ge(S["g_low_ready"], j + 1)
                    pe.wait_ge(S["hits_ready"], j + 1)
                    after(pe, S["y_high_ready"], t.t - 1)
                    after(pe, S["y_low_ready"], t.t - 1)
                    sel = hit[:, t.po, t.odd * P:(t.odd + 1) * P]
                    for d in range(DC):
                        o = zT[t.odd][:, d * P:(d + 1) * P]
                        dd = slice(d * P, (d + 1) * P)
                        nc.tensor.matmul(o, zhi[:, t.odd, dd], ident[:, :], start=True, stop=False)
                        nc.tensor.matmul(o, zlo[:, t.odd, dd], ident[:, :], start=False, stop=False)
                        nc.tensor.matmul(o, zghi[:, t.po, dd], sel, start=False, stop=False)
                        last = nc.tensor.matmul(o, zglo[:, t.po, dd], sel, start=False, stop=True)
                    last.then_inc(S["turned"], 1)

                def multiply(t, chunks=range(DC)):
                    if chunks[0] == 0:
                        pe.wait_ge(S["y_high_ready"], t.t + 1)
                        pe.wait_ge(S["y_low_ready"], t.t + 1)
                        after(pe, S["x1_ready"], t.t - 1)
                    for d in chunks:
                        dd = slice(d * P, (d + 1) * P)
                        for y, W in ((yhi, Whi), (yhi, Wlo), (ylo, Whi)):
                            for h in range(2):
                                hh = slice(h * 512, (h + 1) * 512)
                                last = nc.tensor.matmul(prod[t.odd][:, hh], y[:, t.odd, dd], W[:, d, hh],
                                                        start=(d == 0 and y is yhi and W is Whi),
                                                        stop=(d == DC - 1 and y is ylo))
                    if d == DC - 1:
                        last.then_inc(S["multiplied"], 1)

                def step(k):
                    t = k.plus(1)
                    if t.within(0, TILES):
                        turn_over(t)
                    if k.within(0, TILES):
                        multiply(k)

                for k in range(-1, SAMPLE + 3):
                    step(Tile(0, k))
                pe.wait_ge(S["y_low_ready"], SAMPLE + 3)
                for n in range(DC):
                    find.sum_up(pe, zT[SUMS][:, 0:2], n)
                    multiply(Tile(0, SAMPLE + 3), [n])
                for n in range(DC, SBITS):
                    find.sum_up(pe, zT[SUMS][:, 0:2], n)
                pe.wait_ge(S["bracket_ready"], 1)
                turn_over(Tile(0, SAMPLE + 4))
                for k in range(SAMPLE + 4, LO):
                    step(Tile(0, k))
                with pe.Fori(LO // 4, HI // 4) as i:
                    for u in range(4):
                        step(Tile(i, u))
                for k in range(HI, TILES):
                    step(Tile(0, k))

            @block.vector
            def _(dve):
                v = nc.vector
                st = Steps(dve, S["layers_dve_steps"])

                def stats(n, rows, slot, ready):
                    v.bn_stats(bst[n][:, 0:6], rows[:, 0:512])
                    st.link(v.bn_stats(bst[n][:, 6:12], rows[:, 512:1024]), alone=True)
                    v.bn_aggr(mv[n][:, slot, :], bst[n][:, :]).then_inc(S[ready], 1)

                def coef(n, s, weight, ready):
                    c1 = slice(s, s + 1)
                    st.link(v.reciprocal(rcp[n][:, c1], std[n][:, c1]))
                    st.link(v.tensor_tensor(cf[n][:, s, 0:1], rcp[n][:, c1], weight, ALU.mult))
                    v.scalar_tensor_tensor(out=cf[n][:, s, 1:2], in0=mv[n][:, s, 0:1], scalar=cf[n][:, s, 0:1], in1=weight,
                                           op0=ALU.mult, op1=ALU.subtract, reverse1=True).then_inc(S[ready], 1)

                def keep(t, v_in):
                    rows = TAIL if t.last else P
                    st.link(v.scalar_tensor_tensor(out=mask[0:rows, :], in0=v_in[0:rows, :], scalar=brk[0:rows, 1:2],
                                                   in1=v_in[0:rows, :], op0=ALU.is_le, op1=ALU.mult), alone=True)
                    st.link(v.max(top8[0:rows, t.slot, :], mask[0:rows, :]))
                    return v.tensor_copy(cand[0:rows, bass.ds(t.t * 8, 8)], top8[0:rows, t.slot, :])

                def step(k):
                    t, b, f, e = k.plus(1), k.plus(-1), k.plus(2), k.plus(3)
                    edges = e.odd == 0 and e.within(0, TILES)
                    if f.within(0, TILES):
                        dve.wait_ge(loaded[f.slot], 16 * f.turn + 16)
                        stats("x", xs[:, f.slot, :], f.slot, "x_stats_ready")
                    if edges:
                        dve.wait_ge(gathered[e.po], 32 * e.turn + 32)
                        stats("g", xg[:, e.po, :], e.slot, "g_stats_ready")
                        after(dve, S["turned"], e.t - 2)
                        v.tensor_scalar(hit[:, e.po, :], iota[:, :], edge_key[:, bass.ds(e.half, 1)], None, ALU.is_equal)\
                            .then_inc(S["hits_ready"], 1)
                    if b.within(0, TILES):
                        dve.wait_ge(S["multiplied"], b.t + 1)
                        after(dve, x1_out[b.odd], 16 * b.half)
                        after(dve, S["h0_ready"], b.t - 1)
                        v.scalar_tensor_tensor(out=x1[:, b.odd, :], in0=prod[b.odd][:, :], scalar=dout[:, bass.ds(b.t, 1)],
                                               in1=xs[:, b.slot, :], op0=ALU.mult, op1=ALU.add).then_inc(S["x1_ready"], 1)
                    if f.within(0, TILES):
                        dve.wait_ge(S["x_std_ready"], f.t + 1)
                        coef("x", f.slot, own8[:, bass.ds(f.t, 1)], "x_coef_ready")
                    if edges:
                        dve.wait_ge(S["g_std_ready"], e.half + 1)
                        coef("g", e.slot, dg[:, e.po:e.po + 1], "g_coef_ready")
                    if b.within(0, TILES):
                        dve.wait_ge(S["x1_ready"], b.t + 1)
                        stats("e", x1[:, b.odd, :], b.slot, "x1_stats_ready")
                    if t.within(0, TILES):
                        dve.wait_ge(S["y_high_ready"], t.t + 1)
                        after(dve, S["multiplied"], t.t - 1)
                        v.tensor_tensor(ylo[:, t.odd, :], zT[t.odd][:, :], yhi[:, t.odd, :], ALU.subtract)\
                            .then_inc(S["y_low_ready"], 1)
                    if b.within(0, TILES):
                        dve.wait_ge(S["x1_std_ready"], b.t + 1)
                        s = b.slot
                        st.link(v.reciprocal(cf["e"][:, s, 0:1], std["e"][:, s:s + 1]))
                        v.scalar_tensor_tensor(out=cf["e"][:, s, 1:2], in0=mv["e"][:, s, 0:1], scalar=-1.0,
                                               in1=cf["e"][:, s, 0:1], op0=ALU.mult, op1=ALU.mult)\
                            .then_inc(S["x1_coef_ready"], 1)
                    t = k.plus(-3)
                    if t.within(0, TILES):
                        dve.wait_ge(S["abs_ready"], t.t + 1)
                        if isinstance(t.i, int) and t.t < SAMPLE:
                            v.max(sam[:, t.t * 16:t.t * 16 + 8], vsam[:, t.t, 0:512])
                            v.max(sam[:, t.t * 16 + 8:t.t * 16 + 16], vsam[:, t.t, 512:1024]).then_inc(S["kept"], 1)
                        else:
                            keep(t, vs[:, t.odd, :]).then_inc(S["kept"], 1)

                def bracket():
                    dve.wait_ge(S["kept"], SAMPLE)
                    find.start(st)
                    st.link(v.memset(find.k[:, 0:1], SLO))
                    st.link(v.memset(find.k[:, 1:2], SHI))
                    for n in range(SBITS):
                        find.round(dve, st, zT[SUMS][:, 0:2], n, lambda cnt, thr: v.tensor_scalar(
                            mask[:, 0:SAMPLE * 16], sam[:, :], thr, None, ALU.is_ge, ALU.add, accum_out=cnt), first=(n == 0))
                    st.link(v.tensor_scalar(find.trial[:, 1:2], find.trial[:, 1:2], (1 << (31 - SBITS)) - 1, None, ALU.bitwise_or))
                    st.link(v.tensor_copy(brk[:, :], find.trial[:, :].bitcast(F32)))
                    v.tensor_scalar(nhigh[:, :], brk[:, 1:2], -1.0, None, ALU.mult).then_inc(S["bracket_ready"], 1)

                per = (2 * 4 + 2) + 4 + 2 * 4 + 2 * 2 + 2 * 4
                def late(k):
                    step(k)
                    t = k.plus(-LO)
                    st.link(keep(t, vsam[:, bass.ds(t.t, 1), :].rearrange("p a d -> p (a d)")))

                steps_over(dve, step, -3, LO, HI, LAST + 3, st=st, per=per, between=bracket, late=late, late_per=3 * 4)

    CT, CR = N // 125, 125
    with ExitStack() as c:
        ei = sb(c, "c_edges", [EP, 2, EC], I32)
        ef = sb(c, "c_edgef", [EP, 2, EC])
        own = sb(c, "c_loop", [EP, EC])
        rel = sb(c, "c_rel", [EP, 2, EC])
        hots = sb(c, "c_hots", [EP, 2, EC, CR], BF16)
        off = sb(c, "c_off", [P, 2])
        xr = sb(c, "c_x", [CR, 2, D])
        wt = sb(c, "c_w", [CR, 3])
        bst = sb(c, "c_bst", [CR, 12])
        mv = sb(c, "c_mv", [CR, 2])
        std = sb(c, "c_std", [CR, 1])
        cf = sb(c, "c_cf", [CR, 2])
        z = sb(c, "c_z", [CR, D])
        cnts = sb(c, "c_counts", [CR, CR])
        eye = sb(c, "c_eye", [P, P])
        yacc = sb(c, "c_y", [P, DC, CR])
        yh, yl = sb(c, "c_yhi", [P, DC, CR], F16), sb(c, "c_ylo", [P, DC, CR], F16)
        res = sb(c, "c_res", [CR, 2, D])
        pa = ps(c, "c_pa", [CR, CR])
        py = ps(c, "c_py", [P, DC, P])
        pp = ps(c, "c_pp", [CR, D])
        s_in, s_s, s_t, s_st, s_eye = (sem(c, "c_" + n) for n in ("edges_in", "s_in", "t_in", "stored", "eye_ready"))
        s_var, s_root, s_z, s_hot, s_a, s_as, s_y, s_ya, s_yt, s_yb, s_pp, s_res = (sem(c, "c_" + n) for n in (
            "stats_ready", "root_ready", "z_ready", "hots_ready", "counts_ready", "counts_copied", "part_ready",
            "part_added", "own_turned", "y_ready", "multiplied", "rows_ready"))
        s_dve = sem(c, "c_dve_steps")

        with nc.Block() as block:

            def crowded(eng):
                return eng.If(eng.value_load(flags[0:1, 0:1], min_val=0, max_val=1) > 0)

            @block.sync
            def _(sp):
                with crowded(sp):
                    sp.dma_start(ei[:, 0, :], src_in.rearrange("(p c) -> p c", c=EC)).then_inc(s_in, 16)
                    sp.dma_start(ei[:, 1, :], dst_in.rearrange("(p c) -> p c", c=EC)).then_inc(s_in, 16)
                    with sp.Fori(0, CT) as t:
                        sp.wait_ge(s_res, t + 1)
                        sp.dma_start(xr[:, 0, :], x_in[bass.ds(t * CR, CR), :]).then_inc(s_t, 16)
                        sp.dma_start(wt[:, 0:1], own_dram[bass.ds(t * CR, CR), :]).then_inc(s_t, 16)
                        sp.dma_start(wt[:, 1:2], dis_dram[bass.ds(t * CR, CR), :]).then_inc(s_t, 16)
                        with sp.Fori(0, CT) as s:
                            sp.wait_ge(s_z, t * (CT + 1) + s + 1)
                            sp.dma_start(xr[:, 1, :], x_in[bass.ds(s * CR, CR), :]).then_inc(s_s, 16)
                            sp.dma_start(wt[:, 2:3], dis_dram[bass.ds(s * CR, CR), :]).then_inc(s_s, 16)
                        sp.wait_ge(s_res, t + 2)
                        sp.dma_start(x1_dram[bass.ds(t * CR, CR), :], res[:, 0, :]).then_inc(s_st, 16)
                        sp.dma_start(h2_dram[bass.ds(t * CR, CR), :], res[:, 1, :]).then_inc(s_st, 16)
                        wait_alone(sp, s_st, 32 * t + 32)

            @block.gpsimd
            def _(pool):
                with crowded(pool):
                    nc.gpsimd.memset(eye[:, :], 0.0).then_inc(s_eye, 1)
                    pool.wait_ge(s_eye, 1)
                    nc.gpsimd.affine_select(out=eye[:, :], in_=eye[:, :], compare_op=ALU.not_equal, fill=1.0, base=0,
                                            pattern=[[-1, P]], channel_multiplier=1).then_inc(s_eye, 1)

            @block.scalar
            def _(act):
                with crowded(act):
                    with act.Fori(0, CT) as t:
                        with act.Fori(0, CT + 1) as s:
                            act.wait_ge(s_var, t * (CT + 2) + s + 1)
                            nc.scalar.activation(std[:, :], mv[:, 1:2], ACT.Sqrt, bias=eps_x[0:CR, 0:1]).then_inc(s_root, 1)
                        act.wait_ge(s_var, t * (CT + 2) + CT + 2)
                        nc.scalar.activation(std[:, :], mv[:, 1:2], ACT.Sqrt, bias=eps_xx[0:CR, 0:1],
                                             scale=1.0 + EPS_LN).then_inc(s_root, 1)

            @block.tensor
            def _(pe):
                with crowded(pe):
                    pe.wait_ge(s_eye, 2)
                    with pe.Fori(0, CT) as t:
                        with pe.Fori(0, CT) as s:
                            pe.wait_ge(s_hot, t * CT + s + 1)
                            for e in range(EC):
                                last = nc.tensor.matmul(pa[:, :], hots[:, 1, e, :], hots[:, 0, e, :],
                                                        start=(e == 0), stop=(e == EC - 1))
                            last.then_inc(s_a, 1)
                            pe.wait_ge(s_as, t * CT + s + 1)
                            for d in range(DC):
                                last = nc.tensor.matmul(py[:, d, 0:CR], z[:, d * P:(d + 1) * P], cnts[:, :],
                                                        start=True, stop=True)
                            last.then_inc(s_y, 1)
                        pe.wait_ge(s_z, (t + 1) * (CT + 1) + 1)
                        for d in range(DC):
                            last = nc.tensor.matmul(py[:, d, 0:CR], z[:, d * P:(d + 1) * P], eye[0:CR, 0:CR],
                                                    start=True, stop=True)
                        last.then_inc(s_yt, 1)
                        pe.wait_ge(s_yb, t + 1)
                        for d in range(DC):
                            for y, W in ((yh, Whi), (yh, Wlo), (yl, Whi)):
                                for h in range(2):
                                    hh = slice(h * 512, (h + 1) * 512)
                                    last = nc.tensor.matmul(pp[:, hh], y[:, d, :], W[:, d, hh],
                                                            start=(d == 0 and y is yh and W is Whi),
                                                            stop=(d == DC - 1 and y is yl))
                        last.then_inc(s_pp, 1)

            @block.vector
            def _(dve):
                v = nc.vector
                st = Steps(dve, s_dve)

                def stats(rows):
                    v.bn_stats(bst[:, 0:6], rows[:, 0:512])
                    st.link(v.bn_stats(bst[:, 6:12], rows[:, 512:1024]), alone=True)
                    v.bn_aggr(mv[:, :], bst[:, :]).then_inc(s_var, 1)

                def normalise(rows, weight, out_rows, n_root):
                    dve.wait_ge(s_root, n_root)
                    st.link(v.reciprocal(cf[:, 0:1], std[:, :]))
                    if weight is not None:
                        st.link(v.tensor_tensor(cf[:, 0:1], cf[:, 0:1], weight, ALU.mult))
                    st.link(v.scalar_tensor_tensor(out=cf[:, 1:2], in0=mv[:, 0:1], scalar=-1.0, in1=cf[:, 0:1],
                                                   op0=ALU.mult, op1=ALU.mult))
                    if weight is not None:
                        st.link(v.tensor_tensor(cf[:, 1:2], cf[:, 1:2], weight, ALU.add))
                    return v.tensor_scalar(out_rows, rows, cf[:, 0:1], cf[:, 1:2], ALU.mult, ALU.add)

                def hot(n):
                    st.link(v.tensor_scalar(rel[:, n, :], ef[:, n, :], off[0:EP, n:n + 1], None, ALU.subtract))
                    return v.tensor_tensor(hots[:, n, :, :], iota[0:EP, 0:CR].unsqueeze(1).broadcast_to([EP, EC, CR]),
                                           rel[:, n, :].unsqueeze(2).broadcast_to([EP, EC, CR]), ALU.is_equal)

                with crowded(dve):
                    v.engine_nop().then_inc(s_z, 1)
                    v.engine_nop().then_inc(s_res, 1)
                    dve.wait_ge(s_in, 32)
                    st.link(v.tensor_copy(ef[:, :, :], ei[:, :, :]))
                    st.link(v.tensor_tensor(own[:, :], ef[:, 0, :], ef[:, 1, :], ALU.is_equal))
                    st.link(v.scalar_tensor_tensor(out=ef[:, 0, :], in0=own[:, :], scalar=-2.0 * N, in1=ef[:, 0, :],
                                                   op0=ALU.mult, op1=ALU.add))
                    st.link(v.memset(off[:, 0:1], 0.0))
                    with dve.Fori(0, CT) as t:
                        st.enter(t, 0, 3 + CT * 8 + 16)
                        st.link(v.memset(off[:, 1:2], 0.0))
                        st.link(v.memset(yacc[:, :, :], 0.0))
                        st.link(hot(0), alone=True)
                        with dve.Fori(0, CT) as s:
                            st.enter(s, 0, 8)
                            dve.wait_ge(s_s, (t * CT + s) * 32 + 32)
                            stats(xr[:, 1, :])
                            normalise(xr[:, 1, :], wt[:, 2:3], z[:, :], t * (CT + 2) + s + 1).then_inc(s_z, 1)
                            dve.wait_ge(s_z, t * (CT + 1) + s + 2)
                            hot(1).then_inc(s_hot, 1)
                            dve.wait_ge(s_a, t * CT + s + 1)
                            v.tensor_copy(cnts[:, :], pa[:, :]).then_inc(s_as, 1)
                            dve.wait_ge(s_y, t * CT + s + 1)
                            st.link(v.tensor_tensor(yacc[:, :, :], py[:, :, 0:CR], yacc[:, :, :], ALU.add))
                            st.link(v.tensor_scalar(off[:, 1:2], off[:, 1:2], float(CR), None, ALU.add))
                        st.leave(CT)
                        dve.wait_ge(s_t, t * 48 + 48)
                        stats(xr[:, 0, :])
                        normalise(xr[:, 0, :], wt[:, 0:1], z[:, :], t * (CT + 2) + CT + 1).then_inc(s_z, 1)
                        dve.wait_ge(s_yt, t + 1)
                        st.link(v.tensor_tensor(yacc[:, :, :], py[:, :, 0:CR], yacc[:, :, :], ALU.add))
                        st.link(v.tensor_copy(yh[:, :, :], yacc[:, :, :]))
                        v.tensor_tensor(yl[:, :, :], yacc[:, :, :], yh[:, :, :], ALU.subtract).then_inc(s_yb, 1)
                        st.link(v.tensor_scalar(wt[:, 1:2], wt[:, 1:2], wsc[0:CR, 0:1], None, ALU.mult))
                        dve.wait_ge(s_pp, t + 1)
                        st.link(v.scalar_tensor_tensor(out=res[:, 0, :], in0=pp[:, :], scalar=wt[:, 1:2], in1=xr[:, 0, :],
                                                       op0=ALU.mult, op1=ALU.add))
                        stats(res[:, 0, :])
                        st.link(normalise(res[:, 0, :], None, res[:, 1, :], t * (CT + 2) + CT + 2))
                        st.link(v.tensor_tensor(res[:, 1, :], res[:, 1, :], lng[0:CR, :], ALU.mult))
                        st.link(v.tensor_scalar(off[:, 0:1], off[:, 0:1], float(CR), None, ALU.add))
                        v.tensor_tensor(res[:, 1, :], res[:, 1, :], lnb[0:CR, :], ALU.add).then_inc(s_res, 1)
                    st.leave(CT)

    first = ExitStack()
    h2_buf = sb(first, "h_in", [P, 8, D])
    h2_in = [sem(first, f"h_loaded{i}") for i in range(8)]

    with ExitStack() as c:
        part = sb(c, "part", [P, 4])
        tot = sb(c, "tot", [P, 4])
        chk = sb(c, "chk", [P, 7])
        step = sb(c, "range1_step", [P, 3])
        whole = sb(c, "range1_whole", [P, TILES * 8])
        junk = sb(c, "junk_range", [P, TILES * 8])
        WBITS = 20
        find = Search(c, "range1", 1, top_bit=WBITS - 1, whole=True)
        psum = ps(c, "range1_sums", [P, 8])
        s_part, s_tot = sem(c, "range1_parts_ready"), sem(c, "range1_totals_ready")
        s_dve = sem(c, "range1_dve_steps")

        with nc.Block() as block:

            @block.sync
            def _(sp):
                for k in range(8):
                    sp.dma_start(h2_buf[:, k, :], h2_dram[k * P:(k + 1) * P, :]).then_inc(h2_in[k], 16)

            @block.tensor
            def _(pe):
                pe.wait_ge(s_part, 4)
                nc.tensor.matmul(psum[:, 0:4], ones[:, :], part[:, :], start=True, stop=True).then_inc(s_tot, 1)
                find.sums(pe, psum[:, 4:5])

            @block.vector
            def _(dve):
                v = nc.vector
                st = Steps(dve, s_dve)
                v.tensor_reduce(part[:, 0:1], over[:, :], AX, ALU.add).then_inc(s_part, 1)
                dve.wait_ge(s_part, 1)
                v.tensor_scalar(junk[:, :], cand[:, :], brk[:, 1:2], None, ALU.is_equal, ALU.add,
                                accum_out=part[:, 1:2]).then_inc(s_part, 1)
                dve.wait_ge(s_part, 2)
                v.tensor_scalar(junk[:, :], cand[:, :], brk[:, 0:1], None, ALU.is_ge, ALU.add,
                                accum_out=part[:, 2:3]).then_inc(s_part, 1)
                dve.wait_ge(s_part, 3)
                v.tensor_scalar(junk[:, 0:TILES], cand[:, :].rearrange("p (t k) -> p t k", k=8)[:, :, 7], brk[:, 0:1], None,
                                ALU.is_ge, ALU.add, accum_out=part[:, 3:4]).then_inc(s_part, 1)
                st.link(v.tensor_scalar(step[:, 0:1].bitcast(I32), brk[:, 0:1].bitcast(I32), 0x7F800000, None, ALU.bitwise_and))
                st.link(v.tensor_scalar(step[:, 0:1], step[:, 0:1], 2.0 ** -60, None, ALU.max))
                st.link(v.reciprocal(step[:, 1:2], step[:, 0:1]))
                st.link(v.tensor_scalar(step[:, 1:2], step[:, 1:2], 2.0 ** 23, None, ALU.mult))
                st.link(v.tensor_scalar(whole[:, :], cand[:, :], brk[:, 0:1], step[:, 1:2], ALU.subtract, ALU.mult))
                st.link(v.tensor_scalar(step[:, 2:3], brk[:, 1:2], brk[:, 0:1], step[:, 1:2], ALU.subtract, ALU.mult))
                dve.wait_ge(s_tot, 1)
                st.link(v.tensor_copy(tot[:, :], psum[:, 0:4]))
                st.link(v.tensor_tensor(chk[:, 0:1], tot[:, 0:1], tot[:, 1:2], ALU.subtract))
                st.link(v.tensor_scalar(chk[:, 0:1], chk[:, 0:1], float(N * D), 0.5, ALU.add, ALU.mult))
                st.link(v.tensor_scalar(find.k[:, :], chk[:, 0:1], -1.0, float(RANK1), ALU.mult, ALU.add))
                st.link(v.tensor_scalar(chk[:, 1:2], find.k[:, :], 1.0, None, ALU.is_lt))
                st.link(v.tensor_tensor(chk[:, 2:3], tot[:, 2:3], find.k[:, :], ALU.is_lt))
                st.link(v.tensor_scalar(chk[:, 3:4], tot[:, 3:4], 0.0, None, ALU.is_gt))
                st.link(v.tensor_copy(chk[:, 4:5], flags[:, 0:1]))
                st.link(v.tensor_scalar(chk[:, 5:6], step[:, 2:3], float(1 << WBITS), None, ALU.is_ge))
                st.link(v.tensor_scalar(chk[:, 6:7], brk[:, 0:1], 2.0 ** -60, None, ALU.is_lt))
                st.link(v.tensor_reduce(flags[:, 1:2], chk[:, 1:7], AX, ALU.max))
                st.link(v.tensor_scalar(find.k[:, :], find.k[:, :], 1.0, None, ALU.max))
                find.start(st)
                find.rounds(dve, st, psum[:, 4:5], lambda cnt, thr: v.tensor_scalar(
                    junk[:, :], whole[:, :], thr, None, ALU.is_ge, ALU.add, accum_out=cnt))
                st.link(v.tensor_scalar(find.trial[:, :], find.trial[:, :], -0.5, 2.0 ** -23, ALU.add, ALU.mult))
                st.link(v.scalar_tensor_tensor(out=amax[:, 0:1], in0=find.trial[:, :], scalar=step[:, 0:1], in1=brk[:, 0:1],
                                               op0=ALU.mult, op1=ALU.add))

    with ExitStack() as c:
        hb = sb(c, "f_h2", [P, 2, D])
        junk = sb(c, "f_junk", [P, D])
        mask = sb(c, "f_mask", [P, D])
        find = Search(c, "full", 1, count_dt=F32)
        psum = ps(c, "full_sums", [P, 1])
        s_ld = [sem(c, f"full_loaded{i}") for i in range(2)]
        s_cnt, s_dve = sem(c, "full_counted_tiles"), sem(c, "full_dve_steps")

        with nc.Block() as block:

            def uncovered(eng):
                return eng.If(eng.value_load(flags[0:1, 1:2], min_val=0, max_val=1) > 0)

            @block.sync
            def _(sp):
                with uncovered(sp):
                    with sp.Fori(0, 31) as r:
                        with sp.Fori(0, LAST // 2) as i:
                            for u in range(2):
                                sp.wait_ge(s_cnt, r * TILES + i * 2 + (u + 1))
                                sp.dma_start(hb[:, u, :], h2_dram[bass.ds((i * 2 + u) * P, P), :]).then_inc(s_ld[u], 16)
                        sp.wait_ge(s_cnt, r * TILES + (LAST + 1))
                        sp.dma_start(hb[0:TAIL, 0, :], h2_dram[LAST * P:N, :]).then_inc(s_ld[0], 16)

            @block.tensor
            def _(pe):
                with uncovered(pe):
                    find.sums(pe, psum[:, :])

            @block.vector
            def _(dve):
                v = nc.vector
                st = Steps(dve, s_dve)
                with uncovered(dve):
                    find.start(st)
                    st.link(v.memset(find.k[:, :], float(RANK1)))
                    st.link(v.memset(over[:, :], 0.0), alone=True)
                    v.engine_nop().then_inc(s_cnt, 1)

                    def scan(r, first):
                        def count(u, rows, col):
                            st.link(v.scalar_tensor_tensor(out=junk[0:rows, :], in0=hb[0:rows, u, :], scalar=-1.0,
                                                           in1=hb[0:rows, u, :], op0=ALU.mult, op1=ALU.max))
                            v.tensor_scalar(mask[0:rows, :], junk[0:rows, :], find.trial[0:rows, 0:1].bitcast(F32), None,
                                            ALU.is_ge, ALU.add, accum_out=over[0:rows, col]).then_inc(s_cnt, 1)

                        with dve.Fori(0, LAST // 2) as i:
                            st.enter(i, 0, 2)
                            for u in range(2):
                                dve.wait_ge(s_ld[u], (r * (LAST // 2 + 1 - u) + i) * 16 + 16)
                                count(u, P, bass.ds(i * 2 + u, 1))
                        st.leave(LAST // 2)
                        dve.wait_ge(s_ld[0], (r * (LAST // 2 + 1) + LAST // 2) * 16 + 16)
                        count(0, TAIL, slice(LAST, TILES))
                        dve.wait_ge(s_cnt, r * TILES + (TILES + 1))
                        find.round(dve, st, psum[:, :], r, lambda cnt, thr: v.tensor_reduce(cnt, over[:, :], AX, ALU.add),
                                   first=first)

                    scan(0, True)
                    with dve.Fori(1, 31) as r:
                        st.enter(r, 1, find.steps() + LAST + 1)
                        scan(r, False)
                    st.leave(30)
                    st.link(v.tensor_copy(amax[:, 0:1], find.trial[:, 0:1].bitcast(F32)))


    HALF = P // 2
    with ExitStack() as top2:
        with ExitStack() as c:
            qs = sb(c, "h_q", [P, 4, D], BF16)
            qt = sb(c, "h_qT", [P, 4, D], BF16)
            ga = sb(c, "h_abs", [P, 2, P])
            top16 = sb(c, "h_top", [P, 2, 16])
            identb = sb(c, "h_ident", [P, P], BF16)
            w1sum = sb(c, "h_w1sum", [P, H], BF16)
            w1sumf = sb(c, "h_w1sumf", [P, H])
            neg = sb(c, "h_neg", [P, P], BF16)
            pos = sb(c, "h_pos", [P, 1])
            pT = [ps(c, f"h_pT{i}", [P, D], BF16) for i in range(4)]
            pu = [ps(c, f"h_pu{i}", [P, 512]) for i in range(2)]
            s_id, s_kap, s_r, s_q, s_T, s_qt, s_u, s_G, s_A, s_top, s_c, s_dve = (sem(c, "h_" + n) for n in (
                "constants_ready", "scales_ready", "rounded", "q_ready", "turned", "qT_ready", "multiplied",
                "gelu_ready", "abs_ready", "largest_ready", "kept", "dve_steps"))

            with nc.Block() as block:

                def tiles_over(eng, body, st=None, per=0):
                    for k in range(8):
                        body(Tile(0, k))
                    with eng.Fori(1, 9) as i:
                        if st:
                            st.enter(i, 1, per)
                        for u in range(8):
                            body(Tile(i, u, 8))
                    if st:
                        st.leave(8)
                    for k in range(72, TILES):
                        body(Tile(0, k))

                def place(t):
                    return t.c % 8, t.i + t.c // 8 if t.m == 8 else t.c // 8

                @block.sync
                def _(sp):
                    def load(t):
                        s, _ = place(t)
                        if isinstance(t.i, int) and t.t < 8:
                            return
                        sp.wait_ge(s_q, t.t - 7)
                        if t.last:
                            sp.dma_start(h2_buf[0:TAIL, s, :], h2_dram[LAST * P:N, :]).then_inc(h2_in[s], 16)
                        else:
                            sp.dma_start(h2_buf[:, s, :], h2_dram[bass.ds(t.t * P, P), :]).then_inc(h2_in[s], 16)

                    tiles_over(sp, load)

                @block.gpsimd
                def _(pool):
                    nc.gpsimd.memset(identb[:, :], 0.0).then_inc(s_id, 1)
                    nc.gpsimd.memset(cand2[:, :], 0.0).then_inc(s_id, 1)
                    nc.gpsimd.memset(G[:, GC - P:GC], 0.0).then_inc(s_id, 1)
                    nc.gpsimd.memset(neg[:, :], -128.0).then_inc(s_id, 1)
                    nc.gpsimd.memset(pos[:, :], 128.0).then_inc(s_id, 1)
                    pool.wait_ge(s_id, 5)
                    nc.gpsimd.affine_select(out=identb[:, :], in_=identb[:, :], compare_op=ALU.not_equal, fill=1.0, base=0,
                                            pattern=[[-1, P]], channel_multiplier=1).then_inc(s_id, 1)

                    def keep(t):
                        rows, n = (H, 8) if t.last else (P, 16)
                        wait_alone(pool, s_top, t.half + 1)
                        nc.gpsimd.tensor_copy(cand2[0:rows, bass.ds(t.half * 16, n)], top16[0:rows, t.po, 0:n]).then_inc(s_c, 1)

                    tiles_over(pool, lambda t: keep(t) if t.odd or t.last else None)

                @block.tensor
                def _(pe):
                    def turn(t):
                        pe.wait_ge(s_q, t.t + 1)
                        after(pe, s_qt, t.t - 3)
                        for d in range(DC):
                            last = nc.tensor.matmul(pT[t.slot][:, d * P:(d + 1) * P], qs[:, t.slot, d * P:(d + 1) * P],
                                                    identb[:, :], start=True, stop=True, is_transpose=True)
                        last.then_inc(s_T, 1)

                    def hidden(t):
                        pe.wait_ge(s_qt, t.t + 1)
                        after(pe, s_G, t.half - 1)
                        rows = slice(t.odd * H, (t.odd + 1) * H)
                        nc.tensor.matmul(pu[t.po][rows, 0:P], w1sum[:, :], neg[:, :], start=True, stop=False)
                        for d in range(DC):
                            last = nc.tensor.matmul(pu[t.po][rows, 0:P], w1T[:, d, :], qt[:, t.slot, d * P:(d + 1) * P],
                                                    start=False, stop=(d == DC - 1))
                        last.then_inc(s_u, 1)

                    def both(t):
                        if t.plus(2).within(0, TILES):
                            turn(t.plus(2))
                        hidden(t)

                    pe.wait_ge(s_id, 6)
                    pe.wait_ge(s_kap, 1)
                    turn(Tile(0, 0))
                    turn(Tile(0, 1))
                    tiles_over(pe, both)

                @block.scalar
                def _(act):
                    def gelu(t):
                        rows, n = (H, TAIL) if t.last else (P, P)
                        wait_alone(act, s_u, 2 * t.half + (1 if t.last else 2))
                        g = G[0:rows, bass.ds(t.half * P, n)]
                        nc.scalar.activation(g, pu[t.po][0:rows, 0:n], ACT.Gelu, scale=kap[0:rows, 1:2]).then_inc(s_G, 1)
                        after(act, s_top, t.half - 1)
                        wait_alone(act, s_G, t.half + 1)
                        nc.scalar.activation(ga[0:rows, t.po, 0:n], g, ACT.Abs).then_inc(s_A, 1)

                    def step(t):
                        act.wait_ge(s_T, t.t + 1)
                        after(act, s_u, t.t - 3)
                        nc.scalar.activation(qt[:, t.slot, :], pT[t.slot][:, :], ACT.Relu, bias=pos[:, 0:1]).then_inc(s_qt, 1)
                        if t.odd and t.plus(-2).within(0, TILES):
                            gelu(t.plus(-2))

                    act.wait_ge(s_id, 6)
                    act.wait_ge(s_kap, 1)
                    tiles_over(act, step)
                    gelu(Tile(0, 77))
                    gelu(Tile(0, 78))

                @block.vector
                def _(dve):
                    v = nc.vector
                    st = Steps(dve, s_dve)
                    st.link(v.tensor_scalar(kap[:, 2:3], amax[:, 0:1], EPS_Q, None, ALU.max))
                    st.link(v.reciprocal(kap[:, 3:4], kap[:, 2:3]))
                    st.link(v.tensor_scalar(kap[:, 0:1], kap[:, 3:4], QMAX, None, ALU.mult))
                    st.link(v.reciprocal(kap[:, 3:4], kap[:, 0:1]))
                    st.link(v.tensor_tensor(kap[:, 1:2], kap[:, 3:4], gam[:, 0:1], ALU.mult))
                    st.link(v.tensor_reduce(w1sumf[:, :], w1T[:, :, :].rearrange("p k h -> p h k"), AX, ALU.add))
                    v.tensor_copy(w1sum[:, :], w1sumf[:, :]).then_inc(s_kap, 1)
                    dve.wait_ge(s_id, 6)

                    def rounded(t):
                        s, turn = place(t)
                        dve.wait_ge(h2_in[s], 16 * turn + 16)
                        v.tensor_scalar(h2_buf[:, s, :], h2_buf[:, s, :], kap[:, 0:1], MAGIC, ALU.mult, ALU.add)\
                            .then_inc(s_r, 1)

                    def bounded(t):
                        dve.wait_ge(s_r, t.t + 1)
                        after(dve, s_T, t.t - 3)
                        v.tensor_scalar(qs[:, t.slot, :], h2_buf[:, place(t)[0], :], -MAGIC, QMAX, ALU.add, ALU.min).then_inc(s_q, 1)

                    def largest(t):
                        after(dve, s_c, t.half - 1)
                        wait_alone(dve, s_A, t.half + 1)
                        if t.last:
                            v.max(top16[0:H, t.po, 0:8], ga[0:H, t.po, 0:TAIL]).then_inc(s_top, 1)
                        else:
                            v.max(top16[:, t.po, 0:8], ga[:, t.po, 0:HALF])
                            v.max(top16[:, t.po, 8:16], ga[:, t.po, HALF:P]).then_inc(s_top, 1)

                    def step(t):
                        if t.plus(1).within(0, TILES):
                            rounded(t.plus(1))
                        bounded(t)
                        if t.odd and t.plus(-4).within(0, TILES):
                            largest(t.plus(-4))

                    rounded(Tile(0, 0))
                    tiles_over(dve, step)
                    for k in (75, 77, 78):
                        largest(Tile(0, k))

        first.close()
        lay.close()

        RES = 40
        xres = sb(top2, "x1_resident", [P, RES, D])
        s_res = sem(top2, "x1_resident_loaded")
        with ExitStack() as c:
            junk = sb(c, "r2_junk", [P, PAIRS * 16], BF16)
            chk = sb(c, "r2_chk", [P, 2])
            find = Search(c, "range2", 1)
            psum = ps(c, "range2_sums", [P, 2])
            s_chk, s_tot, s_dve = (sem(c, "range2_" + n) for n in ("full_chunks", "full_total", "dve_steps"))

            with nc.Block() as block:

                @block.sync
                def _(sp):
                    for k in range(RES):
                        sp.dma_start(xres[:, k, :], x1_dram[k * P:(k + 1) * P, :]).then_inc(s_res, 16)

                @block.tensor
                def _(pe):
                    find.sums(pe, psum[:, 0:1])
                    pe.wait_ge(s_chk, 1)
                    nc.tensor.matmul(psum[:, 1:2], ones[:, :], chk[:, 0:1], start=True, stop=True).then_inc(s_tot, 1)

                @block.vector
                def _(dve):
                    v = nc.vector
                    st = Steps(dve, s_dve)
                    find.start(st)
                    st.link(v.memset(find.k[:, :], float(RANK2)))
                    find.rounds(dve, st, psum[:, 0:1], lambda cnt, thr: v.tensor_scalar(
                        junk[:, :], cand2[:, :], thr, None, ALU.is_ge, ALU.add, accum_out=cnt))
                    st.link(v.tensor_copy(amax[:, 1:2], find.trial[:, 0:1].bitcast(F32)))
                    v.tensor_scalar(junk[:, 0:2 * PAIRS], cand2[:, :].rearrange("p (t k) -> p t k", k=8)[:, :, 7], amax[:, 1:2],
                                    None, ALU.is_ge, ALU.add, accum_out=chk[:, 0:1]).then_inc(s_chk, 1)
                    dve.wait_ge(s_tot, 1)
                    st.link(v.tensor_scalar(flags[:, 2:3], psum[:, 1:2], 0.0, None, ALU.is_gt))

        with ExitStack() as c:
            junk = sb(c, "g_junk", [P, D])
            hits = sb(c, "g_hits", [P, D], BF16)
            part = sb(c, "g_parts", [P, GC // D])
            find = Search(c, "fullg", 1, count_dt=F32)
            psum = ps(c, "fullg_sums", [P, 1])
            s_dve = sem(c, "fullg_dve_steps")

            with nc.Block() as block:

                def uncovered2(eng):
                    return eng.If(eng.value_load(flags[0:1, 2:3], min_val=0, max_val=1) > 0)

                @block.tensor
                def _(pe):
                    with uncovered2(pe):
                        find.sums(pe, psum[:, 0:1])

                @block.vector
                def _(dve):
                    v = nc.vector
                    st = Steps(dve, s_dve)
                    with uncovered2(dve):
                        find.start(st)
                        st.link(v.memset(find.k[:, :], float(RANK2)))

                        def scan(n, first):
                            for k in range(GC // D):
                                g = G[:, k * D:(k + 1) * D]
                                st.link(v.scalar_tensor_tensor(out=junk[:, :], in0=g, scalar=-1.0, in1=g,
                                                               op0=ALU.mult, op1=ALU.max))
                                st.link(v.tensor_scalar(hits[:, :], junk[:, :], find.trial[:, 0:1].bitcast(F32), None,
                                                        ALU.is_ge, ALU.add, accum_out=part[:, k:k + 1]))
                            find.round(dve, st, psum[:, :], n, lambda cnt, thr: v.tensor_reduce(cnt, part[:, :], AX, ALU.add),
                                       first=first)

                        scan(0, True)
                        with dve.Fori(1, 31) as n:
                            st.enter(n, 1, find.steps() + 2 * (GC // D))
                            scan(n, False)
                        st.leave(30)
                        st.link(v.tensor_copy(amax[:, 1:2], find.trial[:, 0:1].bitcast(F32)))

        with ExitStack() as c:
            xb = sb(c, "o_x1", [P, 4, D])
            qf = sb(c, "o_qf", [P, P])
            q2 = sb(c, "o_q", [P, 2, P], BF16)
            po = [ps(c, f"o_po{i}", [P, D]) for i in range(4)]
            ld = [sem(c, f"o_loaded{i}") for i in range(4)]
            MIXED = RES // 2
            TURNS = -(-TILES // 4)
            assert RES % 4 == 0
            sr = sem(c, "o_resident_stored")
            sd = [sem(c, f"o_stored{i}") for i in range(4)]
            s_q, s_m, s_o, s_dve = (sem(c, "o_" + n) for n in ("q_ready", "multiplied", "out_ready", "dve_steps"))

            def tail(j):
                return isinstance(j, int) and j >= MIXED

            def pair_of(j, h):
                return 2 * j + h if tail(j) else j + MIXED * h

            def tile_of(j, u):
                return pair_of(j, u // 2) * 2 + u % 2

            def rows_of(j, u):
                t = tile_of(j, u)
                return (TAIL, slice(LAST * P, N)) if isinstance(t, int) and t == LAST else (P, bass.ds(t * P, P))

            def slot_of(n, a, u):
                j = 2 * n + a
                if tail(j):
                    return u, MIXED // 2 + j - MIXED
                return (2 * a + u - 2, n) if u >= 2 else None

            def rows_at(n, a, u):
                where = slot_of(n, a, u)
                if where:
                    return xb[:, where[0], :]
                return xres[:, bass.ds(4 * n + 2 * a + u, 1), :].rearrange("p a d -> p (a d)")

            def turns_over(eng, body, st=None, per=0):
                def some(first, last):
                    for k in range(first, last):
                        body(k // 8, k // 4 % 2, k % 4)

                some(0, 8)
                with eng.Fori(1, MIXED // 2 - 1) as n:
                    if st:
                        st.enter(n, 1, per)
                    for k in range(8):
                        body(n, k // 4, k % 4)
                if st:
                    st.leave(MIXED // 2 - 2)
                some(4 * MIXED - 8, TILES)

            with nc.Block() as block:

                @block.sync
                def _(sp):
                    def load(n, a, u):
                        where = slot_of(n, a, u)
                        if where:
                            slot, before = where
                            rows, src = rows_of(2 * n + a, u)
                            after(sp, sd[slot], 16 * before)
                            sp.dma_start(xb[0:rows, slot, :], x1_dram[src, :]).then_inc(ld[slot], 16)

                    turns_over(sp, load)

                @block.scalar
                def _(act):
                    def store(n, a, u):
                        j = 2 * n + a
                        act.wait_ge(s_o, 4 * j + (u + 1))
                        rows, dst = rows_of(j, u)
                        where = slot_of(n, a, u)
                        act.dma_start(out[dst, :], rows_at(n, a, u)[0:rows, :]).then_inc(sd[where[0]] if where else sr, 16)

                    turns_over(act, store)
                    act.wait_ge(sr, 16 * RES)
                    tiles = [slot_of(k // 8, k // 4 % 2, k % 4) for k in range(TILES)]
                    for slot in range(4):
                        act.wait_ge(sd[slot], 16 * len([w for w in tiles if w and w[0] == slot]))

                @block.tensor
                def _(pe):
                    def step(n, a, u):
                        j, h = 2 * n + a, u // 2
                        pe.wait_ge(s_q, 2 * j + h + 1)
                        after(pe, s_o, 4 * j + u - 3)
                        rows = slice((u % 2) * H, (u % 2 + 1) * H)
                        for k in range(2):
                            last = nc.tensor.matmul(po[u][:, k * 512:(k + 1) * 512], q2[rows, h, :],
                                                    w2T[rows, k * 512:(k + 1) * 512], start=True, stop=True)
                        last.then_inc(s_m, 1)

                    turns_over(pe, step)

                @block.vector
                def _(dve):
                    v = nc.vector
                    st = Steps(dve, s_dve)
                    st.link(v.tensor_scalar(kap[:, 2:3], amax[:, 1:2], EPS_Q, None, ALU.max))
                    st.link(v.reciprocal(kap[:, 3:4], kap[:, 2:3]))
                    st.link(v.tensor_scalar(kap[:, 4:5], kap[:, 3:4], QMAX, None, ALU.mult))
                    st.link(v.reciprocal(kap[:, 3:4], kap[:, 4:5]))
                    st.link(v.tensor_tensor(kap[:, 5:6], kap[:, 3:4], gam[:, 1:2], ALU.mult))

                    def quantise(j, h):
                        pair = pair_of(j, h)
                        last = isinstance(pair, int) and pair == PAIRS - 1
                        rows, n = (H, TAIL) if last else (P, P)
                        after(dve, s_q, 2 * j + h)
                        st.link(v.tensor_scalar(qf[0:rows, 0:n], G[0:rows, bass.ds(pair * P, n)], kap[0:rows, 4:5], MAGIC,
                                                ALU.mult, ALU.add))
                        st.link(v.tensor_scalar(qf[0:rows, 0:n], qf[0:rows, 0:n], MAGIC - 128.0, MAGIC + 127.0, ALU.max, ALU.min))
                        after(dve, s_m, 4 * j + 2 * h - 2)
                        v.tensor_scalar(q2[0:rows, h, 0:n], qf[0:rows, 0:n], -MAGIC, None, ALU.add).then_inc(s_q, 1)

                    def step(n, a, u):
                        j = 2 * n + a
                        if u == 0 and not (isinstance(j, int) and 2 * j + 1 >= PAIRS):
                            quantise(j, 1)
                        if u == 2 and not (isinstance(j, int) and 2 * j + 2 >= PAIRS):
                            quantise(j + 1, 0)
                        dve.wait_ge(s_m, 4 * j + (u + 1))
                        where = slot_of(n, a, u)
                        if where:
                            dve.wait_ge(ld[where[0]], 16 * where[1] + 16)
                        x = rows_at(n, a, u)
                        v.scalar_tensor_tensor(out=x, in0=po[u][:, :], scalar=kap[:, 5:6], in1=x,
                                               op0=ALU.mult, op1=ALU.add).then_inc(s_o, 1)

                    quantise(0, 0)
                    dve.wait_ge(s_res, 16 * RES)
                    turns_over(dve, step, st, 8)

    top.close()


def kernel(x, src, dst, L0_gnn_W, L0_gnn_b, L0_ffn_ln_g, L0_ffn_ln_b, L0_ffn_w1, L0_ffn_w2):
    import concourse.bacc as bacc
    import numpy as np
    from concourse.bass_utils import run_bass_kernel_spmd

    nc = bacc.Bacc("TRN2", target_bir_lowering=False, num_devices=1)
    given = {"x": x, "src": src, "dst": dst, "W": L0_gnn_W, "b": L0_gnn_b, "ln_g": L0_ffn_ln_g, "ln_b": L0_ffn_ln_b,
             "w1": L0_ffn_w1, "w2": L0_ffn_w2}
    arrays = {"in_" + k: np.ascontiguousarray(a) for k, a in given.items()}
    ins = [nc.dram_tensor(k, a.shape, mybir.dt.from_np(a.dtype), kind="ExternalInput").ap() for k, a in arrays.items()]
    out = nc.dram_tensor("out_rows", (N, D), F32, kind="ExternalOutput").ap()
    build(nc, *ins, out)
    return run_bass_kernel_spmd(nc, [arrays], core_ids=[0]).results[0]["out_rows"]
```
